# Optimizing a Trainium2 kernel written in Bass

```python
import numpy as np
import jax
import jax.numpy as jnp

def _softmax(x, axis=-1):
    return jax.nn.softmax(x, axis=axis)
def _gelu(x):
    return jax.nn.gelu(x, approximate=True)
def _silu(x):
    return jax.nn.silu(x)
def _sigmoid(x):
    return jax.nn.sigmoid(x)
def _layernorm(x, axis=-1, eps=1e-5):
    m = jnp.mean(x, axis=axis, keepdims=True)
    v = jnp.var(x, axis=axis, keepdims=True)
    return (x - m) / jnp.sqrt(v + eps)
def _scatter_add(tgt, idx, src, axis=0):
    return tgt.at[idx].add(src)
def _segment_sum(src, seg, n):
    return jax.ops.segment_sum(src, seg, n)

kernel_name = 'mk_vit_tower_d1_tok_img256_a38d9d'

def setup_inputs(seed: int = 0):
    np.random.seed(seed)
    _w = jnp.asarray
    def _rec_inputs():
        import jax
        import jax.numpy as jnp
        _rk = jax.random.key(seed)
        x = (7.22013e-05 + 1.00017 * jax.random.normal(jax.random.fold_in(_rk, 1), (2, 1, 4096, 256), jnp.float32))
        return x
    x = _rec_inputs()
    def _L0_tok_setup():
        import jax, jax.numpy as jnp
        import numpy as np
        T, D_IN, D_INT, D_OUT, B = (4096, 256, 256, 256, 8)
        key = jax.random.key(seed)
        ks = jax.random.split(key, 12)
        s_in = 1.0 / np.sqrt(D_IN)
        s_int = 1.0 / np.sqrt(D_INT)
        return {'x_batched': jax.random.normal(ks[0], (B, 1, T, D_IN), dtype=jnp.float32), 'd_gamma_batched': jax.random.uniform(ks[1], (T, T), dtype=jnp.float32), 'Wq': jax.random.uniform(ks[2], (D_IN, D_INT), jnp.float32, -s_in, s_in), 'bq': jax.random.uniform(ks[3], (D_INT,), jnp.float32, -s_in, s_in), 'Wk': jax.random.uniform(ks[4], (D_IN, D_INT), jnp.float32, -s_in, s_in), 'bk': jax.random.uniform(ks[5], (D_INT,), jnp.float32, -s_in, s_in), 'Wv': jax.random.uniform(ks[6], (D_IN, D_INT), jnp.float32, -s_in, s_in), 'bv': jax.random.uniform(ks[7], (D_INT,), jnp.float32, -s_in, s_in), 'Wo': jax.random.uniform(ks[8], (D_INT, D_OUT), jnp.float32, -s_int, s_int), 'bo': jax.random.uniform(ks[9], (D_OUT,), jnp.float32, -s_int, s_int), 'prelu_a': jnp.float32(0.25)}
    _L0_tok_all = _L0_tok_setup()
    _L0_tok_in = {k: v for k, v in _L0_tok_all.items() if k in ('d_gamma_batched', 'Wq', 'bq', 'Wk', 'bk', 'Wv', 'bv', 'Wo', 'bo', 'prelu_a', )}
    del _L0_tok_all

    def _L0_attn_setup():
        import jax, jax.numpy as jnp
        import numpy as np
        import math
        N_SEQ, L_RES, D_MODEL = (512, 384, 256)
        N_HEAD, C_HEAD = (8, 32)
        EPS = 1e-05
        key = jax.random.key(seed)
        ks = jax.random.split(key, 8)
        s = 1.0 / math.sqrt(D_MODEL)
        return {'m': jax.random.normal(ks[0], (N_SEQ, L_RES, D_MODEL), jnp.float32), 'gamma': jnp.ones((D_MODEL,), jnp.float32), 'beta': jnp.zeros((D_MODEL,), jnp.float32), 'Wq': jax.random.normal(ks[1], (D_MODEL, N_HEAD * C_HEAD), jnp.float32) * s, 'Wk': jax.random.normal(ks[2], (D_MODEL, N_HEAD * C_HEAD), jnp.float32) * s, 'Wv': jax.random.normal(ks[3], (D_MODEL, N_HEAD * C_HEAD), jnp.float32) * s, 'Wg': jax.random.normal(ks[4], (D_MODEL, N_HEAD * C_HEAD), jnp.float32) * s, 'bg': jnp.zeros((N_HEAD * C_HEAD,), jnp.float32), 'Wo': jax.random.normal(ks[5], (N_HEAD * C_HEAD, D_MODEL), jnp.float32) * s, 'bo': jnp.zeros((D_MODEL,), jnp.float32)}
    _L0_attn_all = _L0_attn_setup()
    _L0_attn_in = {k: v for k, v in _L0_attn_all.items() if k in ('gamma', 'beta', 'Wq', 'Wk', 'Wv', 'Wg', 'bg', 'Wo', 'bo', )}
    del _L0_attn_all

    def _L0_ffn_setup():
        import jax, jax.numpy as jnp
        import numpy as np
        B, S, D = (8, 4096, 256)
        H = 4 * D
        CAPACITY = 0.5
        key = jax.random.key(seed)
        ks = jax.random.split(key, 6)
        x = jax.random.normal(ks[0], (B, S, D), dtype=jnp.float32)
        attention_mask = jnp.zeros((B, 1, 1, S), dtype=jnp.float32)
        wr = jax.random.normal(ks[1], (D, 1), dtype=jnp.float32) * 0.02
        br = jnp.zeros((1,), dtype=jnp.float32)
        w1 = jax.random.normal(ks[2], (D, H), dtype=jnp.float32) * 0.02
        b1 = jnp.zeros((H,), dtype=jnp.float32)
        w2 = jax.random.normal(ks[3], (H, D), dtype=jnp.float32) * 0.02
        b2 = jnp.zeros((D,), dtype=jnp.float32)
        return {'x': x, 'attention_mask': attention_mask, 'wr': wr, 'br': br, 'w1': w1, 'b1': b1, 'w2': w2, 'b2': b2}
    _L0_ffn_all = _L0_ffn_setup()
    _L0_ffn_in = {k: v for k, v in _L0_ffn_all.items() if k in ('attention_mask', 'wr', 'br', 'w1', 'b1', 'w2', 'b2', )}
    del _L0_ffn_all

    return {
        "x": x,
        "L0_tok_d_gamma_batched": _L0_tok_in["d_gamma_batched"],
        "L0_tok_Wq": _L0_tok_in["Wq"],
        "L0_tok_bq": _L0_tok_in["bq"],
        "L0_tok_Wk": _L0_tok_in["Wk"],
        "L0_tok_bk": _L0_tok_in["bk"],
        "L0_tok_Wv": _L0_tok_in["Wv"],
        "L0_tok_bv": _L0_tok_in["bv"],
        "L0_tok_Wo": _L0_tok_in["Wo"],
        "L0_tok_bo": _L0_tok_in["bo"],
        "L0_tok_prelu_a": _L0_tok_in["prelu_a"],
        "L0_attn_gamma": _L0_attn_in["gamma"],
        "L0_attn_beta": _L0_attn_in["beta"],
        "L0_attn_Wq": _L0_attn_in["Wq"],
        "L0_attn_Wk": _L0_attn_in["Wk"],
        "L0_attn_Wv": _L0_attn_in["Wv"],
        "L0_attn_Wg": _L0_attn_in["Wg"],
        "L0_attn_bg": _L0_attn_in["bg"],
        "L0_attn_Wo": _L0_attn_in["Wo"],
        "L0_attn_bo": _L0_attn_in["bo"],
        "L0_ffn_attention_mask": _L0_ffn_in["attention_mask"],
        "L0_ffn_wr": _L0_ffn_in["wr"],
        "L0_ffn_br": _L0_ffn_in["br"],
        "L0_ffn_w1": _L0_ffn_in["w1"],
        "L0_ffn_b1": _L0_ffn_in["b1"],
        "L0_ffn_w2": _L0_ffn_in["w2"],
        "L0_ffn_b2": _L0_ffn_in["b2"],
    }

def reference(x, L0_tok_d_gamma_batched, L0_tok_Wq, L0_tok_bq, L0_tok_Wk, L0_tok_bk, L0_tok_Wv, L0_tok_bv, L0_tok_Wo, L0_tok_bo, L0_tok_prelu_a, L0_attn_gamma, L0_attn_beta, L0_attn_Wq, L0_attn_Wk, L0_attn_Wv, L0_attn_Wg, L0_attn_bg, L0_attn_Wo, L0_attn_bo, L0_ffn_attention_mask, L0_ffn_wr, L0_ffn_br, L0_ffn_w1, L0_ffn_b1, L0_ffn_w2, L0_ffn_b2):
    import jax
    import jax.numpy as jnp
    def _L0_tok_ref(x_batched, d_gamma_batched, Wq, bq, Wk, bk, Wv, bv, Wo, bo, prelu_a):
        import jax, jax.numpy as jnp
        import numpy as np
        T, D_IN, D_INT, D_OUT, B = (4096, 256, 256, 256, 8)
        x = x_batched.reshape(x_batched.shape[0], T, D_IN)
        q = x @ Wq + bq
        k = x @ Wk + bk
        v = x @ Wv + bv
        scores = jnp.einsum('btd,bsd->bts', q, k)
        retained = jnp.einsum('bts,bsd->btd', d_gamma_batched * scores, v)
        y = retained @ Wo + bo
        out = jnp.where(y >= 0, y, prelu_a * y)
        return out

    def _L0_attn_ref(m, gamma, beta, Wq, Wk, Wv, Wg, bg, Wo, bo):
        import jax, jax.numpy as jnp
        import numpy as np
        import math
        N_SEQ, L_RES, D_MODEL = (512, 384, 256)
        N_HEAD, C_HEAD = (8, 32)
        EPS = 1e-05
        N, L, D = m.shape
        H, C = (N_HEAD, C_HEAD)
        mu = jnp.mean(m, axis=-1, keepdims=True)
        var = jnp.mean(jnp.square(m - mu), axis=-1, keepdims=True)
        mn = (m - mu) * jax.lax.rsqrt(var + EPS) * gamma + beta
        q = (mn @ Wq).reshape(N, L, H, C)
        k = (mn @ Wk).reshape(N, L, H, C)
        v = (mn @ Wv).reshape(N, L, H, C)
        g = jax.nn.sigmoid(mn @ Wg + bg).reshape(N, L, H, C)
        scale = 1.0 / math.sqrt(C) / math.sqrt(L)
        att = jnp.einsum('slhc,tlhc->sth', q, k) * scale
        att = jax.nn.softmax(att, axis=1)
        o = jnp.einsum('sth,tlhc->slhc', att, v) * g
        return o.reshape(N, L, H * C) @ Wo + bo

    def _L0_ffn_ref(x, attention_mask, wr, br, w1, b1, w2, b2):
        import jax, jax.numpy as jnp
        import numpy as np
        B, S, D = (8, 4096, 256)
        H = 4 * D
        CAPACITY = 0.5
        b, s, d = x.shape
        weights = (jnp.einsum('bsd,do->bso', x, wr) + br)[..., 0]
        k = max(1, int(CAPACITY * s))
        kk = k - 1 if k > 1 else 1
        _, idx = jax.lax.top_k(weights, k)
        sel_idx = idx[:, :kk]
        sel = jnp.take_along_axis(x, sel_idx[:, :, None], axis=1)
        h = jax.nn.gelu(jnp.einsum('bkd,dh->bkh', sel, w1) + b1)
        y = jnp.einsum('bkh,hd->bkd', h, w2) + b2
        w_sel = jnp.take_along_axis(weights, sel_idx, axis=1)
        y = y * w_sel[..., None]
        batch_idx = jnp.arange(b)[:, None]
        processed = jnp.zeros_like(x).at[batch_idx, sel_idx].set(y)
        return processed + x

    h = _L0_tok_ref(x, L0_tok_d_gamma_batched, L0_tok_Wq, L0_tok_bq, L0_tok_Wk, L0_tok_bk, L0_tok_Wv, L0_tok_bv, L0_tok_Wo, L0_tok_bo, L0_tok_prelu_a)
    h = h + _L0_attn_ref(_layernorm(h, axis=-1), L0_attn_gamma, L0_attn_beta, L0_attn_Wq, L0_attn_Wk, L0_attn_Wv, L0_attn_Wg, L0_attn_bg, L0_attn_Wo, L0_attn_bo)
    h = h + _L0_ffn_ref(_layernorm(h, axis=-1), L0_ffn_attention_mask, L0_ffn_wr, L0_ffn_br, L0_ffn_w1, L0_ffn_b1, L0_ffn_w2, L0_ffn_b2)
    return h


_drawn_inputs = setup_inputs


def setup_inputs(seed=0):
    import zlib

    import numpy as np

    out = dict(_drawn_inputs(seed))
    spreads = {'L0_attn_gamma': (1.0, 0.6),
     'L0_attn_beta': (0.0, 0.8),
     'L0_attn_bg': (0.0, 0.8),
     'L0_attn_bo': (0.0, 2.0),
     'L0_ffn_b1': (0.0, 2.0),
     'L0_ffn_b2': (0.0, 2.0)}
    factors = {'L0_tok_bo': 200.0,
     'L0_attn_Wq': 8.0,
     'L0_attn_Wk': 8.0,
     'L0_attn_Wv': 8.0,
     'L0_attn_Wg': 8.0,
     'L0_attn_Wo': 8.0,
     'L0_ffn_wr': 8.0,
     'L0_ffn_w1': 8.0,
     'L0_ffn_w2': 8.0}
    for name, (base, spread) in spreads.items():
        noise = np.random.default_rng([zlib.crc32(name.encode()), seed]).standard_normal(out[name].shape)
        drawn = base * np.exp(spread * noise) if base else spread * noise
        out[name] = jnp.asarray(drawn.astype(out[name].dtype))
    for name, factor in factors.items():
        out[name] = (out[name] * factor).astype(out[name].dtype)
    return out
```

```python
from contextlib import ExitStack

import concourse.bass as bass
from concourse import mybir

P = 128
CH = 512
TPC = CH // P
GT = 2
RG = 4
RP = 4
EPS = 1e-5
HEADS = 8

F32 = mybir.dt.float32
F32R = mybir.dt.float32r
BF16 = mybir.dt.bfloat16
I32 = mybir.dt.int32
ALU = mybir.AluOpType
ACT = mybir.ActivationFunctionType
AX_X = mybir.AxisListType.X


def split_products(hi_w, lo_w, hi_x, lo_x):
    return ((hi_w, hi_x), (hi_w, lo_x), (lo_w, hi_x))


class Program:

    def __init__(self, nc, ctx, ins, out, batches, tokens, width, heads, hidden):
        self.nc, self.ctx, self.ins, self.out = nc, ctx, ins, out
        self.B, self.T, self.D, self.H, self.F = batches, tokens, width, heads, hidden
        self.KD = width // P
        self.NC = tokens // CH
        self.ST = tokens // P
        self.NG = self.ST // GT
        self.used = {}

    def stand_alone(self, eng):
        eng.sem_inc(self.sem("went_on"), 1)

    def sem(self, name):
        if name not in self.used:
            self.used[name] = self.ctx.enter_context(self.nc.semaphore(name))
        return self.used[name]


def early(c, n):
    return isinstance(c, int) and c < n


def sb(nc, ctx, name, shape, dt=F32):
    return ctx.enter_context(nc.sbuf_tensor(name, shape, dt))


def ps(nc, ctx, name, shape=(P, CH), dt=F32):
    return ctx.enter_context(nc.psum_tensor(name, list(shape), dt))


def setup_weights(pr, W, ident):
    nc, ins, KD, D = pr.nc, pr.ins, pr.KD, pr.D
    with ExitStack() as ctx:
        wqT, wkT, wvT, wo = (sb(nc, ctx, n, [P, KD, D]) for n in ("wqT", "wkT", "wvT", "wo"))
        bq2, bk2, bv2 = (sb(nc, ctx, n, [P, KD, 2]) for n in ("bq2", "bk2", "bv2"))
        ones = sb(nc, ctx, "ones_setup", [P, P])
        bq_rows, bv_rows = (sb(nc, ctx, n, [P, KD, P]) for n in ("bq_rows", "bv_rows"))
        a_f, vo_f = sb(nc, ctx, "a_f", [P, KD, D]), sb(nc, ctx, "vo_f", [P, KD, D + 2])
        pa = [ps(nc, ctx, f"pa{j}") for j in range(KD)]
        pv = [ps(nc, ctx, f"pv{j}") for j in range(KD)]
        pb, pr_ = ps(nc, ctx, "pb"), ps(nc, ctx, "pr_")
        loaded, made, rows, prod, kept, hi_ok, lo_ok = (
            pr.sem(n) for n in ("w_loaded", "w_consts", "w_rows", "w_products", "w_kept", "w_hi", "w_lo"))
        n_loads = 4 + 3 * 2 + 1 + 2
        block = ctx.enter_context(nc.Block())

        @block.sync
        def _(sp):
            for t, name in ((wqT, "tok_WqT"), (wkT, "tok_WkT"), (wvT, "tok_WvT"), (wo, "tok_Wo")):
                sp.dma_start(t[:, :, :], ins[name].rearrange("(k p) n -> p k n", p=P)).then_inc(loaded, 16)
            with nc.allow_non_contiguous_dma(reason="bias columns, once"):
                for t, name in ((bq2, "tok_bq"), (bk2, "tok_bk"), (bv2, "tok_bv")):
                    for j in range(2):
                        sp.dma_start(t[:, :, j], ins[name].rearrange("(k p) -> p k", p=P)).then_inc(loaded, 16)
                sp.dma_start(W["bo_col"][:, :], ins["tok_bo"].rearrange("(k p) -> p k", p=P)).then_inc(loaded, 16)
            sp.dma_start(W["gamma"][:, :], ins["attn_gamma"].partition_broadcast(P)).then_inc(loaded, 16)
            sp.dma_start(W["beta"][:, :], ins["attn_beta"].partition_broadcast(P)).then_inc(loaded, 16)
            sp.dma_start(W["prelu"][:, :], ins["tok_prelu_a"].partition_broadcast(P)).then_inc(loaded, 16)

        @block.gpsimd
        def _(pool):
            nc.gpsimd.memset(ident[:, :], 0.0).then_inc(made, 1)
            nc.gpsimd.memset(ones[:, :], 1.0).then_inc(made, 1)
            pool.wait_ge(made, 2)
            nc.gpsimd.affine_select(out=ident[:, :], in_=ident[:, :], compare_op=ALU.not_equal, fill=1.0,
                                    base=0, pattern=[[-1, P]], channel_multiplier=1).then_inc(made, 1)

        @block.vector
        def _(dve):
            dve.wait_ge(loaded, 16 * (n_loads + 1))
            dve.wait_ge(made, 3)
            for k in range(KD):
                nc.vector.tensor_scalar(bq_rows[:, k, :], ones[:, :], bq2[:, k, 0:1], None,
                                        ALU.mult).then_inc(rows, 1)
                nc.vector.tensor_scalar(bv_rows[:, k, :], ones[:, :], bv2[:, k, 0:1], None,
                                        ALU.mult).then_inc(rows, 1)
            dve.wait_ge(prod, 1)
            for j in range(KD):
                nc.vector.tensor_copy(a_f[:, j, :], pa[j][:, 0:D]).then_inc(kept, 1)
                nc.vector.tensor_copy(vo_f[:, j, :], pv[j][:, 0:D + 2]).then_inc(kept, 1)
            nc.vector.tensor_copy(W["bk_col"][:, :], pb[:, 0:2 * KD:2]).then_inc(kept, 1)
            nc.vector.tensor_copy(W["v_bias"][:, :], pr_[:, 0:D + 2]).then_inc(kept, 1)
            dve.wait_ge(hi_ok, 2)
            nc.vector.tensor_tensor(W["a_lo"][:, :, :], a_f[:, :, :], W["a_hi"][:, :, :].bitcast(F32),
                                    ALU.subtract).then_inc(lo_ok, 1)
            nc.vector.tensor_tensor(W["vo_lo"][:, :, :], vo_f[:, :, :], W["vo_hi"][:, :, :].bitcast(F32),
                                    ALU.subtract).then_inc(lo_ok, 1)

        @block.scalar
        def _(act):
            act.wait_ge(kept, 2 * KD)
            nc.scalar.activation(W["a_hi"][:, :, :], a_f[:, :, :], ACT.Copy).then_inc(hi_ok, 1)
            nc.scalar.activation(W["vo_hi"][:, :, :], vo_f[:, :, :], ACT.Copy).then_inc(hi_ok, 1)

        @block.tensor
        def _(pe):
            pe.wait_ge(rows, 2 * KD)
            for j in range(KD):
                cols = slice(j * P, (j + 1) * P)
                for k in range(KD):
                    pe.matmul(pa[j][:, 0:D], wkT[:, k, cols], wqT[:, k, :], start=k == 0, stop=k == KD - 1)
                for k in range(KD):
                    pe.matmul(pv[j][:, 0:D], wvT[:, k, cols], wo[:, k, :], start=k == 0, stop=k == KD - 1,
                              skip_group_check=True)
                for k in range(KD):
                    pe.matmul(pv[j][:, D:D + 2], wkT[:, k, cols], bq2[:, k, :], start=False,
                              stop=k == KD - 1, skip_group_check=True)
                for k in range(KD):
                    pe.matmul(pb[:, 2 * j:2 * j + 2], wqT[:, k, cols], bk2[:, k, :], start=j == 0 and k == 0,
                              stop=k == KD - 1, skip_group_check=True)
            for k in range(KD):
                pe.matmul(pr_[:, 0:D], bv_rows[:, k, :], wo[:, k, :], start=k == 0, stop=k == KD - 1,
                          skip_group_check=True)
            for k in range(KD):
                last = pe.matmul(pr_[:, D:D + 2], bq_rows[:, k, :], bk2[:, k, :], start=False,
                                 stop=k == KD - 1, skip_group_check=True)
            last.then_inc(prod, 1)


def tokenizer(pr, W, ident, scratch):
    nc, ins, D, KD, NC, ST, NG = pr.nc, pr.ins, pr.D, pr.KD, pr.NC, pr.ST, pr.NG
    assert KD == 2 and NG % RG == 0 and NC % 2 == 0
    PAIRS = NC // 2
    TURN_Y, RECTIFY, NORM, SPLIT_X, TURN_MN, KEEP_MN = 4, 5, 8, 6, ST - 5, ST - 3

    with ExitStack() as ctx:
        kt_hi, kt_lo = (sb(nc, ctx, n, [P, KD, pr.T], F32R) for n in ("kt_hi", "kt_lo"))
        v_hi, v_lo = (sb(nc, ctx, n, [P, ST, D], F32R) for n in ("v_hi", "v_lo"))
        d_col = sb(nc, ctx, "d_col", [P, ST])
        gate = sb(nc, ctx, "gate", [P, RG, GT, CH])
        p32 = sb(nc, ctx, "p32", [P, RP, CH])
        p_hi, p_lo = (sb(nc, ctx, n, [P, 2, CH], F32R) for n in ("p_hi", "p_lo"))
        x32 = sb(nc, ctx, "x32", [P, KD, CH])
        x_hi, x_lo = (sb(nc, ctx, n, [P, 2, KD, CH], F32R) for n in ("x_hi", "x_lo"))
        vf = sb(nc, ctx, "vf", [P, 2, D + 2])
        yT = sb(nc, ctx, "yT", [P, KD, CH])
        h_sb, mn_sb = (sb(nc, ctx, n, [P, TPC, D]) for n in ("h_sb", "mn_sb"))
        mnT_sb = sb(nc, ctx, "mnT_sb", [P, KD, CH])
        stats, mv = sb(nc, ctx, "stats", [P, TPC, 6]), sb(nc, ctx, "mv", [P, TPC, 2])
        spread, rstd, power = sb(nc, ctx, "spread", [P, TPC]), sb(nc, ctx, "rstd", [P, TPC]), sb(nc, ctx, "power", [P, TPC])
        S = [ps(nc, ctx, f"S{i}") for i in range(2)]
        Y = [ps(nc, ctx, f"Y{i}") for i in range(2)]
        TR = [ps(nc, ctx, f"TR{i}") for i in range(4)]
        KP, VP = S, [Y[0], Y[1], TR[0], TR[1]]

        (xp_ld, xp_hi, xp_lo, kp, k_evac, k_hi_ok, k_lo_ok, vp, v_evac, v_hi_ok, v_lo_ok, d_ok,
         xm_ld, xm_hi, xm_lo, scores, mul_done, hi_done, lo_done, ret_done, y_evac,
         y_turned, neg_ok, h_ok, stats_ok, mv_ok, spread_ok, rstd_ok, z_ok, scaled, mn_ok,
         mn_turned, mnT_ok, st_h, st_mn, st_mnT, power_ok) = (pr.sem(n) for n in (
            "xp_ld", "xp_hi", "xp_lo", "kp", "k_evac", "k_hi_ok", "k_lo_ok", "vp", "v_evac", "v_hi_ok",
            "v_lo_ok", "d_ok", "xm_ld", "xm_hi", "xm_lo", "scores", "mul_done", "hi_done", "lo_done",
            "ret_done", "y_evac", "y_turned", "neg_ok", "h_ok", "stats_ok", "mv_ok", "spread_ok", "rstd_ok",
            "z_ok", "scaled", "mn_ok", "mn_turned", "mnT_ok", "st_h", "st_mn", "st_mnT", "power_ok"))
        gate_ld = [pr.sem(f"gate_ld{r}") for r in range(RG)]
        block = ctx.enter_context(nc.Block())

        def projection(eng, b, step):
            with eng.Fori(0, PAIRS - 1) as p:
                for h in range(2):
                    step(p * 2 + h, b * NC + p * 2 + h, h, False)
            for c in (NC - 2, NC - 1):
                step(c, b * NC + c, c % 2, c == NC - 1)

        def attention(eng, b, step):
            for c in range(2):
                step(c, b * NC + c, c, c == 0, False)
            if PAIRS > 2:
                with eng.Fori(1, PAIRS - 1) as p:
                    for h in range(2):
                        step(p * 2 + h, b * NC + p * 2 + h, h, False, False)
            for c in range(NC - 2, NC):
                step(c, b * NC + c, c % 2, False, c == NC - 1)

        @block.sync
        def _(sp):
            def load_x(b, c, sem):
                sp.dma_start(x32[:, :, :], ins["xT"][b, c]).then_inc(sem, 16)

            def store(Q, b, c, sem, ready, count, tile, dram):
                sp.wait_ge(ready, (Q + 1) * count)
                sp.dma_start(dram[b, c], tile).then_inc(sem, 16)

            stores = ((NG // 2, st_h, h_ok, 2, h_sb[:, :, :], scratch["h"]),
                      (NG * 3 // 4 + 1, st_mn, mn_ok, 1, mn_sb[:, :, :], scratch["mn"]),
                      (NG - 1, st_mnT, mnT_ok, 2, mnT_sb[:, :, :], scratch["mnT"]))

            with sp.Fori(0, pr.B) as b:
                sp.wait_ge(xm_lo, b * NC)
                load_x(b, 0, xp_ld)

                def project(c, J, h, last):
                    sp.wait_ge(xp_lo, J + 1)
                    if last:
                        load_x(b, 0, xm_ld)
                    else:
                        load_x(b, c + 1, xp_ld)

                projection(sp, b, project)

                def attend(c, M, h, first, last):
                    if not last:
                        sp.wait_ge(xm_lo, M + 1)
                        load_x(b, c + 1, xm_ld)
                    for g in range(NG):
                        if first and g < RG:
                            sp.wait_ge(mul_done, M * ST)
                        else:
                            sp.wait_ge(mul_done, M * ST + (g - RG + 1) * GT)
                        sp.dma_start(gate[:, g % RG, :, :], ins["gateT"][c, g]).then_inc(gate_ld[g % RG], 16)
                        if not first:
                            for at, *what in stores:
                                if g == at:
                                    store(M - 1, b, c - 1, *what)

                attention(sp, b, attend)
                for _, *what in stores:
                    store(b * NC + NC - 1, b, NC - 1, *what)
            for sem in (st_h, st_mn, st_mnT):
                sp.wait_ge(sem, 16 * pr.B * NC)

        @block.scalar
        def _(act):
            def split_x(half, sem_ld, sem_hi, J):
                act.wait_ge(sem_ld, (J + 1) * 16)
                nc.scalar.activation(x_hi[:, half], x32[:, :, :], ACT.Copy).then_inc(sem_hi, 1)

            def keep_mnT(Q):
                act.wait_ge(mn_turned, Q + 1)
                act.wait_ge(st_mnT, Q * 16)
                for m in range(KD):
                    nc.scalar.activation(mnT_sb[:, m, :], TR[2 + m][:, :], ACT.Copy).then_inc(mnT_ok, 1)

            def keep_y(Q):
                act.wait_ge(ret_done, (Q + 1) * ST)
                nc.scalar.activation(yT[:, 0, :], Y[0][:, :], ACT.Identity,
                                     bias=W["bo_col"][:, 0:1]).then_inc(y_evac, 1)

            with act.Fori(0, pr.B) as b:
                split_x(0, xp_ld, xp_hi, b * NC)

                def project(c, J, h, last):
                    if last:
                        split_x(1 - h, xm_ld, xm_hi, b * NC)
                    else:
                        split_x(1 - h, xp_ld, xp_hi, J + 1)
                    for m in range(KD):
                        if m == 0:
                            act.wait_ge(k_lo_ok, J * 2)
                        act.wait_ge(kp, J * 2 + m + 1)
                        nc.scalar.activation(p32[:, m, :], KP[m][:, :], ACT.Identity,
                                             bias=W["bk_col"][:, m:m + 1]).then_inc(k_evac, 1)
                        act.wait_ge(k_evac, J * 2 + m + 1)
                        nc.scalar.activation(kt_hi[:, m, bass.ds(c * CH, CH)], p32[:, m, :],
                                             ACT.Copy).then_inc(k_hi_ok, 1)
                    for j in range(TPC):
                        act.wait_ge(v_evac, J * TPC + j + 1)
                        nc.scalar.activation(v_hi[:, c * TPC + j, :], vf[:, j % 2, 0:D],
                                             ACT.Copy).then_inc(v_hi_ok, 1)

                projection(act, b, project)

                def attend(c, M, h, first, last):
                    for i in range(ST):
                        if i == 1 and not first:
                            keep_y(M - 1)
                        act.wait_ge(mul_done, M * ST + i + 1)
                        if not (first and i < 2):
                            act.wait_ge(ret_done, M * ST + i - 1)
                        nc.scalar.activation(p_hi[:, i % 2, :], p32[:, i % RP, :], ACT.Copy).then_inc(hi_done, 1)
                        if i == SPLIT_X and not last:
                            split_x(1 - h, xm_ld, xm_hi, M + 1)
                        if i == KEEP_MN and not first:
                            keep_mnT(M - 1)

                attention(act, b, attend)
                keep_y(b * NC + NC - 1)
                keep_mnT(b * NC + NC - 1)

        @block.vector
        def _(dve):
            def split_x(half, sem_hi, sem_lo, J):
                dve.wait_ge(sem_hi, J + 1)
                nc.vector.tensor_tensor(x_lo[:, half], x32[:, :, :], x_hi[:, half].bitcast(F32),
                                        ALU.subtract).then_inc(sem_lo, 1)

            def keep_y(Q):
                dve.wait_ge(ret_done, (Q + 1) * ST)
                nc.vector.tensor_scalar(yT[:, 1, :], Y[1][:, :], W["bo_col"][:, 1:2], None,
                                        ALU.add).then_inc(y_evac, 1)

            def rectify(Q):
                dve.wait_ge(y_turned, Q + 1)
                dve.wait_ge(st_h, Q * 16)
                dve.wait_ge(st_mn, Q * 16)
                for i in range(2):
                    nc.vector.tensor_scalar(mn_sb[:, 2 * i:2 * i + 2, :], TR[i][:, :], 0.0, W["prelu"][:, 0:1],
                                            ALU.min, ALU.mult).then_inc(neg_ok, 1)
                for i in range(2):
                    dve.wait_ge(neg_ok, Q * 2 + i + 1)
                    nc.vector.scalar_tensor_tensor(h_sb[:, 2 * i:2 * i + 2, :], TR[i][:, :], 0.0,
                                                   mn_sb[:, 2 * i:2 * i + 2, :], ALU.max, ALU.add).then_inc(h_ok, 1)
                for j in range(TPC):
                    dve.wait_ge(h_ok, Q * 2 + j // 2 + 1)
                    nc.vector.bn_stats(stats[:, j, :], h_sb[:, j, :]).then_inc(stats_ok, 1)
                for j in range(TPC):
                    dve.wait_ge(stats_ok, Q * TPC + j + 1)
                    pr.stand_alone(dve)
                    nc.vector.bn_aggr(mv[:, j, :], stats[:, j, :]).then_inc(mv_ok, 1)

            def norm(Q):
                dve.wait_ge(rstd_ok, Q + 1)
                for j in range(TPC):
                    nc.vector.tensor_scalar(mn_sb[:, j, :], h_sb[:, j, :], mv[:, j, 0:1], rstd[:, j:j + 1],
                                            ALU.subtract, ALU.mult).then_inc(z_ok, 1)

            with dve.Fori(0, pr.B) as b:
                split_x(0, xp_hi, xp_lo, b * NC)

                def project(c, J, h, last):
                    if last:
                        split_x(1 - h, xm_hi, xm_lo, b * NC)
                    else:
                        split_x(1 - h, xp_hi, xp_lo, J + 1)
                    for m in range(KD):
                        dve.wait_ge(k_hi_ok, J * 2 + m + 1)
                        nc.vector.tensor_tensor(kt_lo[:, m, bass.ds(c * CH, CH)], p32[:, m, :],
                                                kt_hi[:, m, bass.ds(c * CH, CH)].bitcast(F32),
                                                ALU.subtract).then_inc(k_lo_ok, 1)
                    for j in range(TPC):
                        dve.wait_ge(v_lo_ok, J * TPC + max(j - 1, 0))
                        dve.wait_ge(vp, J * TPC + j + 1)
                        nc.vector.tensor_tensor(vf[:, j % 2, :], VP[j][:, 0:D + 2], W["v_bias"][:, :],
                                                ALU.add).then_inc(v_evac, 1)

                projection(dve, b, project)

                def attend(c, M, h, first, last):
                    def low(i):
                        dve.wait_ge(hi_done, M * ST + i + 1)
                        nc.vector.tensor_tensor(p_lo[:, i % 2, :], p32[:, i % RP, :], p_hi[:, i % 2, :].bitcast(F32),
                                                ALU.subtract).then_inc(lo_done, 1)

                    if first:
                        dve.wait_ge(d_ok, (b + 1) * NC * TPC)
                    for i in range(ST):
                        g, j = i // GT, i % GT
                        dve.wait_ge(scores, M * ST + i + 1)
                        if j == 0:
                            dve.wait_ge(gate_ld[g % RG], (M * (NG // RG) + g // RG + 1) * 16)
                        if not (first and i < RP):
                            dve.wait_ge(lo_done, M * ST + i - RP + 1)
                        elif i < KD:
                            dve.wait_ge(k_lo_ok, (b + 1) * NC * KD)
                        nc.vector.scalar_tensor_tensor(p32[:, i % RP, :], S[i % 2][:, :], d_col[:, i:i + 1],
                                                       gate[:, g % RG, j, :], ALU.add, ALU.mult).then_inc(mul_done, 1)
                        if i == 1 and not first:
                            keep_y(M - 1)
                        if i:
                            low(i - 1)
                        if i == SPLIT_X and not last:
                            split_x(1 - h, xm_hi, xm_lo, M + 1)
                        if not first:
                            if i == RECTIFY:
                                rectify(M - 1)
                            if i == NORM:
                                norm(M - 1)
                    low(ST - 1)

                attention(dve, b, attend)
                keep_y(b * NC + NC - 1)
                rectify(b * NC + NC - 1)
                norm(b * NC + NC - 1)

        @block.gpsimd
        def _(pool):
            nc.gpsimd.memset(power[:, :], -0.5).then_inc(power_ok, 1)

            def scale(Q):
                pool.wait_ge(mv_ok, (Q + 1) * TPC)
                pr.stand_alone(pool)
                nc.gpsimd.tensor_scalar(spread[:, :], mv[:, :, 1], 1.0 + EPS, EPS * EPS, ALU.mult,
                                        ALU.add).then_inc(spread_ok, 1)
                pool.wait_ge(spread_ok, Q + 1)
                pool.wait_ge(power_ok, 1)
                nc.gpsimd.tensor_tensor(rstd[:, :], spread[:, :], power[:, :], ALU.pow).then_inc(rstd_ok, 1)
                pool.wait_ge(z_ok, (Q + 1) * TPC)
                for j in range(TPC):
                    nc.gpsimd.tensor_tensor(mn_sb[:, j, :], mn_sb[:, j, :], W["gamma"][:, :],
                                            ALU.mult).then_inc(scaled, 1)
                for j in range(TPC):
                    pool.wait_ge(scaled, Q * TPC + j + 1)
                    ins_ = nc.gpsimd.tensor_tensor(mn_sb[:, j, :], mn_sb[:, j, :], W["beta"][:, :], ALU.add)
                ins_.then_inc(mn_ok, 1)

            with pool.Fori(0, pr.B) as b:
                def project(c, J, h, last):
                    for j in range(TPC):
                        pool.wait_ge(v_evac, J * TPC + j + 1)
                        pr.stand_alone(pool)
                        nc.gpsimd.tensor_copy(d_col[:, bass.ds(c * TPC + j, 1)], vf[:, j % 2, D:D + 1]).then_inc(d_ok, 1)
                        pool.wait_ge(v_hi_ok, J * TPC + j + 1)
                        nc.gpsimd.tensor_tensor(v_lo[:, c * TPC + j, :], vf[:, j % 2, 0:D],
                                                v_hi[:, c * TPC + j, :].bitcast(F32), ALU.subtract).then_inc(v_lo_ok, 1)

                projection(pool, b, project)

                def attend(c, M, h, first, last):
                    if not first:
                        scale(M - 1)

                attention(pool, b, attend)
                scale(b * NC + NC - 1)

        @block.tensor
        def _(pe):
            def turn_y(Q):
                pe.wait_ge(y_evac, (Q + 1) * 2)
                for j in range(TPC):
                    for m in range(KD):
                        last = pe.transpose(TR[j // 2][:, (j % 2) * D + m * P:(j % 2) * D + (m + 1) * P],
                                            yT[:, m, j * P:(j + 1) * P], ident[:, :])
                last.then_inc(y_turned, 1)

            def turn_mn(Q):
                pe.wait_ge(mn_ok, Q + 1)
                pe.wait_ge(mnT_ok, Q * 2)
                for m in range(KD):
                    for j in range(TPC):
                        last = pe.transpose(TR[2 + m][:, j * P:(j + 1) * P], mn_sb[:, j, m * P:(m + 1) * P], ident[:, :])
                last.then_inc(mn_turned, 1)

            with pe.Fori(0, pr.B) as b:
                pe.wait_ge(y_evac, b * NC * 2)
                pr.stand_alone(pe)

                def project(c, J, h, last):
                    pe.wait_ge(xp_lo, J + 1)
                    pe.wait_ge(k_evac, J * 2)
                    for m in range(KD):
                        cols = slice(m * P, (m + 1) * P)
                        n = 0
                        for k in range(KD):
                            for w, x in split_products(W["a_hi"][:, k, cols], W["a_lo"][:, k, cols],
                                                       x_hi[:, h, k, :], x_lo[:, h, k, :]):
                                n += 1
                                mm = pe.matmul(KP[m][:, :], w, x, start=n == 1, stop=n == 3 * KD)
                        mm.then_inc(kp, 1)
                    pe.wait_ge(v_evac, J * TPC)
                    for j in range(TPC):
                        rows = slice(j * P, (j + 1) * P)
                        n = 0
                        for k in range(KD):
                            for x, w in split_products(x_hi[:, h, k, rows], x_lo[:, h, k, rows],
                                                       W["vo_hi"][:, k, :], W["vo_lo"][:, k, :]):
                                n += 1
                                mm = pe.matmul(VP[j][:, 0:D + 2], x, w, start=n == 1, stop=n == 3 * KD)
                        mm.then_inc(vp, 1)

                projection(pe, b, project)
                pe.wait_ge(k_lo_ok, (b + 1) * NC * 2)
                pe.wait_ge(v_lo_ok, (b + 1) * NC * TPC)
                pr.stand_alone(pe)

                def retain(M, i):
                    pe.wait_ge(lo_done, M * ST + i + 1)
                    if i == 0:
                        pe.wait_ge(y_evac, M * 2)
                    for m in range(KD):
                        cols = slice(m * P, (m + 1) * P)
                        for n, (v, p) in enumerate(split_products(v_hi[:, i, cols], v_lo[:, i, cols],
                                                                  p_hi[:, i % 2, :], p_lo[:, i % 2, :])):
                            mm = pe.matmul(Y[m][:, :], v, p, start=i == 0 and n == 0, stop=i == ST - 1 and n == 2)
                    mm.then_inc(ret_done, 1)

                def attend(c, M, h, first, last):
                    pe.wait_ge(xm_lo, M + 1)
                    for i in range(ST):
                        if not (first and i < 2):
                            pe.wait_ge(mul_done, M * ST + i - 1)
                        rows = slice(i * P, (i + 1) * P)
                        n = 0
                        for k in range(KD):
                            for w, x in split_products(kt_hi[:, k, rows], kt_lo[:, k, rows],
                                                       x_hi[:, h, k, :], x_lo[:, h, k, :]):
                                n += 1
                                mm = pe.matmul(S[i % 2][:, :], w, x, start=n == 1, stop=n == 3 * KD)
                        mm.then_inc(scores, 1)
                        if i >= 2:
                            retain(M, i - 2)
                        elif not first:
                            retain(M - 1, ST - 2 + i)
                        if not first:
                            if i == TURN_Y:
                                turn_y(M - 1)
                            if i == TURN_MN:
                                turn_mn(M - 1)

                attention(pe, b, attend)
                for i in (ST - 2, ST - 1):
                    retain(b * NC + NC - 1, i)
                turn_y(b * NC + NC - 1)
                turn_mn(b * NC + NC - 1)


def gram(pr, scratch, grams):
    nc, D, KD, NC = pr.nc, pr.D, pr.KD, pr.NC
    with ExitStack() as ctx:
        m32 = sb(nc, ctx, "m32", [P, 2, 2, TPC, D])
        m_hi, m_lo = (sb(nc, ctx, n, [P, 2, 2, TPC, D], F32R) for n in ("gm_hi", "gm_lo"))
        G = [ps(nc, ctx, f"G{i}") for i in range(4)]
        ld = [pr.sem(f"gm_ld{h}") for h in range(2)]
        hi_ok, lo_ok, done, kept = (pr.sem(n) for n in ("gm_hi", "gm_lo", "gm_done", "gm_kept"))
        block = ctx.enter_context(nc.Block())

        def chunks(eng, step):
            for c in range(2):
                step(c, c, c == 0)
            with eng.Fori(1, NC // 2) as p:
                for h in range(2):
                    step(p * 2 + h, h, False)

        @block.sync
        def _(sp):
            def step(c, h, first):
                if not early(c, 2):
                    sp.wait_ge(lo_ok, c - 1)
                for b in range(2):
                    sp.dma_start(m32[:, h, b], scratch["mn"][b, c]).then_inc(ld[h], 16)
            chunks(sp, step)

        @block.scalar
        def _(act):
            def step(c, h, first):
                act.wait_ge(ld[h], (c - h) * 16 + 32)
                if not early(c, 2):
                    act.wait_ge(done, c - 1)
                nc.scalar.activation(m_hi[:, h], m32[:, h], ACT.Copy).then_inc(hi_ok, 1)
            chunks(act, step)

        @block.vector
        def _(dve):
            def step(c, h, first):
                dve.wait_ge(hi_ok, c + 1)
                nc.vector.tensor_tensor(m_lo[:, h], m32[:, h], m_hi[:, h].bitcast(F32), ALU.subtract).then_inc(lo_ok, 1)
            chunks(dve, step)
            dve.wait_ge(done, NC)
            for i in range(4):
                n = 2 * D if i < 2 else D
                nc.vector.tensor_copy(grams[:, i, 0:n], G[i][:, 0:n]).then_inc(kept, 1)
            dve.wait_ge(kept, 4)

        @block.tensor
        def _(pe):
            def step(c, h, first):
                pe.wait_ge(lo_ok, c + 1)
                for j in range(TPC):
                    for i in range(4):
                        b, cols = i // 2, slice((i % 2) * P, (i % 2 + 1) * P)
                        out = G[i][:, 0:2 * D] if b == 0 else G[i][:, 0:D]
                        for n, (w, x) in enumerate(split_products(
                                m_hi[:, h, b, j, cols], m_lo[:, h, b, j, cols],
                                m_hi[:, h, b:2, j, :], m_lo[:, h, b:2, j, :])):
                            mm = pe.matmul(out, w, x, start=first and j == 0 and n == 0, stop=False,
                                           skip_group_check=True)
                mm.then_inc(done, 1)
            chunks(pe, step)


def head_weights(pr, W2, grams):
    nc, ins, D, KD, B = pr.nc, pr.ins, pr.D, pr.KD, pr.B
    head = D // pr.H
    scale = head ** -0.5 * pr.T ** -0.5
    with ExitStack() as ctx:
        wq, wk = sb(nc, ctx, "wq", [P, KD, D]), sb(nc, ctx, "wk", [P, KD, D])
        wsrc = {n: sb(nc, ctx, f"src_{n}", [P, KD, D]) for n in ("v", "g", "o")}
        prod = sb(nc, ctx, "prod", [P, 4, KD, D])
        same_head = sb(nc, ctx, "same_head", [P, P])
        ones = sb(nc, ctx, "ones_att", [P, 2])
        cols, att = sb(nc, ctx, "cols", [P, 16]), sb(nc, ctx, "att", [P, 2, 2, 2])
        top, shifted, expd, total, inv = (sb(nc, ctx, n, sh) for n, sh in (
            ("top", [P, 2, 2]), ("shifted", [P, 2, 2, 2]), ("expd", [P, 2, 2, 2]), ("total", [P, 2, 2]), ("inv", [P, 2, 2])))
        TP = [ps(nc, ctx, f"TP{i}", (P, KD, D)) for i in range(4)]
        colp, attp = ps(nc, ctx, "colp"), ps(nc, ctx, "attp")
        ld, made, tp, prod_ok, col_ok, cols_sb, att_ok, step, exp_ok, whi = (pr.sem(n) for n in (
            "hw_ld", "hw_made", "hw_tp", "hw_prod", "hw_col", "hw_cols", "hw_att", "hw_step", "hw_exp", "hw_hi"))
        block = ctx.enter_context(nc.Block())
        n_ld = 5 + 1 + TPC + 2

        @block.sync
        def _(sp):
            for t, n in ((wq, "attn_Wq"), (wk, "attn_Wk"), (wsrc["v"], "attn_Wv"), (wsrc["g"], "attn_Wg"), (wsrc["o"], "attn_Wo")):
                sp.dma_start(t[:, :, :], ins[n].rearrange("(k p) n -> p k n", p=P)).then_inc(ld, 16)
            with nc.allow_non_contiguous_dma(reason="a bias column, once"):
                sp.dma_start(W2["bg_col"][:, :], ins["attn_bg"].rearrange("(k p) -> p k", p=P)).then_inc(ld, 16)
            for j in range(TPC):
                sp.dma_start(W2["bo4"][:, j, :], ins["attn_bo"].partition_broadcast(P)).then_inc(ld, 16)
            sp.dma_start(W2["wr"][:, :], ins["ffn_wr"].partition_broadcast(P)).then_inc(ld, 16)
            sp.dma_start(W2["br"][:, :], ins["ffn_br"].partition_broadcast(P)).then_inc(ld, 16)

        @block.gpsimd
        def _(pool):
            nc.gpsimd.memset(same_head[:, :], 0.0).then_inc(made, 1)
            nc.gpsimd.memset(ones[:, :], 1.0).then_inc(made, 1)
            pool.wait_ge(made, 2)
            for h in range(P // head):
                r = slice(h * head, (h + 1) * head)
                nc.gpsimd.memset(same_head[r, r], 1.0).then_inc(made, 1)

        @block.tensor
        def _(pe):
            pe.wait_ge(ld, 16 * n_ld)
            for i, (g0, c0, w) in enumerate(((0, 0, wk), (0, D, wq), (0, D, wk), (2, 0, wk))):
                for m in range(KD):
                    for k in range(KD):
                        mm = pe.matmul(TP[i][:, m, :], grams[:, g0 + k, c0 + m * P:c0 + (m + 1) * P], w[:, k, :],
                                       start=m == 0 and k == 0, stop=k == KD - 1, skip_group_check=True)
                mm.then_inc(tp, 1)
            pe.wait_ge(made, 2 + P // head)
            for i in range(4):
                pe.wait_ge(prod_ok, i + 1)
                for j in range(KD):
                    for m in range(KD):
                        mm = pe.matmul(colp[:, 4 * i + 2 * j:4 * i + 2 * j + 2], prod[:, i, m, j * P:(j + 1) * P], ones[:, :],
                                       start=i == 0 and j == 0 and m == 0, stop=m == KD - 1, skip_group_check=True)
            mm.then_inc(col_ok, 1)
            pe.wait_ge(cols_sb, 1)
            pe.matmul(attp[:, 0:16], same_head[:, :], cols[:, :], start=True, stop=True).then_inc(att_ok, 1)

        @block.vector
        def _(dve):
            dve.wait_ge(ld, 16 * n_ld)
            for i, w in enumerate((wq, wk, wq, wq)):
                dve.wait_ge(tp, i + 1)
                nc.vector.tensor_tensor(prod[:, i], TP[i][:, :, :], w[:, :, :], ALU.mult).then_inc(prod_ok, 1)
            for n, x in enumerate("vgo"):
                dve.wait_ge(whi, n + 1)
                nc.vector.tensor_tensor(W2[x + "_lo"][:, :, :], wsrc[x][:, :, :], W2[x + "_hi"][:, :, :].bitcast(F32),
                                        ALU.subtract).then_inc(prod_ok, 1)
            dve.wait_ge(col_ok, 1)
            nc.vector.tensor_copy(cols[:, :], colp[:, 0:16]).then_inc(cols_sb, 1)
            dve.wait_ge(att_ok, 1)
            nc.vector.tensor_copy(att[:, :, :, :], attp[:, 0:16:2].rearrange("p (s t j) -> p s t j", s=2, t=2)).then_inc(step, 1)
            dve.wait_ge(step, 1)
            nc.vector.tensor_tensor(top[:, :, :], att[:, :, 0, :], att[:, :, 1, :], ALU.max).then_inc(step, 1)
            dve.wait_ge(step, 2)
            for t in range(2):
                nc.vector.tensor_tensor(shifted[:, :, t, :], att[:, :, t, :], top[:, :, :], ALU.subtract).then_inc(step, 1)
            dve.wait_ge(exp_ok, 1)
            nc.vector.tensor_tensor(total[:, :, :], expd[:, :, 0, :], expd[:, :, 1, :], ALU.add).then_inc(step, 1)
            dve.wait_ge(step, 5)
            nc.vector.reciprocal(inv[:, :, :], total[:, :, :]).then_inc(step, 1)
            dve.wait_ge(step, 6)
            for t in range(2):
                nc.vector.tensor_tensor(W2["att"][:, :, t, :], expd[:, :, t, :], inv[:, :, :], ALU.mult).then_inc(step, 1)
            dve.wait_ge(step, 8)

        @block.scalar
        def _(act):
            act.wait_ge(ld, 16 * n_ld)
            for x in "vgo":
                nc.scalar.activation(W2[x + "_hi"][:, :, :], wsrc[x][:, :, :], ACT.Copy).then_inc(whi, 1)
            act.wait_ge(step, 4)
            nc.scalar.activation(expd[:, :, :, :], shifted[:, :, :, :], ACT.Exp, scale=scale).then_inc(exp_ok, 1)


def mix(pr, W2, ident, scratch, base, router):
    nc, D, KD, NC = pr.nc, pr.D, pr.KD, pr.NC
    with ExitStack() as ctx:
        m32 = sb(nc, ctx, "mT32", [P, 2, KD, CH])
        m_hi, m_lo = (sb(nc, ctx, n, [P, 2, 2, KD, CH], F32R) for n in ("mT_hi", "mT_lo"))
        og_hi, og_lo = (sb(nc, ctx, n, [P, 2, 2, KD, CH], F32R) for n in ("og_hi", "og_lo"))
        h_in = sb(nc, ctx, "h_in", [P, 2, 2, TPC, D])
        xn = sb(nc, ctx, "xn", [P, 2, 2, TPC, D])
        xnT = sb(nc, ctx, "xnT", [P, 2, KD, CH])
        t1, o32, g_sb, og32 = (sb(nc, ctx, n, [P, 2, CH]) for n in ("t1", "o32", "g_sb", "og32"))
        stats, mv = sb(nc, ctx, "stats2", [P, 2, TPC, 6]), sb(nc, ctx, "mv2", [P, 2, TPC, 2])
        spread, rstd, power = (sb(nc, ctx, n, [P, 2, TPC]) for n in ("spread2", "rstd2", "power2"))
        scrap, w_now = sb(nc, ctx, "scrap", [P, D]), sb(nc, ctx, "w_now", [P, 2, TPC])
        V = [ps(nc, ctx, f"V{i}") for i in range(2)]
        GB = [ps(nc, ctx, f"GB{i}") for i in range(2)]
        OP = [ps(nc, ctx, f"OP{i}") for i in range(2)]
        TR = [ps(nc, ctx, f"XT{i}") for i in range(2)]
        (m_ld, hi_ok, lo_ok, vv, gg, t_ok, g_ok, o_ok, og_ok, ogh_ok, ogl_ok, op, hb_ok, h2_ok, st_ok, mv_ok,
         sp_ok, rs_ok, xn_ok, base_ok, w_ok, w_kept, turned, xnT_ok, power_ok) = (pr.sem("mx_" + n) for n in (
            "m_ld", "hi_ok", "lo_ok", "vv", "gg", "t_ok", "g_ok", "o_ok", "og_ok", "ogh_ok", "ogl_ok", "op",
            "hb_ok", "h2_ok", "st_ok", "mv_ok", "sp_ok", "rs_ok", "xn_ok", "base_ok", "w_ok", "w_kept",
            "turned", "xnT_ok", "power_ok"))
        h_ld = [pr.sem(f"mx_h_ld{h}") for h in range(2)]
        st_x = [pr.sem(f"mx_st_x{s}") for s in range(2)]
        block = ctx.enter_context(nc.Block())

        def chunks(eng, step):
            for c in range(2):
                step(c, c)
            if NC > 4:
                with eng.Fori(1, NC // 2 - 1) as p:
                    for h in range(2):
                        step(p * 2 + h, h)
            for c in range(NC - 2, NC):
                step(c, c % 2)

        def last(c):
            return isinstance(c, int) and c == NC - 1

        @block.sync
        def _(sp):
            def load_m(c):
                for b in range(2):
                    sp.dma_start(m32[:, b], scratch["mnT"][b, c]).then_inc(m_ld, 16)

            def store(c):
                for s in range(2):
                    sp.wait_ge(xnT_ok, c * 4 + 2 * s + 2)
                    sp.dma_start(scratch["xnT"][s, c], xnT[:, s]).then_inc(st_x[s], 16)

            def step(c, h):
                if not last(c):
                    sp.wait_ge(lo_ok, c + 1)
                    load_m(c + 1)
                if not early(c, 2):
                    sp.wait_ge(base_ok, c * 2 - 2)
                for s in range(2):
                    sp.dma_start(h_in[:, h, s], scratch["h"][s, c]).then_inc(h_ld[h], 16)
                if not early(c, 2):
                    store(c - 2)

            load_m(0)
            chunks(sp, step)
            store(NC - 2)
            store(NC - 1)
            for s in range(2):
                sp.wait_ge(st_x[s], 16 * NC)

        @block.scalar
        def _(act):
            def split(c, h):
                act.wait_ge(m_ld, (c + 1) * 32)
                nc.scalar.activation(m_hi[:, h], m32[:, :, :, :], ACT.Copy).then_inc(hi_ok, 1)

            def keep_xT(c):
                for s in range(2):
                    act.wait_ge(st_x[s], c * 16)
                    act.wait_ge(turned, c * 2 + s + 1)
                    for k in range(KD):
                        nc.scalar.activation(xnT[:, s, k, :], TR[k][:, :], ACT.Copy).then_inc(xnT_ok, 1)

            def step(c, h):
                for j in range(KD):
                    n = c * 4 + 2 * j
                    act.wait_ge(vv, n + 2)
                    if not (early(c, 1) and j == 0):
                        act.wait_ge(o_ok, n)
                    for s in range(2):
                        nc.scalar.activation(t1[:, s, :], V[1][:, :], ACT.Copy,
                                             scale=W2["att"][:, s, 1, j:j + 1]).then_inc(t_ok, 1)
                    for s in range(2):
                        act.wait_ge(gg, n + s + 1)
                        if not (early(c, 1) and j == 0):
                            act.wait_ge(og_ok, n)
                        nc.scalar.activation(g_sb[:, s, :], GB[s][:, :], ACT.Sigmoid,
                                             bias=W2["bg_col"][:, j:j + 1]).then_inc(g_ok, 1)
                    for s in range(2):
                        if not early(c, 2):
                            act.wait_ge(op, (c - 1) * 4)
                        act.wait_ge(og_ok, n + s + 1)
                        nc.scalar.activation(og_hi[:, h, s, j, :], og32[:, s, :], ACT.Copy).then_inc(ogh_ok, 1)
                if not last(c):
                    split(c + 1, 1 - h)
                if not early(c, 2):
                    keep_xT(c - 2)

            split(0, 0)
            chunks(act, step)
            keep_xT(NC - 2)
            keep_xT(NC - 1)

        @block.vector
        def _(dve):
            def split(c, h):
                dve.wait_ge(hi_ok, c + 1)
                nc.vector.tensor_tensor(m_lo[:, h], m32[:, :, :, :], m_hi[:, h].bitcast(F32), ALU.subtract).then_inc(lo_ok, 1)

            def norm(c, h):
                for s in range(2):
                    dve.wait_ge(hb_ok, c * 2 + s + 1)
                    for i in range(2):
                        dve.wait_ge(op, c * 4 + 2 * s + i + 1)
                        nc.vector.tensor_tensor(h_in[:, h, s, 2 * i:2 * i + 2, :], OP[i][:, :],
                                                h_in[:, h, s, 2 * i:2 * i + 2, :], ALU.add).then_inc(h2_ok, 1)
                    for j in range(TPC):
                        dve.wait_ge(h2_ok, c * 4 + 2 * s + j // 2 + 1)
                        nc.vector.bn_stats(stats[:, s, j, :], h_in[:, h, s, j, :]).then_inc(st_ok, 1)
                    for j in range(TPC):
                        dve.wait_ge(st_ok, c * 8 + 4 * s + j + 1)
                        pr.stand_alone(dve)
                        nc.vector.bn_aggr(mv[:, s, j, :], stats[:, s, j, :]).then_inc(mv_ok, 1)
                for s in range(2):
                    dve.wait_ge(rs_ok, c * 2 + s + 1)
                    for j in range(TPC):
                        nc.vector.tensor_scalar(xn[:, h, s, j, :], h_in[:, h, s, j, :], mv[:, s, j, 0:1],
                                                rstd[:, s, j:j + 1], ALU.subtract, ALU.mult).then_inc(xn_ok, 1)
                dve.wait_ge(w_kept, c)
                for s in range(2):
                    for j in range(TPC):
                        dve.wait_ge(xn_ok, c * 8 + 4 * s + j + 1)
                        nc.vector.tensor_tensor_reduce(out=scrap[:, :], in0=xn[:, h, s, j, :], in1=W2["wr"][:, :],
                                                       scale=1.0, scalar=0.0, op0=ALU.mult, op1=ALU.add,
                                                       accum_out=w_now[:, s, j:j + 1]).then_inc(w_ok, 1)
                        dve.wait_ge(w_ok, c * 8 + 4 * s + j + 1)
                nc.vector.tensor_copy(router[:, :, bass.ds(c * TPC, TPC)], w_now[:, :, :]).then_inc(w_kept, 1)

            def step(c, h):
                for j in range(KD):
                    n = c * 4 + 2 * j
                    for s in range(2):
                        dve.wait_ge(t_ok, n + s + 1)
                        if not (early(c, 1) and j == 0):
                            dve.wait_ge(og_ok, n)
                        nc.vector.scalar_tensor_tensor(o32[:, s, :], V[0][:, :], W2["att"][:, s, 0, j:j + 1], t1[:, s, :],
                                                       ALU.mult, ALU.add).then_inc(o_ok, 1)
                if not last(c):
                    split(c + 1, 1 - h)
                if not early(c, 1):
                    norm(c - 1, 1 - h)

            split(0, 0)
            chunks(dve, step)
            norm(NC - 1, 1)
            dve.wait_ge(w_kept, NC)

        @block.gpsimd
        def _(pool):
            nc.gpsimd.memset(power[:, :, :], -0.5).then_inc(power_ok, 1)

            def finish(c, h):
                for s in range(2):
                    pool.wait_ge(mv_ok, c * 8 + 4 * s + 4)
                    pr.stand_alone(pool)
                    nc.gpsimd.tensor_scalar(spread[:, s, :], mv[:, s, :, 1], EPS, None, ALU.add).then_inc(sp_ok, 1)
                    pool.wait_ge(power_ok, 1)
                    pool.wait_ge(sp_ok, c * 2 + s + 1)
                    nc.gpsimd.tensor_tensor(rstd[:, s, :], spread[:, s, :], power[:, s, :], ALU.pow).then_inc(rs_ok, 1)
                for s in range(2):
                    pool.wait_ge(xn_ok, c * 8 + 4 * s + 4)
                    nc.gpsimd.tensor_tensor(base[:, s, bass.ds(c * TPC, TPC), :], h_in[:, h, s], xn[:, h, s],
                                            ALU.add).then_inc(base_ok, 1)

            def step(c, h):
                pool.wait_ge(h_ld[h], (c - h) * 16 + 32)
                for s in range(2):
                    nc.gpsimd.tensor_tensor(h_in[:, h, s], h_in[:, h, s], W2["bo4"][:, :, :], ALU.add).then_inc(hb_ok, 1)
                for j in range(KD):
                    n = c * 4 + 2 * j
                    for s in range(2):
                        pool.wait_ge(o_ok, n + s + 1)
                        pool.wait_ge(g_ok, n + s + 1)
                        if not (early(c, 1) and j == 0):
                            pool.wait_ge(ogl_ok, n)
                        nc.gpsimd.tensor_tensor(og32[:, s, :], o32[:, s, :], g_sb[:, s, :], ALU.mult).then_inc(og_ok, 1)
                    for s in range(2):
                        pool.wait_ge(ogh_ok, n + s + 1)
                        nc.gpsimd.tensor_tensor(og_lo[:, h, s, j, :], og32[:, s, :], og_hi[:, h, s, j, :].bitcast(F32),
                                                ALU.subtract).then_inc(ogl_ok, 1)
                if not early(c, 1):
                    finish(c - 1, 1 - h)

            chunks(pool, step)
            finish(NC - 1, 1)
            pool.wait_ge(base_ok, 2 * NC)

        @block.tensor
        def _(pe):
            def values_and_gates(c, h):
                pe.wait_ge(lo_ok, c + 1)
                for j in range(KD):
                    cols = slice(j * P, (j + 1) * P)
                    n = c * 4 + 2 * j
                    if not (early(c, 1) and j == 0):
                        pe.wait_ge(o_ok, n)
                    for w, bank, sem, b in (("v", V[1], vv, 1), ("v", V[0], vv, 0), ("g", GB[0], gg, 0), ("g", GB[1], gg, 1)):
                        if w == "g" and not (early(c, 1) and j == 0):
                            pe.wait_ge(g_ok, n - 1 + b)
                        i = 0
                        for k in range(KD):
                            for ww, x in split_products(W2[w + "_hi"][:, k, cols], W2[w + "_lo"][:, k, cols],
                                                        m_hi[:, h, b, k, :], m_lo[:, h, b, k, :]):
                                i += 1
                                mm = pe.matmul(bank[:, :], ww, x, start=i == 1, stop=i == 3 * KD)
                        mm.then_inc(sem, 1)

            def project(c, h, s):
                pe.wait_ge(ogl_ok, c * 4 + 3 + s)
                for i in range(2):
                    if not (early(c, 1) and s == 0):
                        pe.wait_ge(h2_ok, c * 4 + 2 * s - 1 + i)
                    for j in (2 * i, 2 * i + 1):
                        rows = slice(j * P, (j + 1) * P)
                        n = 0
                        for k in range(KD):
                            for x, w in split_products(og_hi[:, h, s, k, rows], og_lo[:, h, s, k, rows],
                                                       W2["o_hi"][:, k, :], W2["o_lo"][:, k, :]):
                                mm = pe.matmul(OP[i][:, (j % 2) * D:(j % 2 + 1) * D], x, w,
                                               start=j % 2 == 0 and n == 0, stop=n == 5, skip_group_check=True)
                                n += 1
                    mm.then_inc(op, 1)

            def turn(c, h, s):
                pe.wait_ge(xn_ok, c * 8 + 4 * s + 4)
                if not (early(c, 1) and s == 0):
                    pe.wait_ge(xnT_ok, c * 4 + 2 * s)
                for k in range(KD):
                    for j in range(TPC):
                        t = pe.transpose(TR[k][:, j * P:(j + 1) * P], xn[:, h, s, j, k * P:(k + 1) * P], ident[:, :])
                t.then_inc(turned, 1)

            def step(c, h):
                values_and_gates(c, h)
                for s in range(2):
                    if not early(c, 2):
                        turn(c - 2, h, s)
                    if not early(c, 1):
                        project(c - 1, 1 - h, s)

            chunks(pe, step)
            for s in range(2):
                turn(NC - 2, 0, s)
                project(NC - 1, 1, s)
            for s in range(2):
                turn(NC - 1, 1, s)


STEPS = 4
PIV = 15


def split_mlp_weights(pr, W3):
    nc, ins, KD, F, D = pr.nc, pr.ins, pr.KD, pr.F, pr.D
    FT = F // P
    with ExitStack() as ctx:
        w1, w2 = sb(nc, ctx, "w1", [P, KD, F]), sb(nc, ctx, "w2", [P, FT, D])
        ld, hi, lo, made = (pr.sem(n) for n in ("mw_ld", "mw_hi", "mw_lo", "mw_made"))
        block = ctx.enter_context(nc.Block())

        @block.sync
        def _(sp):
            sp.dma_start(w1[:, :, :], ins["ffn_w1"].rearrange("(k p) n -> p k n", p=P)).then_inc(ld, 16)
            sp.dma_start(w2[:, :, :], ins["ffn_w2"].rearrange("(k p) n -> p k n", p=P)).then_inc(ld, 16)
            for i in range(2):
                sp.dma_start(W3["b2"][:, i, :], ins["ffn_b2"].partition_broadcast(P)).then_inc(ld, 16)
            with nc.allow_non_contiguous_dma(reason="a bias column, once"):
                sp.dma_start(W3["b1"][:, :], ins["ffn_b1"].rearrange("(k p) -> p k", p=P)).then_inc(ld, 16)
            sp.wait_ge(ld, 80)

        @block.gpsimd
        def _(pool):
            nc.gpsimd.memset(W3["ones"][:, :], 1.0).then_inc(made, 1)
            pool.wait_ge(made, 1)
            nc.gpsimd.affine_select(out=W3["before"][:, :], in_=W3["ones"][:, :], compare_op=ALU.is_gt, fill=0.0,
                                    base=0, pattern=[[1, P]], channel_multiplier=-1).then_inc(made, 1)
            nc.gpsimd.iota(W3["index"][:, :], pattern=[[1, PIV]], base=1, channel_multiplier=0).then_inc(made, 1)
            pool.wait_ge(made, 3)
            nc.gpsimd.tensor_copy(W3["digit"][:, :], W3["index"][:, :]).then_inc(made, 1)
            pool.wait_ge(made, 4)

        @block.scalar
        def _(act):
            act.wait_ge(ld, 80)
            nc.scalar.activation(W3["w1_hi"][:, :, :], w1[:, :, :], ACT.Copy).then_inc(hi, 1)
            nc.scalar.activation(W3["w2_hi"][:, :, :], w2[:, :, :], ACT.Copy).then_inc(hi, 1)

        @block.vector
        def _(dve):
            for n, (x, w) in enumerate((("w1", w1), ("w2", w2))):
                dve.wait_ge(hi, n + 1)
                nc.vector.tensor_tensor(W3[x + "_lo"][:, :, :], w[:, :, :], W3[x + "_hi"][:, :, :].bitcast(F32),
                                        ALU.subtract).then_inc(lo, 1)
            dve.wait_ge(lo, 2)


def mlp(pr, W2, W3, scratch, base, router):
    nc, D, KD, NC, ST, F, B = pr.nc, pr.D, pr.KD, pr.NC, pr.ST, pr.F, pr.B
    FT, NU = F // P, B * NC
    K = max(1, int(0.5 * pr.T)) - 1
    LAG = 2
    with ExitStack() as ctx:
        x32 = sb(nc, ctx, "fx32", [P, KD, CH])
        x_hi, x_lo = (sb(nc, ctx, n, [P, 2, KD, CH], F32R) for n in ("fx_hi", "fx_lo"))
        act32 = sb(nc, ctx, "act32", [P, 2, CH])
        a_hi, a_lo = (sb(nc, ctx, n, [P, 2, CH], F32R) for n in ("act_hi", "act_lo"))
        y = sb(nc, ctx, "y", [P, B * ST, D])
        out_sb = sb(nc, ctx, "out_sb", [P, 2, TPC, D])
        key_f, w_br = sb(nc, ctx, "key_f", [P, B, ST]), sb(nc, ctx, "w_br", [P, B, ST])
        low_f, above, equal, pick = (sb(nc, ctx, n, [P, B, ST]) for n in ("low_f", "above", "equal", "pick"))
        sign, key, part = (sb(nc, ctx, n, [P, B, ST], I32) for n in ("sign", "key", "part"))
        equal_b, earlier_b = (sb(nc, ctx, n, [P, B, ST], BF16) for n in ("equal_b", "earlier_b"))
        pivots, counts = sb(nc, ctx, "pivots", [P, B, PIV]), sb(nc, ctx, "counts", [P, B * PIV], BF16)
        passed = sb(nc, ctx, "passed", [P, B, PIV, ST], BF16)
        found, digit, need = sb(nc, ctx, "found", [P, B]), sb(nc, ctx, "dig", [P, B]), sb(nc, ctx, "need", [P, B])
        reach, zero = sb(nc, ctx, "reach", [P, B, PIV]), sb(nc, ctx, "zero", [P, ST])
        high, above_n = sb(nc, ctx, "high", [P, B]), sb(nc, ctx, "above_n", [P, B], BF16)
        HB = [ps(nc, ctx, f"HB{i}") for i in range(2)]
        YB = [[ps(nc, ctx, f"YB{h}{i}") for i in range(2)] for h in range(2)]
        CB = ps(nc, ctx, "CB")
        (x_ld, hi_ok, lo_ok, h1, gelu_ok, ah_ok, al_ok, y_done, y_kept, chain, counted, summed, out_ok) = (
            pr.sem("ff_" + n) for n in ("x_ld", "hi_ok", "lo_ok", "h1", "gelu_ok", "ah_ok", "al_ok", "y_done",
                                        "y_kept", "chain", "counted", "summed", "out_ok"))
        st_out = [pr.sem(f"ff_st_out{h}") for h in range(2)]
        block = ctx.enter_context(nc.Block())

        def chunks(eng, step):
            for u in range(2):
                step(u, u)
            with eng.Fori(1, NU // 2 - 1) as p:
                for h in range(2):
                    step(p * 2 + h, h)
            for u in range(NU - 2, NU):
                step(u, u % 2)

        def last(u):
            return isinstance(u, int) and u == NU - 1

        x_all = scratch["xnT"].rearrange("b c p k t -> (b c) p k t")
        out_all = pr.out.rearrange("b (c j p) d -> (b c) p j d", p=P, j=TPC)

        @block.sync
        def _(sp):
            def store(k, h):
                sp.wait_ge(out_ok, (k + 1) * TPC)
                sp.dma_start(out_all[k], out_sb[:, h]).then_inc(st_out[h], 16)

            def step(u, h):
                if not last(u):
                    sp.wait_ge(lo_ok, u + 1)
                    sp.dma_start(x32[:, :, :], x_all[u + 1]).then_inc(x_ld, 16)
                if not early(u, 2):
                    store(u - 2, h)

            sp.dma_start(x32[:, :, :], x_all[0]).then_inc(x_ld, 16)
            chunks(sp, step)
            store(NU - 2, 0)
            store(NU - 1, 1)
            for h in range(2):
                sp.wait_ge(st_out[h], 16 * (NU // 2))

        @block.scalar
        def _(act):
            def split(u, h):
                act.wait_ge(x_ld, (u + 1) * 16)
                nc.scalar.activation(x_hi[:, h], x32[:, :, :], ACT.Copy).then_inc(hi_ok, 1)

            def step(u, h):
                for j in range(FT):
                    first = early(u, 1) and j < 2
                    act.wait_ge(h1, u * FT + j + 1)
                    if not first:
                        act.wait_ge(al_ok, u * FT + j - 1)
                    nc.scalar.activation(act32[:, j % 2, :], HB[j % 2][:, :], ACT.Gelu_apprx_tanh,
                                         bias=W3["b1"][:, j:j + 1]).then_inc(gelu_ok, 1)
                    if not first:
                        act.wait_ge(y_done, u * FT + j - 1)
                    act.wait_ge(gelu_ok, u * FT + j + 1)
                    nc.scalar.activation(a_hi[:, j % 2, :], act32[:, j % 2, :], ACT.Copy).then_inc(ah_ok, 1)
                    if j == 4 and not last(u):
                        split(u + 1, 1 - h)

            split(0, 0)
            chunks(act, step)

        @block.vector
        def _(dve):
            links = [0]

            def link(ins):
                links[0] += 1
                ins.then_inc(chain, 1)
                dve.wait_ge(chain, links[0])

            def split(u, h):
                dve.wait_ge(hi_ok, u + 1)
                nc.vector.tensor_tensor(x_lo[:, h], x32[:, :, :], x_hi[:, h].bitcast(F32), ALU.subtract).then_inc(lo_ok, 1)

            def make_keys():
                w = w_br[:, :, :]
                link(nc.vector.tensor_scalar(w, router[:, :, :], W2["br"][:, 0:1], None, ALU.add))
                bits = w.bitcast(I32)
                link(nc.vector.tensor_scalar(sign[:, :, :], bits, 31, -2147483648, ALU.arith_shift_right, ALU.bitwise_or))
                link(nc.vector.tensor_tensor(key[:, :, :], bits, sign[:, :, :], ALU.bitwise_xor))
                link(nc.vector.tensor_scalar(part[:, :, :], key[:, :, :], 16, None, ALU.logical_shift_right))
                link(nc.vector.tensor_copy(key_f[:, :, :], part[:, :, :]))
                link(nc.vector.tensor_scalar(part[:, :, :], key[:, :, :], 65535, None, ALU.bitwise_and))
                link(nc.vector.tensor_copy(low_f[:, :, :], part[:, :, :]))
                link(nc.vector.memset(found[:, :], 0.0))
                link(nc.vector.memset(zero[:, :], 0.0))

            def count(q):
                for b in range(B):
                    link(nc.vector.tensor_scalar(pivots[:, b, :], W3["digit"][:, :], float(16 ** (STEPS - 1 - q)),
                                                 found[:, b:b + 1], ALU.mult, ALU.add))
                shape = [P, B, PIV, ST]
                link(nc.vector.tensor_tensor(passed[:, :, :, :], key_f[:, :, :].unsqueeze(2).to_broadcast(shape),
                                             pivots[:, :, :].unsqueeze(3).to_broadcast(shape), ALU.is_ge))
                with nc.allow_low_precision("counts up to 32"):
                    nc.vector.tensor_reduce(counts[:, :], passed[:, :, :, :].rearrange("p b q t -> p (b q) t"), AX_X,
                                            ALU.add).then_inc(counted, 1)

            def advance(n, q):
                dve.wait_ge(summed, n + 1)
                for b in range(B):
                    link(nc.vector.tensor_scalar(reach[:, b, :], CB[:, b * PIV:(b + 1) * PIV], float(K), None, ALU.is_ge))
                link(nc.vector.tensor_reduce(digit[:, :], reach[:, :, :], AX_X, ALU.add))
                link(nc.vector.scalar_tensor_tensor(found[:, :], digit[:, :], float(16 ** (STEPS - 1 - q)), found[:, :],
                                                    ALU.mult, ALU.add))

            def compare(out, in0, op):
                for b in range(B):
                    link(nc.vector.tensor_scalar(out[:, b, :], in0[:, b, :], found[:, b:b + 1], None, op))

            def low_keys():
                compare(above, key_f, ALU.is_gt)
                compare(equal, key_f, ALU.is_equal)
                link(nc.vector.scalar_tensor_tensor(low_f[:, :, :], low_f[:, :, :], 1.0, equal[:, :, :], ALU.add, ALU.mult))
                link(nc.vector.scalar_tensor_tensor(key_f[:, :, :], above[:, :, :], 131072.0, low_f[:, :, :], ALU.mult, ALU.add))
                link(nc.vector.memset(found[:, :], 1.0))

            def tie_counts():
                compare(above, key_f, ALU.is_gt)
                compare(equal, key_f, ALU.is_equal)
                with nc.allow_low_precision("counts up to 32"):
                    link(nc.vector.tensor_reduce(above_n[:, :], above[:, :, :], AX_X, ALU.add))
                link(nc.vector.tensor_copy(equal_b[:, :, :], equal[:, :, :]))
                for b in range(B):
                    link(nc.vector.tensor_tensor_scan(pick[:, b, :], zero[:, :], equal[:, b, :], 0.0, ALU.add, ALU.add))
                nc.vector.tensor_tensor(earlier_b[:, :, :], pick[:, :, :], equal[:, :, :], ALU.subtract).then_inc(counted, 1)

            def choose():
                dve.wait_ge(summed, 2 * STEPS + 1)
                link(nc.vector.tensor_scalar(need[:, :], CB[:, 256:256 + B], -1.0, float(K), ALU.mult, ALU.add))
                for b in range(B):
                    link(nc.vector.tensor_scalar(pick[:, b, :], CB[:, b * ST:(b + 1) * ST], need[:, b:b + 1], None, ALU.is_lt))
                link(nc.vector.tensor_tensor(pick[:, :, :], pick[:, :, :], equal[:, :, :], ALU.mult))
                link(nc.vector.tensor_tensor(pick[:, :, :], pick[:, :, :], above[:, :, :], ALU.add))
                link(nc.vector.tensor_tensor(pick[:, :, :], pick[:, :, :], w_br[:, :, :], ALU.mult))

            def keep_y(u, h):
                for i in range(2):
                    dve.wait_ge(y_done, (u + 1) * FT)
                    nc.vector.tensor_tensor(y[:, bass.ds(u * TPC + 2 * i, 2), :], YB[h][i][:, :], W3["b2"][:, :, :],
                                            ALU.add).then_inc(y_kept, 1)

            def give(k, h):
                if not early(k, 2):
                    dve.wait_ge(st_out[h], (k - h) * 8)
                dve.wait_ge(y_kept, (k + 1) * 2)
                flat = pick[:, :, :].rearrange("p b t -> p (b t)")
                for j in range(TPC):
                    nc.vector.scalar_tensor_tensor(out_sb[:, h, j, :], y[:, k * TPC + j, :],
                                                   flat[:, bass.ds(k * TPC + j, 1)],
                                                   base[:, :, :, :].rearrange("p b t d -> p (b t) d")[:, k * TPC + j, :],
                                                   ALU.mult, ALU.add).then_inc(out_ok, 1)

            def step(u, h):
                for j in range(FT):
                    dve.wait_ge(ah_ok, u * FT + j + 1)
                    nc.vector.tensor_tensor(a_lo[:, j % 2, :], act32[:, j % 2, :], a_hi[:, j % 2, :].bitcast(F32),
                                            ALU.subtract).then_inc(al_ok, 1)
                    if j == 2 and not early(u, 1):
                        keep_y(u - 1, 1 - h)
                    if j == 4 and not last(u):
                        split(u + 1, 1 - h)
                    if j == 6 and not early(u, 2):
                        give(u - 2, h)
                    if early(u, 2):
                        if j % 2:
                            advance(u * STEPS + j // 2, j // 2)
                            if j == FT - 1:
                                low_keys() if u == 0 else tie_counts()
                        else:
                            count(j // 2)
                if isinstance(u, int) and u == 1:
                    choose()

            split(0, 0)
            make_keys()
            chunks(dve, step)
            keep_y(NU - 1, 1)
            give(NU - 2, 0)
            give(NU - 1, 1)

        @block.tensor
        def _(pe):
            def second(u, h, j):
                pe.wait_ge(al_ok, u * FT + j + 1)
                if j == 0 and not early(u, 2):
                    pe.wait_ge(y_kept, (u - 1) * 2)
                for t in range(TPC):
                    rows = slice(t * P, (t + 1) * P)
                    for n, (a, w) in enumerate(split_products(a_hi[:, j % 2, rows], a_lo[:, j % 2, rows],
                                                              W3["w2_hi"][:, j, :], W3["w2_lo"][:, j, :])):
                        mm = pe.matmul(YB[h][t // 2][:, (t % 2) * D:(t % 2 + 1) * D], a, w,
                                       start=j == 0 and t % 2 == 0 and n == 0, stop=j == FT - 1 and n == 2,
                                       skip_group_check=True)
                mm.then_inc(y_done, 1)

            def step(u, h):
                pe.wait_ge(lo_ok, u + 1)
                for j in range(FT):
                    if not (early(u, 1) and j < 2):
                        pe.wait_ge(gelu_ok, u * FT + j - 1)
                    cols = slice(j * P, (j + 1) * P)
                    n = 0
                    for k in range(KD):
                        for w, x in split_products(W3["w1_hi"][:, k, cols], W3["w1_lo"][:, k, cols],
                                                   x_hi[:, h, k, :], x_lo[:, h, k, :]):
                            n += 1
                            mm = pe.matmul(HB[j % 2][:, :], w, x, start=n == 1, stop=n == 3 * KD)
                    mm.then_inc(h1, 1)
                    if j >= LAG:
                        second(u, h, j - LAG)
                    elif not early(u, 1):
                        second(u - 1, 1 - h, FT - LAG + j)
                    if early(u, 2) and j % 2:
                        n = u * STEPS + j // 2
                        pe.wait_ge(counted, n + 1)
                        pe.matmul(CB[:, 0:B * PIV], W3["ones"][:, :], counts[:, :], start=True, stop=True).then_inc(summed, 1)
                if isinstance(u, int) and u == 1:
                    pe.wait_ge(counted, 2 * STEPS + 1)
                    flat = (equal_b[:, :, :].rearrange("p b t -> p (b t)"), earlier_b[:, :, :].rearrange("p b t -> p (b t)"))
                    pe.matmul(CB[:, 0:B * ST], W3["before"][:, :], flat[0], start=True, stop=False, skip_group_check=True)
                    pe.matmul(CB[:, 0:B * ST], W3["ones"][:, :], flat[1], start=False, stop=True, skip_group_check=True)
                    pe.matmul(CB[:, 256:256 + B], W3["ones"][:, :], above_n[:, :], start=False, stop=True,
                              skip_group_check=True).then_inc(summed, 1)

            chunks(pe, step)
            for j in range(FT - LAG, FT):
                second(NU - 1, 1, j)


def tokenizer_tables(pr, ctx):
    nc, KD, D = pr.nc, pr.KD, pr.D
    W = {n: sb(nc, ctx, n, [P, D]) for n in ("gamma", "beta")}
    W["prelu"] = sb(nc, ctx, "prelu", [P, 1])
    W["bo_col"], W["bk_col"] = sb(nc, ctx, "bo_col", [P, KD]), sb(nc, ctx, "bk_col", [P, KD])
    W["v_bias"] = sb(nc, ctx, "v_bias", [P, D + 2])
    W["a_hi"], W["a_lo"] = (sb(nc, ctx, n, [P, KD, D], F32R) for n in ("a_hi", "a_lo"))
    W["vo_hi"], W["vo_lo"] = (sb(nc, ctx, n, [P, KD, D + 2], F32R) for n in ("vo_hi", "vo_lo"))
    return W


def build(nc, ins, out, batches, tokens, width, heads, hidden):
    KD, NC = width // P, tokens // CH
    with ExitStack() as ctx:
        pr = Program(nc, ctx, ins, out, batches, tokens, width, heads, hidden)
        scratch = {n: nc.dram_tensor(f"scratch_{n}", (batches, NC, P) + s, F32, kind="Internal").ap() for n, s in (
            ("h", (TPC, width)), ("mn", (TPC, width)), ("mnT", (KD, CH)), ("xnT", (KD, CH)))}
        ident = sb(nc, ctx, "ident", [P, P])
        with ExitStack() as phase:
            W = tokenizer_tables(pr, phase)
            setup_weights(pr, W, ident)
            tokenizer(pr, W, ident, scratch)
        base = sb(nc, ctx, "base", [P, batches, pr.ST, width])
        router = sb(nc, ctx, "router", [P, batches, pr.ST])
        W2 = {"wr": sb(nc, ctx, "wr", [P, width]), "br": sb(nc, ctx, "br", [P, 1])}
        with ExitStack() as phase:
            grams = sb(nc, phase, "grams", [P, 4, 2 * width])
            gram(pr, scratch, grams)
            W2["bo4"], W2["bg_col"] = sb(nc, phase, "bo4", [P, TPC, width]), sb(nc, phase, "bg_col", [P, KD])
            W2["att"] = sb(nc, phase, "att_w", [P, 2, 2, KD])
            for x in "vgo":
                W2[x + "_hi"], W2[x + "_lo"] = (sb(nc, phase, f"w{x}{n}", [P, KD, width], F32R) for n in ("_hi", "_lo"))
            head_weights(pr, W2, grams)
            mix(pr, W2, ident, scratch, base, router)
        with ExitStack() as phase:
            W3 = {f"{w}_{n}": sb(nc, phase, f"{w}_{n}", s, F32R) for w, s in (
                ("w1", [P, KD, hidden]), ("w2", [P, hidden // P, width])) for n in ("hi", "lo")}
            W3["b1"], W3["b2"] = sb(nc, phase, "b1", [P, hidden // P]), sb(nc, phase, "b2", [P, 2, width])
            W3["ones"], W3["before"] = sb(nc, phase, "ones", [P, P], BF16), sb(nc, phase, "before", [P, P], BF16)
            W3["index"], W3["digit"] = sb(nc, phase, "index", [P, PIV], I32), sb(nc, phase, "digit", [P, PIV])
            split_mlp_weights(pr, W3)
            mlp(pr, W2, W3, scratch, base, router)


def _layouts(inputs):
    import numpy as np

    a = {k: np.asarray(v) for k, v in inputs.items()}
    x, dg = a["x"], a["L0_tok_d_gamma_batched"]
    B, _, T, D = x.shape
    out = {
        "xT": x.reshape(B, T // CH, CH, D // P, P).transpose(0, 1, 4, 3, 2),
        "gateT": dg.reshape(T // CH, CH, T // P // GT, GT, P).transpose(0, 2, 4, 3, 1),
    }
    for n in ("Wq", "Wk", "Wv"):
        out[f"tok_{n}T"] = a[f"L0_tok_{n}"].T
    for n in ("Wo", "bq", "bk", "bv", "bo"):
        out[f"tok_{n}"] = a[f"L0_tok_{n}"]
    out["tok_prelu_a"] = a["L0_tok_prelu_a"].reshape(1)
    for n in ("gamma", "beta", "Wq", "Wk", "Wv", "Wg", "bg", "Wo", "bo"):
        out[f"attn_{n}"] = a[f"L0_attn_{n}"]
    out["ffn_wr"] = a["L0_ffn_wr"].reshape(-1)
    for n in ("br", "w1", "b1", "w2", "b2"):
        out[f"ffn_{n}"] = a[f"L0_ffn_{n}"]
    return {k: np.ascontiguousarray(v) for k, v in out.items()}, (B, T, D, a["L0_ffn_w1"].shape[1])


def kernel(**inputs):
    import concourse.bacc as bacc
    from concourse.bass_utils import run_bass_kernel_spmd

    arrays, (B, T, D, F) = _layouts(inputs)
    nc = bacc.Bacc("TRN2", target_bir_lowering=False, num_devices=1, dynamic_dma_scratch_size=1024)
    ins = {n: nc.dram_tensor(f"in_{n}", a.shape, mybir.dt.from_np(a.dtype), kind="ExternalInput").ap()
           for n, a in arrays.items()}
    out = nc.dram_tensor("out_0", (B, T, D), F32, kind="ExternalOutput").ap()
    build(nc, ins, out, B, T, D, HEADS, F)
    r = run_bass_kernel_spmd(nc, [{f"in_{n}": a for n, a in arrays.items()}], core_ids=[0])
    return r.results[0]["out_0"]
```

```python
from contextlib import ExitStack

import concourse.bass as bass
from concourse import mybir

P = 128
CH = 512
TPC = CH // P
GT = 2
RG = 4
RP = 4
EPS = 1e-5
HEADS = 8

F32 = mybir.dt.float32
F32R = mybir.dt.float32r
BF16 = mybir.dt.bfloat16
I32 = mybir.dt.int32
ALU = mybir.AluOpType
ACT = mybir.ActivationFunctionType
AX_X = mybir.AxisListType.X


def split_products(hi_w, lo_w, hi_x, lo_x):
    return ((hi_w, hi_x), (hi_w, lo_x), (lo_w, hi_x))


class Program:

    def __init__(self, nc, ctx, ins, out, batches, tokens, width, heads, hidden):
        self.nc, self.ctx, self.ins, self.out = nc, ctx, ins, out
        self.B, self.T, self.D, self.H, self.F = batches, tokens, width, heads, hidden
        self.KD = width // P
        self.NC = tokens // CH
        self.ST = tokens // P
        self.NG = self.ST // GT
        self.used = {}

    def stand_alone(self, eng):
        eng.sem_inc(self.sem("went_on"), 1)

    def sem(self, name):
        if name not in self.used:
            self.used[name] = self.ctx.enter_context(self.nc.semaphore(name))
        return self.used[name]


def early(c, n):
    return isinstance(c, int) and c < n


def past(eng, sem, n):
    if not early(n, 1):
        eng.wait_ge(sem, n)


def sb(nc, ctx, name, shape, dt=F32):
    return ctx.enter_context(nc.sbuf_tensor(name, shape, dt))


def ps(nc, ctx, name, shape=(P, CH), dt=F32):
    return ctx.enter_context(nc.psum_tensor(name, list(shape), dt))


def setup_weights(pr, W, ident_r):
    nc, ins, KD, D = pr.nc, pr.ins, pr.KD, pr.D
    with ExitStack() as ctx:
        wqT, wkT, wvT, wo = (sb(nc, ctx, n, [P, KD, D]) for n in ("wqT", "wkT", "wvT", "wo"))
        bq2, bk2, bv2 = (sb(nc, ctx, n, [P, KD, 2]) for n in ("bq2", "bk2", "bv2"))
        ones, ident = sb(nc, ctx, "ones_setup", [P, P]), sb(nc, ctx, "ident", [P, P])
        bq_rows, bv_rows = (sb(nc, ctx, n, [P, KD, P]) for n in ("bq_rows", "bv_rows"))
        a_f, vo_f = sb(nc, ctx, "a_f", [P, KD, D]), sb(nc, ctx, "vo_f", [P, KD, D + 2])
        pa = [ps(nc, ctx, f"pa{j}") for j in range(KD)]
        pv = [ps(nc, ctx, f"pv{j}") for j in range(KD)]
        pb, pr_ = ps(nc, ctx, "pb"), ps(nc, ctx, "pr_")
        loaded, made, rows, prod, kept, hi_ok, lo_ok = (
            pr.sem(n) for n in ("w_loaded", "w_consts", "w_rows", "w_products", "w_kept", "w_hi", "w_lo"))
        n_loads = 4 + 3 * 2 + 1 + 4
        block = ctx.enter_context(nc.Block())

        @block.sync
        def _(sp):
            for t, name in ((wqT, "tok_WqT"), (wkT, "tok_WkT"), (wvT, "tok_WvT"), (wo, "tok_Wo")):
                sp.dma_start(t[:, :, :], ins[name].rearrange("(k p) n -> p k n", p=P)).then_inc(loaded, 16)
            with nc.allow_non_contiguous_dma(reason="bias columns, once"):
                for t, name in ((bq2, "tok_bq"), (bk2, "tok_bk"), (bv2, "tok_bv")):
                    for j in range(2):
                        sp.dma_start(t[:, :, j], ins[name].rearrange("(k p) -> p k", p=P)).then_inc(loaded, 16)
                sp.dma_start(W["bo_col"][:, :], ins["tok_bo"].rearrange("(k p) -> p k", p=P)).then_inc(loaded, 16)
            sp.dma_start(W["gamma"][:, :], ins["attn_gamma"].partition_broadcast(P)).then_inc(loaded, 16)
            sp.dma_start(W["beta"][:, :], ins["attn_beta"].partition_broadcast(P)).then_inc(loaded, 16)
            sp.dma_start(W["attn_bo"][:, :], ins["attn_bo"].partition_broadcast(P)).then_inc(loaded, 16)
            sp.dma_start(W["prelu"][:, :], ins["tok_prelu_a"].partition_broadcast(P)).then_inc(loaded, 16)

        @block.gpsimd
        def _(pool):
            nc.gpsimd.memset(ident[:, :], 0.0).then_inc(made, 1)
            nc.gpsimd.memset(ones[:, :], 1.0).then_inc(made, 1)
            pool.wait_ge(made, 2)
            nc.gpsimd.affine_select(out=ident[:, :], in_=ident[:, :], compare_op=ALU.not_equal, fill=1.0,
                                    base=0, pattern=[[-1, P]], channel_multiplier=1).then_inc(made, 1)

        @block.vector
        def _(dve):
            dve.wait_ge(loaded, 16 * n_loads)
            dve.wait_ge(made, 3)
            for k in range(KD):
                nc.vector.tensor_scalar(bq_rows[:, k, :], ones[:, :], bq2[:, k, 0:1], None,
                                        ALU.mult).then_inc(rows, 1)
                nc.vector.tensor_scalar(bv_rows[:, k, :], ones[:, :], bv2[:, k, 0:1], None,
                                        ALU.mult).then_inc(rows, 1)
            dve.wait_ge(prod, 1)
            for j in range(KD):
                nc.vector.tensor_copy(a_f[:, j, :], pa[j][:, 0:D]).then_inc(kept, 1)
                nc.vector.tensor_copy(vo_f[:, j, :], pv[j][:, 0:D + 2]).then_inc(kept, 1)
            nc.vector.tensor_copy(W["bk_col"][:, :], pb[:, 0:2 * KD:2]).then_inc(kept, 1)
            nc.vector.tensor_copy(W["v_bias"][:, :], pr_[:, 0:D + 2]).then_inc(kept, 1)
            dve.wait_ge(hi_ok, 2)
            nc.vector.tensor_tensor(W["a_lo"][:, :, :], a_f[:, :, :], W["a_hi"][:, :, :].bitcast(F32),
                                    ALU.subtract).then_inc(lo_ok, 1)
            nc.vector.tensor_tensor(W["vo_lo"][:, :, :], vo_f[:, :, :], W["vo_hi"][:, :, :].bitcast(F32),
                                    ALU.subtract).then_inc(lo_ok, 1)

        @block.scalar
        def _(act):
            act.wait_ge(made, 3)
            nc.scalar.activation(ident_r[:, :], ident[:, :], ACT.Copy).then_inc(made, 1)
            act.wait_ge(kept, 2 * KD)
            nc.scalar.activation(W["a_hi"][:, :, :], a_f[:, :, :], ACT.Copy).then_inc(hi_ok, 1)
            nc.scalar.activation(W["vo_hi"][:, :, :], vo_f[:, :, :], ACT.Copy).then_inc(hi_ok, 1)

        @block.tensor
        def _(pe):
            pe.wait_ge(rows, 2 * KD)
            for j in range(KD):
                cols = slice(j * P, (j + 1) * P)
                for k in range(KD):
                    pe.matmul(pa[j][:, 0:D], wkT[:, k, cols], wqT[:, k, :], start=k == 0, stop=k == KD - 1)
                for k in range(KD):
                    pe.matmul(pv[j][:, 0:D], wvT[:, k, cols], wo[:, k, :], start=k == 0, stop=k == KD - 1,
                              skip_group_check=True)
                for k in range(KD):
                    pe.matmul(pv[j][:, D:D + 2], wkT[:, k, cols], bq2[:, k, :], start=False,
                              stop=k == KD - 1, skip_group_check=True)
                for k in range(KD):
                    pe.matmul(pb[:, 2 * j:2 * j + 2], wqT[:, k, cols], bk2[:, k, :], start=j == 0 and k == 0,
                              stop=k == KD - 1, skip_group_check=True)
            for k in range(KD):
                pe.matmul(pr_[:, 0:D], bv_rows[:, k, :], wo[:, k, :], start=k == 0, stop=k == KD - 1,
                          skip_group_check=True)
            for k in range(KD):
                last = pe.matmul(pr_[:, D:D + 2], bq_rows[:, k, :], bk2[:, k, :], start=False,
                                 stop=k == KD - 1, skip_group_check=True)
            last.then_inc(prod, 1)


def gram_view(work, D):
    return work[:, 0:4 * 2 * D].rearrange("p (i n) -> p i n", i=4)


def tokenizer(pr, W, ident_r, scratch, work):
    nc, ins, D, KD, NC, ST, NG = pr.nc, pr.ins, pr.D, pr.KD, pr.NC, pr.ST, pr.NG
    assert KD == 2 and NG % RG == 0 and NC % 2 == 0 and pr.B == 2 and RG * GT * CH == 2 * 2 * TPC * D
    PAIRS = NC // 2
    TURN_Y, RECTIFY, MOMENTS, NORM, SPLIT_X = 4, 5, 7, 10, 12
    MN_HI, MN_LO, TURN_MN, KEEP_MN = (max(n, ST * m // 16) for n, m in ((13, 7), (14, 8), (15, 10), (15, 12)))

    with ExitStack() as ctx:
        kt_hi, kt_lo = (sb(nc, ctx, n, [P, KD, pr.T], F32R) for n in ("kt_hi", "kt_lo"))
        v_hi, v_lo = (sb(nc, ctx, n, [P, ST, D], F32R) for n in ("v_hi", "v_lo"))
        d_col = sb(nc, ctx, "d_col", [P, ST])
        gate = sb(nc, ctx, "gate", [P, RG, GT, CH])
        p32 = work[:, 0:RP * CH].rearrange("p (i t) -> p i t", i=RP)
        h_sb = work[:, RP * CH:RP * CH + TPC * D].rearrange("p (j d) -> p j d", j=TPC)
        x32 = work[:, RP * CH + TPC * D:RP * CH + 2 * TPC * D].rearrange("p (k t) -> p k t", k=KD)
        grams = gram_view(work, D)
        p_hi, p_lo = (sb(nc, ctx, n, [P, 2, CH], F32R) for n in ("p_hi", "p_lo"))
        x_hi, x_lo = (sb(nc, ctx, n, [P, 2, KD, CH], F32R) for n in ("x_hi", "x_lo"))
        vf = sb(nc, ctx, "vf", [P, TPC, D + 2])
        turn_hi, turn_lo = (sb(nc, ctx, n, [P, TPC * D], F32R) for n in ("turn_hi", "turn_lo"))
        mn_sb = sb(nc, ctx, "mn_sb", [P, TPC, D])
        mnT_sb = sb(nc, ctx, "mnT_sb", [P, KD, CH])
        stats, mv = sb(nc, ctx, "stats", [P, TPC, 6]), sb(nc, ctx, "mv", [P, TPC, 2])
        spread, rstd, power = (sb(nc, ctx, n, [P, TPC]) for n in ("spread", "rstd", "power"))
        yT_hi, yT_lo = (t[:, :].rearrange("p (m t) -> p m t", m=KD) for t in (turn_hi, turn_lo))
        mn_hi, mn_lo = (t[:, :].rearrange("p (j d) -> p j d", j=TPC) for t in (turn_hi, turn_lo))
        g32 = gate[:, :, :, :].rearrange("p (h b) g t -> p h b (g t)", h=2)
        g_hi, g_lo = (t[:, :, :].rearrange("p k t -> p (k t)")[:, 0:4 * TPC * D].rearrange(
            "p (h b n) -> p h b n", h=2, b=2) for t in (kt_hi, kt_lo))
        S = [ps(nc, ctx, f"S{i}") for i in range(2)]
        Y = [ps(nc, ctx, f"Y{i}") for i in range(2)]
        TR = [ps(nc, ctx, f"TR{i}") for i in range(4)]
        KP, VP, G = S, [Y[0], Y[1], TR[0], TR[1]], [S[0], S[1], Y[0], Y[1]]

        (xp_ld, xp_hi, xp_lo, kp, k_evac, k_hi_ok, k_lo_ok, vp, v_evac, v_hi_ok, v_lo_ok, d_ok,
         xm_ld, xm_hi, xm_lo, scores, mul_done, hi_done, lo_done, ret_done, y_hi_ok, y_evac,
         y_turned, neg_ok, h_ok, stats_ok, mv_ok, spread_ok, rstd_ok, z_ok, scaled, mn_ok, hb_ok,
         mn_hi_ok, mn_lo_ok, mn_turned, mnT_ok, st_h, st_mn, st_mnT, power_ok, g_hi_ok, g_lo_ok,
         g_done, g_kept) = (pr.sem(n) for n in (
            "xp_ld", "xp_hi", "xp_lo", "kp", "k_evac", "k_hi_ok", "k_lo_ok", "vp", "v_evac", "v_hi_ok",
            "v_lo_ok", "d_ok", "xm_ld", "xm_hi", "xm_lo", "scores", "mul_done", "hi_done", "lo_done",
            "ret_done", "y_hi_ok", "y_evac", "y_turned", "neg_ok", "h_ok", "stats_ok", "mv_ok", "spread_ok",
            "rstd_ok", "z_ok", "scaled", "mn_ok", "hb_ok", "mn_hi_ok", "mn_lo_ok", "mn_turned", "mnT_ok",
            "st_h", "st_mn", "st_mnT", "power_ok", "g_hi_ok", "g_lo_ok", "g_done", "g_kept"))
        gate_ld = [pr.sem(f"gate_ld{r}") for r in range(RG)]
        block = ctx.enter_context(nc.Block())
        END = pr.B * NC

        def chunks(eng, b, step):
            for c in range(2):
                step(c, b * NC + c, c)
            if PAIRS > 2:
                with eng.Fori(1, PAIRS - 1) as p:
                    for h in range(2):
                        step(p * 2 + h, b * NC + p * 2 + h, h)
            for c in range(NC - 2, NC):
                step(c, b * NC + c, c % 2)

        def gram_chunks(eng, step):
            for c in range(2):
                step(c, c)
            if PAIRS > 2:
                with eng.Fori(1, PAIRS - 1) as p:
                    for h in range(2):
                        step(p * 2 + h, h)
            for c in range(NC - 2, NC):
                step(c, c % 2)

        def is_last(c):
            return isinstance(c, int) and c == NC - 1

        def before(b, c):
            return (b - 1, NC - 1) if early(c, 1) else (b, c - 1)

        @block.sync
        def _(sp):
            def load_x(b, c, sem):
                sp.dma_start(x32[:, :, :], ins["xT"][b, c]).then_inc(sem, 16)

            def store(Q, b, c, sem, ready, count, tile, dram):
                sp.wait_ge(ready, (Q + 1) * count)
                sp.dma_start(dram[b, c], tile).then_inc(sem, 16)

            stores = ((max(NG // 2, 6), st_h, hb_ok, TPC, h_sb[:, :, :], scratch["h"]),
                      (max(NG * 5 // 8, 6), st_mn, mn_ok, TPC, mn_sb[:, :, :], scratch["mn"]),
                      (NG - 1, st_mnT, mnT_ok, 2, mnT_sb[:, :, :], scratch["mnT"]))

            def load_gate(c, M, g):
                past(sp, mul_done, M * ST + (g - RG + 1) * GT)
                sp.dma_start(gate[:, g % RG, :, :], ins["gateT"][c, g]).then_inc(gate_ld[g % RG], 16)

            load_x(0, 0, xp_ld)
            for b in range(pr.B):
                def project(c, J, h):
                    sp.wait_ge(xp_lo, J + 1)
                    if is_last(c):
                        load_x(b, 0, xm_ld)
                    else:
                        load_x(b, c + 1, xp_ld)
                    if early(c, 1):
                        for g in range(RG):
                            load_gate(0, b * NC, g)

                chunks(sp, b, project)

                def attend(c, M, h):
                    if not (is_last(c) and b == pr.B - 1):
                        sp.wait_ge(xm_lo, M + 1)
                        if is_last(c):
                            load_x(b + 1, 0, xp_ld)
                        else:
                            load_x(b, c + 1, xm_ld)
                    for g in range(NG):
                        if not (early(c, 1) and g < RG):
                            load_gate(c, M, g)
                        if not early(M, 1):
                            for at, *what in stores:
                                if g == at:
                                    store(M - 1, *before(b, c), *what)

                chunks(sp, b, attend)

            def load_mn(c, h, last):
                if last:
                    for _, *what in stores[0:2]:
                        store(END - 1, pr.B - 1, NC - 1, *what)
                    sp.wait_ge(st_mn, 16 * END)
                past(sp, g_lo_ok, c - 1)
                for s in range(2):
                    sp.dma_start(gate[:, 2 * h + s, :, :], scratch["mn"][s, c].rearrange("p j d -> p (j d)")).then_inc(
                        gate_ld[2 * h + s], 16)

            sp.wait_ge(mul_done, END * ST)
            sp.wait_ge(st_mn, 16 * (END - 1))
            gram_chunks(sp, lambda c, h: load_mn(c, h, is_last(c)))
            store(END - 1, pr.B - 1, NC - 1, *stores[2][1:])
            for sem in (st_h, st_mn, st_mnT):
                sp.wait_ge(sem, 16 * END)

        @block.scalar
        def _(act):
            def split_x(half, sem_ld, sem_hi, J):
                act.wait_ge(sem_ld, (J + 1) * 16)
                nc.scalar.activation(x_hi[:, half], x32[:, :, :], ACT.Copy).then_inc(sem_hi, 1)

            def keep_y(Q):
                act.wait_ge(ret_done, (Q + 1) * ST)
                for m in range(KD):
                    nc.scalar.activation(yT_hi[:, m, :], Y[m][:, :], ACT.Identity,
                                         bias=W["bo_col"][:, m:m + 1]).then_inc(y_hi_ok, 1)

            def split_mn(Q):
                act.wait_ge(mn_ok, (Q + 1) * TPC)
                act.wait_ge(y_turned, Q + 1)
                nc.scalar.activation(mn_hi, mn_sb[:, :, :], ACT.Copy).then_inc(mn_hi_ok, 1)

            def keep_mnT(Q):
                past(act, st_mnT, Q * 16)
                act.wait_ge(mn_turned, Q + 1)
                for m in range(KD):
                    nc.scalar.activation(mnT_sb[:, m, :], TR[2 + m][:, :], ACT.Copy).then_inc(mnT_ok, 1)

            split_x(0, xp_ld, xp_hi, 0)
            for b in range(pr.B):
                def project(c, J, h):
                    if is_last(c):
                        split_x(1 - h, xm_ld, xm_hi, b * NC)
                    else:
                        split_x(1 - h, xp_ld, xp_hi, J + 1)
                    for m in range(KD):
                        past(act, k_lo_ok, J * 2 + m - 3)
                        act.wait_ge(kp, J * 2 + m + 1)
                        nc.scalar.activation(p32[:, 2 * h + m, :], KP[m][:, :], ACT.Identity,
                                             bias=W["bk_col"][:, m:m + 1]).then_inc(k_evac, 1)
                    for m in range(KD):
                        act.wait_ge(k_evac, J * 2 + m + 1)
                        nc.scalar.activation(kt_hi[:, m, bass.ds(c * CH, CH)], p32[:, 2 * h + m, :],
                                             ACT.Copy).then_inc(k_hi_ok, 1)
                    for j in range(TPC):
                        act.wait_ge(v_evac, J * TPC + j + 1)
                        nc.scalar.activation(v_hi[:, c * TPC + j, :], vf[:, j, 0:D], ACT.Copy).then_inc(v_hi_ok, 1)

                chunks(act, b, project)

                def attend(c, M, h):
                    for i in range(ST):
                        if i == 1 and not early(c, 1):
                            keep_y(M - 1)
                        act.wait_ge(mul_done, M * ST + i + 1)
                        past(act, ret_done, M * ST + i - 1)
                        nc.scalar.activation(p_hi[:, i % 2, :], p32[:, i % RP, :], ACT.Copy).then_inc(hi_done, 1)
                        if i == SPLIT_X and not is_last(c):
                            split_x(1 - h, xm_ld, xm_hi, M + 1)
                        if not early(M, 1):
                            if i == MN_HI:
                                split_mn(M - 1)
                            if i == KEEP_MN:
                                keep_mnT(M - 1)
                    if is_last(c):
                        if b < pr.B - 1:
                            split_x(0, xp_ld, xp_hi, (b + 1) * NC)
                        keep_y(M)

                chunks(act, b, attend)

            def gram(c, h):
                act.wait_ge(gate_ld[2 * h], END * (NG // RG) * 16 + (c - h) * 8 + 16)
                act.wait_ge(gate_ld[2 * h + 1], END * (NG // RG) * 16 + (c - h) * 8 + 16)
                past(act, g_done, c - 1)
                nc.scalar.activation(g_hi[:, h], g32[:, h], ACT.Copy).then_inc(g_hi_ok, 1)
                if early(c, 2) and h == 1:
                    split_mn(END - 1)
                if isinstance(c, int) and c == NC - 2:
                    keep_mnT(END - 1)

            gram_chunks(act, gram)

        @block.vector
        def _(dve):
            def split_x(half, sem_hi, sem_lo, J):
                dve.wait_ge(sem_hi, J + 1)
                nc.vector.tensor_tensor(x_lo[:, half], x32[:, :, :], x_hi[:, half].bitcast(F32),
                                        ALU.subtract).then_inc(sem_lo, 1)

            def keep_y(Q):
                for m in range(KD):
                    dve.wait_ge(y_hi_ok, Q * 2 + m + 1)
                    nc.vector.scalar_tensor_tensor(yT_lo[:, m, :], Y[m][:, :], W["bo_col"][:, m:m + 1],
                                                   yT_hi[:, m, :].bitcast(F32), ALU.add, ALU.subtract).then_inc(y_evac, 1)

            def rectify(Q, part):
                for i in range(2):
                    if part == 0:
                        dve.wait_ge(y_turned, Q + 1)
                        past(dve, st_h, Q * 16)
                        past(dve, st_mn, Q * 16)
                        nc.vector.tensor_scalar(mn_sb[:, 2 * i:2 * i + 2, :], TR[i][:, :], 0.0, W["prelu"][:, 0:1],
                                                ALU.min, ALU.mult).then_inc(neg_ok, 1)
                    else:
                        dve.wait_ge(neg_ok, Q * 2 + i + 1)
                        nc.vector.scalar_tensor_tensor(h_sb[:, 2 * i:2 * i + 2, :], TR[i][:, :], 0.0,
                                                       mn_sb[:, 2 * i:2 * i + 2, :], ALU.max, ALU.add).then_inc(h_ok, 1)

            def moments(Q, part):
                for j in (2 * part, 2 * part + 1):
                    dve.wait_ge(h_ok, Q * 2 + part + 1)
                    nc.vector.bn_stats(stats[:, j, :], h_sb[:, j, :]).then_inc(stats_ok, 1)
                for j in (2 * part, 2 * part + 1):
                    dve.wait_ge(stats_ok, Q * TPC + j + 1)
                    pr.stand_alone(dve)
                    nc.vector.bn_aggr(mv[:, j, :], stats[:, j, :]).then_inc(mv_ok, 1)

            def norm(Q, part):
                dve.wait_ge(rstd_ok, Q + 1)
                for j in (2 * part, 2 * part + 1):
                    nc.vector.tensor_scalar(mn_sb[:, j, :], h_sb[:, j, :], mv[:, j, 0:1], rstd[:, j:j + 1],
                                            ALU.subtract, ALU.mult).then_inc(z_ok, 1)

            def split_mn(Q):
                dve.wait_ge(mn_hi_ok, Q + 1)
                nc.vector.tensor_tensor(mn_lo, mn_sb[:, :, :], mn_hi.bitcast(F32), ALU.subtract).then_inc(mn_lo_ok, 1)

            split_x(0, xp_hi, xp_lo, 0)
            for b in range(pr.B):
                def project(c, J, h):
                    if is_last(c):
                        split_x(1 - h, xm_hi, xm_lo, b * NC)
                    else:
                        split_x(1 - h, xp_hi, xp_lo, J + 1)
                    for m in range(KD):
                        dve.wait_ge(k_hi_ok, J * 2 + m + 1)
                        nc.vector.tensor_tensor(kt_lo[:, m, bass.ds(c * CH, CH)], p32[:, 2 * h + m, :],
                                                kt_hi[:, m, bass.ds(c * CH, CH)].bitcast(F32),
                                                ALU.subtract).then_inc(k_lo_ok, 1)
                    for j in range(TPC):
                        past(dve, v_lo_ok, J * TPC + j - 3)
                        dve.wait_ge(vp, J * TPC + j + 1)
                        nc.vector.tensor_tensor(vf[:, j, :], VP[j][:, 0:D + 2], W["v_bias"][:, :],
                                                ALU.add).then_inc(v_evac, 1)

                chunks(dve, b, project)
                dve.wait_ge(d_ok, (b + 1) * NC * TPC)
                dve.wait_ge(k_lo_ok, (b + 1) * NC * KD)
                pr.stand_alone(dve)

                def attend(c, M, h):
                    def low(i):
                        dve.wait_ge(hi_done, M * ST + i + 1)
                        nc.vector.tensor_tensor(p_lo[:, i % 2, :], p32[:, i % RP, :], p_hi[:, i % 2, :].bitcast(F32),
                                                ALU.subtract).then_inc(lo_done, 1)

                    for i in range(ST):
                        g, j = i // GT, i % GT
                        dve.wait_ge(scores, M * ST + i + 1)
                        if j == 0:
                            dve.wait_ge(gate_ld[g % RG], (M * (NG // RG) + g // RG + 1) * 16)
                        past(dve, lo_done, M * ST + i - RP + 1)
                        nc.vector.scalar_tensor_tensor(p32[:, i % RP, :], S[i % 2][:, :], d_col[:, i:i + 1],
                                                       gate[:, g % RG, j, :], ALU.add, ALU.mult).then_inc(mul_done, 1)
                        if i == 0 and not early(c, 1):
                            low(0)
                            keep_y(M - 1)
                        elif i > 1 or i == 1 and early(c, 1):
                            low(i - 1)
                        if i == SPLIT_X and not is_last(c):
                            split_x(1 - h, xm_hi, xm_lo, M + 1)
                        if not early(M, 1):
                            for at, what in ((RECTIFY, rectify), (MOMENTS, moments), (NORM, norm)):
                                if i in (at, at + 1):
                                    what(M - 1, i - at)
                            if i == MN_LO:
                                split_mn(M - 1)
                    low(ST - 1)
                    if is_last(c):
                        if b < pr.B - 1:
                            split_x(0, xp_hi, xp_lo, (b + 1) * NC)
                        keep_y(M)

                chunks(dve, b, attend)

            def gram(c, h):
                dve.wait_ge(g_hi_ok, c + 1)
                nc.vector.tensor_tensor(g_lo[:, h], g32[:, h], g_hi[:, h].bitcast(F32), ALU.subtract).then_inc(g_lo_ok, 1)
                if early(c, 1):
                    for what in (rectify, moments):
                        for part in range(2):
                            what(END - 1, part)
                elif early(c, 2):
                    for part in range(2):
                        norm(END - 1, part)
                    split_mn(END - 1)

            gram_chunks(dve, gram)
            dve.wait_ge(g_done, NC)
            for i in range(4):
                n = 2 * D if i < 2 else D
                nc.vector.tensor_copy(grams[:, i, 0:n], G[i][:, 0:n]).then_inc(g_kept, 1)
            dve.wait_ge(g_kept, 4)

        @block.gpsimd
        def _(pool):
            nc.gpsimd.memset(power[:, :], -0.5).then_inc(power_ok, 1)

            def scale(Q):
                pool.wait_ge(mv_ok, (Q + 1) * TPC)
                pr.stand_alone(pool)
                nc.gpsimd.tensor_scalar(spread[:, :], mv[:, :, 1], 1.0 + EPS, EPS * EPS, ALU.mult,
                                        ALU.add).then_inc(spread_ok, 1)
                pool.wait_ge(spread_ok, Q + 1)
                pool.wait_ge(power_ok, 1)
                nc.gpsimd.tensor_tensor(rstd[:, :], spread[:, :], power[:, :], ALU.pow).then_inc(rstd_ok, 1)
                pool.wait_ge(z_ok, (Q + 1) * TPC)
                for j in range(TPC):
                    nc.gpsimd.tensor_tensor(mn_sb[:, j, :], mn_sb[:, j, :], W["gamma"][:, :],
                                            ALU.mult).then_inc(scaled, 1)
                for j in range(TPC):
                    pool.wait_ge(scaled, Q * TPC + j + 1)
                    nc.gpsimd.tensor_tensor(mn_sb[:, j, :], mn_sb[:, j, :], W["beta"][:, :], ALU.add).then_inc(mn_ok, 1)
                for j in range(TPC):
                    nc.gpsimd.tensor_tensor(h_sb[:, j, :], h_sb[:, j, :], W["attn_bo"][:, :], ALU.add).then_inc(hb_ok, 1)

            for b in range(pr.B):
                def project(c, J, h):
                    for j in range(TPC):
                        pool.wait_ge(v_evac, J * TPC + j + 1)
                        pr.stand_alone(pool)
                        nc.gpsimd.tensor_copy(d_col[:, bass.ds(c * TPC + j, 1)], vf[:, j, D:D + 1]).then_inc(d_ok, 1)
                        pool.wait_ge(v_hi_ok, J * TPC + j + 1)
                        nc.gpsimd.tensor_tensor(v_lo[:, c * TPC + j, :], vf[:, j, 0:D],
                                                v_hi[:, c * TPC + j, :].bitcast(F32), ALU.subtract).then_inc(v_lo_ok, 1)

                chunks(pool, b, project)

                def attend(c, M, h):
                    if not early(M, 1):
                        scale(M - 1)

                chunks(pool, b, attend)
            scale(END - 1)

        @block.tensor
        def _(pe):
            def turn(out, hi, lo):
                pe.matmul(out, hi, ident_r[:, :], start=True, stop=False)
                return pe.matmul(out, lo, ident_r[:, :], start=False, stop=True)

            def turn_y(Q):
                pe.wait_ge(y_evac, (Q + 1) * 2)
                for j in range(TPC):
                    for m in range(KD):
                        t = slice(j * P, (j + 1) * P)
                        last = turn(TR[j // 2][:, (j % 2) * D + m * P:(j % 2) * D + (m + 1) * P],
                                    yT_hi[:, m, t], yT_lo[:, m, t])
                last.then_inc(y_turned, 1)

            def turn_mn(Q):
                past(pe, mnT_ok, Q * 2)
                pe.wait_ge(mn_lo_ok, Q + 1)
                for m in range(KD):
                    for j in range(TPC):
                        d = slice(m * P, (m + 1) * P)
                        last = turn(TR[2 + m][:, j * P:(j + 1) * P], mn_hi[:, j, d], mn_lo[:, j, d])
                last.then_inc(mn_turned, 1)

            for b in range(pr.B):
                def project(c, J, h):
                    pe.wait_ge(xp_lo, J + 1)
                    for m in range(KD):
                        past(pe, k_evac, J * 2 + m - 1)
                        cols = slice(m * P, (m + 1) * P)
                        n = 0
                        for k in range(KD):
                            for w, x in split_products(W["a_hi"][:, k, cols], W["a_lo"][:, k, cols],
                                                       x_hi[:, h, k, :], x_lo[:, h, k, :]):
                                n += 1
                                mm = pe.matmul(KP[m][:, :], w, x, start=n == 1, stop=n == 3 * KD)
                        mm.then_inc(kp, 1)
                    if early(c, 1):
                        past(pe, y_evac, b * NC * 2)
                    for j in range(TPC):
                        past(pe, v_evac, J * TPC + j - 3)
                        rows = slice(j * P, (j + 1) * P)
                        n = 0
                        for k in range(KD):
                            for x, w in split_products(x_hi[:, h, k, rows], x_lo[:, h, k, rows],
                                                       W["vo_hi"][:, k, :], W["vo_lo"][:, k, :]):
                                n += 1
                                mm = pe.matmul(VP[j][:, 0:D + 2], x, w, start=n == 1, stop=n == 3 * KD)
                        mm.then_inc(vp, 1)

                chunks(pe, b, project)
                pe.wait_ge(k_lo_ok, (b + 1) * NC * 2)
                pe.wait_ge(v_evac, (b + 1) * NC * TPC)

                def retain(M, i):
                    if i == 0:
                        past(pe, y_evac, M * 2)
                    pe.wait_ge(lo_done, M * ST + i + 1)
                    for m in range(KD):
                        cols = slice(m * P, (m + 1) * P)
                        for n, (v, p) in enumerate(split_products(v_hi[:, i, cols], v_lo[:, i, cols],
                                                                  p_hi[:, i % 2, :], p_lo[:, i % 2, :])):
                            mm = pe.matmul(Y[m][:, :], v, p, start=i == 0 and n == 0, stop=i == ST - 1 and n == 2)
                    mm.then_inc(ret_done, 1)

                def attend(c, M, h):
                    pe.wait_ge(xm_lo, M + 1)
                    for i in range(ST):
                        past(pe, mul_done, M * ST + i - 1)
                        rows = slice(i * P, (i + 1) * P)
                        n = 0
                        for k in range(KD):
                            for w, x in split_products(kt_hi[:, k, rows], kt_lo[:, k, rows],
                                                       x_hi[:, h, k, :], x_lo[:, h, k, :]):
                                n += 1
                                mm = pe.matmul(S[i % 2][:, :], w, x, start=n == 1, stop=n == 3 * KD)
                        mm.then_inc(scores, 1)
                        if early(c, 1) and i == 2:
                            pe.wait_ge(v_lo_ok, (b + 1) * NC * TPC)
                        if i >= 2:
                            retain(M, i - 2)
                        elif i == 0 and not early(c, 1):
                            for back in (2, 1):
                                retain(M - 1, ST - back)
                        if not early(M, 1):
                            if i == TURN_Y:
                                turn_y(M - 1)
                            if i == TURN_MN:
                                turn_mn(M - 1)
                    if is_last(c):
                        for back in (2, 1):
                            retain(M, ST - back)

                chunks(pe, b, attend)

            def gram(c, h):
                if isinstance(c, int) and c == NC - 2:
                    turn_mn(END - 1)
                if early(c, 1):
                    turn_y(END - 1)
                pe.wait_ge(g_lo_ok, c + 1)
                for j in range(TPC):
                    for i in range(4):
                        s, m = i // 2, i % 2
                        cols = slice(j * D + m * P, j * D + (m + 1) * P)
                        tile = slice(j * D, (j + 1) * D)
                        out = G[i][:, 0:2 * D] if s == 0 else G[i][:, 0:D]
                        for n, (w, x) in enumerate(split_products(
                                g_hi[:, h, s, cols], g_lo[:, h, s, cols],
                                g_hi[:, h, s:2, tile], g_lo[:, h, s:2, tile])):
                            mm = pe.matmul(out, w, x, start=early(c, 1) and j == 0 and n == 0,
                                           stop=False, skip_group_check=True)
                mm.then_inc(g_done, 1)

            gram_chunks(pe, gram)


def head_weights(pr, W2, grams):
    nc, ins, D, KD, B = pr.nc, pr.ins, pr.D, pr.KD, pr.B
    head = D // pr.H
    scale = head ** -0.5 * pr.T ** -0.5
    with ExitStack() as ctx:
        wq, wk = sb(nc, ctx, "wq", [P, KD, D]), sb(nc, ctx, "wk", [P, KD, D])
        wsrc = {n: sb(nc, ctx, f"src_{n}", [P, KD, D]) for n in ("v", "g", "o")}
        prod = sb(nc, ctx, "prod", [P, 4, KD, D])
        same_head = sb(nc, ctx, "same_head", [P, P])
        ones = sb(nc, ctx, "ones_att", [P, 2])
        cols, att = sb(nc, ctx, "cols", [P, 16]), sb(nc, ctx, "att", [P, 2, 2, 2])
        top, shifted, expd, total, inv = (sb(nc, ctx, n, sh) for n, sh in (
            ("top", [P, 2, 2]), ("shifted", [P, 2, 2, 2]), ("expd", [P, 2, 2, 2]), ("total", [P, 2, 2]), ("inv", [P, 2, 2])))
        TP = [ps(nc, ctx, f"TP{i}", (P, KD, D)) for i in range(4)]
        colp, attp = ps(nc, ctx, "colp"), ps(nc, ctx, "attp")
        ld, made, tp, prod_ok, col_ok, cols_sb, att_ok, step, exp_ok, whi = (pr.sem(n) for n in (
            "hw_ld", "hw_made", "hw_tp", "hw_prod", "hw_col", "hw_cols", "hw_att", "hw_step", "hw_exp", "hw_hi"))
        block = ctx.enter_context(nc.Block())
        n_ld = 5 + 1 + 2

        @block.sync
        def _(sp):
            for t, n in ((wq, "attn_Wq"), (wk, "attn_Wk"), (wsrc["v"], "attn_Wv"), (wsrc["g"], "attn_Wg"), (wsrc["o"], "attn_Wo")):
                sp.dma_start(t[:, :, :], ins[n].rearrange("(k p) n -> p k n", p=P)).then_inc(ld, 16)
            with nc.allow_non_contiguous_dma(reason="a bias column, once"):
                sp.dma_start(W2["bg_col"][:, :], ins["attn_bg"].rearrange("(k p) -> p k", p=P)).then_inc(ld, 16)
            sp.dma_start(W2["wr"][:, :], ins["ffn_wr"].partition_broadcast(P)).then_inc(ld, 16)
            sp.dma_start(W2["br"][:, :], ins["ffn_br"].partition_broadcast(P)).then_inc(ld, 16)

        @block.gpsimd
        def _(pool):
            nc.gpsimd.memset(same_head[:, :], 0.0).then_inc(made, 1)
            nc.gpsimd.memset(ones[:, :], 1.0).then_inc(made, 1)
            pool.wait_ge(made, 2)
            for h in range(P // head):
                r = slice(h * head, (h + 1) * head)
                nc.gpsimd.memset(same_head[r, r], 1.0).then_inc(made, 1)

        @block.tensor
        def _(pe):
            pe.wait_ge(ld, 16 * n_ld)
            for i, (g0, c0, w) in enumerate(((0, 0, wk), (0, D, wq), (0, D, wk), (2, 0, wk))):
                for m in range(KD):
                    for k in range(KD):
                        mm = pe.matmul(TP[i][:, m, :], grams[:, g0 + k, c0 + m * P:c0 + (m + 1) * P], w[:, k, :],
                                       start=m == 0 and k == 0, stop=k == KD - 1, skip_group_check=True)
                mm.then_inc(tp, 1)
            pe.wait_ge(made, 2 + P // head)
            for i in range(4):
                pe.wait_ge(prod_ok, i + 1)
                for j in range(KD):
                    for m in range(KD):
                        mm = pe.matmul(colp[:, 4 * i + 2 * j:4 * i + 2 * j + 2], prod[:, i, m, j * P:(j + 1) * P], ones[:, :],
                                       start=i == 0 and j == 0 and m == 0, stop=m == KD - 1, skip_group_check=True)
            mm.then_inc(col_ok, 1)
            pe.wait_ge(cols_sb, 1)
            pe.matmul(attp[:, 0:16], same_head[:, :], cols[:, :], start=True, stop=True).then_inc(att_ok, 1)

        @block.vector
        def _(dve):
            dve.wait_ge(ld, 16 * n_ld)
            for i, w in enumerate((wq, wk, wq, wq)):
                dve.wait_ge(tp, i + 1)
                nc.vector.tensor_tensor(prod[:, i], TP[i][:, :, :], w[:, :, :], ALU.mult).then_inc(prod_ok, 1)
            for n, x in enumerate("vgo"):
                dve.wait_ge(whi, n + 1)
                nc.vector.tensor_tensor(W2[x + "_lo"][:, :, :], wsrc[x][:, :, :], W2[x + "_hi"][:, :, :].bitcast(F32),
                                        ALU.subtract).then_inc(prod_ok, 1)
            dve.wait_ge(col_ok, 1)
            nc.vector.tensor_copy(cols[:, :], colp[:, 0:16]).then_inc(cols_sb, 1)
            dve.wait_ge(att_ok, 1)
            nc.vector.tensor_copy(att[:, :, :, :], attp[:, 0:16:2].rearrange("p (s t j) -> p s t j", s=2, t=2)).then_inc(step, 1)
            dve.wait_ge(step, 1)
            nc.vector.tensor_tensor(top[:, :, :], att[:, :, 0, :], att[:, :, 1, :], ALU.max).then_inc(step, 1)
            dve.wait_ge(step, 2)
            for t in range(2):
                nc.vector.tensor_tensor(shifted[:, :, t, :], att[:, :, t, :], top[:, :, :], ALU.subtract).then_inc(step, 1)
            dve.wait_ge(exp_ok, 1)
            nc.vector.tensor_tensor(total[:, :, :], expd[:, :, 0, :], expd[:, :, 1, :], ALU.add).then_inc(step, 1)
            dve.wait_ge(step, 5)
            nc.vector.reciprocal(inv[:, :, :], total[:, :, :]).then_inc(step, 1)
            dve.wait_ge(step, 6)
            for t in range(2):
                nc.vector.tensor_tensor(W2["att"][:, :, t, :], expd[:, :, t, :], inv[:, :, :], ALU.mult).then_inc(step, 1)
            dve.wait_ge(step, 8)

        @block.scalar
        def _(act):
            act.wait_ge(ld, 16 * n_ld)
            for x in "vgo":
                nc.scalar.activation(W2[x + "_hi"][:, :, :], wsrc[x][:, :, :], ACT.Copy).then_inc(whi, 1)
            act.wait_ge(step, 4)
            nc.scalar.activation(expd[:, :, :, :], shifted[:, :, :, :], ACT.Exp, scale=scale).then_inc(exp_ok, 1)


def mix(pr, W2, scratch, base, router, mlp_raw):
    nc, ins, D, KD, NC = pr.nc, pr.ins, pr.D, pr.KD, pr.NC
    with ExitStack() as ctx:
        m32 = sb(nc, ctx, "mT32", [P, 2, KD, CH])
        m_hi, m_lo = (sb(nc, ctx, n, [P, 2, 2, KD, CH], F32R) for n in ("mT_hi", "mT_lo"))
        og_hi, og_lo = (sb(nc, ctx, n, [P, 2, 2, KD, CH], F32R) for n in ("og_hi", "og_lo"))
        h_in = sb(nc, ctx, "h_in", [P, 2, 2, TPC, D])
        xn = sb(nc, ctx, "xn", [P, 2, 2, TPC, D])
        t1, o32, g_sb, og32 = (sb(nc, ctx, n, [P, 2, CH]) for n in ("t1", "o32", "g_sb", "og32"))
        stats, mv = sb(nc, ctx, "stats2", [P, 2, TPC, 6]), sb(nc, ctx, "mv2", [P, 2, TPC, 2])
        spread, rstd, power, shift = (sb(nc, ctx, n, [P, 2, TPC]) for n in ("spread2", "rstd2", "power2", "shift2"))
        scrap, w_now = sb(nc, ctx, "scrap", [P, D]), sb(nc, ctx, "w_now", [P, 2, TPC])
        V = [ps(nc, ctx, f"V{i}") for i in range(2)]
        GB = [ps(nc, ctx, f"GB{i}") for i in range(2)]
        OP = [[ps(nc, ctx, f"OP{s}{i}") for i in range(2)] for s in range(2)]
        (m_ld, hi_ok, lo_ok, vv, gg, t_ok, g_ok, o_ok, og_ok, ogh_ok, ogl_ok, op, h2_ok, st_ok, mv_ok,
         sp_ok, rs_ok, rs2_ok, sh_ok, xn_ok, w_ok, w_kept, power_ok, raw_ld) = (pr.sem("mx_" + n) for n in (
            "m_ld", "hi_ok", "lo_ok", "vv", "gg", "t_ok", "g_ok", "o_ok", "og_ok", "ogh_ok", "ogl_ok", "op",
            "h2_ok", "st_ok", "mv_ok", "sp_ok", "rs_ok", "rs2_ok", "sh_ok", "xn_ok", "w_ok", "w_kept", "power_ok", "raw_ld"))
        xn_ok = [xn_ok, pr.sem("mx_xn_ok1")]
        h_ld = [pr.sem(f"mx_h_ld{h}") for h in range(2)]
        st_x = [[pr.sem(f"mx_st_x{s}{h}") for h in range(2)] for s in range(2)]
        block = ctx.enter_context(nc.Block())

        def chunks(eng, step):
            for c in range(2):
                step(c, c)
            if NC > 4:
                with eng.Fori(1, NC // 2 - 1) as p:
                    for h in range(2):
                        step(p * 2 + h, h)
            for c in range(NC - 2, NC + 2):
                step(c, c % 2)

        def within(c, back=0):
            return not isinstance(c, int) or 0 <= c - back < NC

        @block.sync
        def _(sp):
            def load_m(c):
                for b in range(2):
                    sp.dma_start(m32[:, b], scratch["mnT"][b, c]).then_inc(m_ld, 16)

            def store(c, h, s):
                sp.wait_ge(xn_ok[s], (c + 1) * TPC)
                sp.dma_start(scratch["xn"][s, c], xn[:, h, s]).then_inc(st_x[s][h], 16)

            def step(c, h):
                if within(c, -1):
                    sp.wait_ge(lo_ok, c + 1)
                    load_m(c + 1)
                if within(c):
                    past(sp, h2_ok, c * 4 - 4)
                    for s in range(2):
                        sp.dma_start(h_in[:, h, s], scratch["h"][s, c]).then_inc(h_ld[h], 16)
                if within(c, 2):
                    store(c - 2, h, 1)
                if within(c, 1):
                    store(c - 1, 1 - h, 0)

            for s in range(2):
                for h in range(2):
                    sp.sem_inc(st_x[s][h], 1)
            load_m(0)
            chunks(sp, step)
            sp.dma_start(mlp_raw["w1"], ins["ffn_w1"].rearrange("(k p) n -> p k n", p=P)).then_inc(raw_ld, 16)
            sp.dma_start(mlp_raw["w2"], ins["ffn_w2"].rearrange("(k p) n -> p k n", p=P)).then_inc(raw_ld, 16)
            for s in range(2):
                for h in range(2):
                    sp.wait_ge(st_x[s][h], 8 * NC + 1)
            sp.wait_ge(raw_ld, 32)

        @block.scalar
        def _(act):
            def split(c, h):
                act.wait_ge(m_ld, (c + 1) * 32)
                nc.scalar.activation(m_hi[:, h], m32[:, :, :, :], ACT.Copy).then_inc(hi_ok, 1)

            def norm(c, h, s):
                past(act, st_x[s][h], (c - h) * 8 + 1)
                act.wait_ge(sh_ok, c * 2 + s + 1)
                for j in range(TPC):
                    nc.scalar.activation(xn[:, h, s, j, :], base[:, s, c * TPC + j, :], ACT.Identity,
                                         bias=shift[:, s, j:j + 1], scale=rstd[:, s, j:j + 1]).then_inc(xn_ok[s], 1)

            def blend(c, j):
                n = c * 4 + 2 * j
                act.wait_ge(vv, n + 2)
                past(act, o_ok, n)
                for s in range(2):
                    nc.scalar.activation(t1[:, s, :], V[1][:, :], ACT.Copy,
                                         scale=W2["att"][:, s, 1, j:j + 1]).then_inc(t_ok, 1)
                past(act, og_ok, n)
                for s in range(2):
                    act.wait_ge(gg, n + s + 1)
                    nc.scalar.activation(g_sb[:, s, :], GB[s][:, :], ACT.Sigmoid,
                                         bias=W2["bg_col"][:, j:j + 1]).then_inc(g_ok, 1)

            def high(c, h, j):
                past(act, op, (c - 1) * 4)
                for s in range(2):
                    act.wait_ge(og_ok, c * 4 + 2 * j + s + 1)
                    nc.scalar.activation(og_hi[:, h, s, j, :], og32[:, s, :], ACT.Copy).then_inc(ogh_ok, 1)

            def step(c, h):
                if within(c):
                    blend(c, 0)
                    high(c, h, 0)
                if within(c, 2):
                    norm(c - 2, h, 1)
                if within(c, -1):
                    split(c + 1, 1 - h)
                if within(c):
                    blend(c, 1)
                if within(c, 1):
                    norm(c - 1, 1 - h, 0)
                if within(c):
                    high(c, h, 1)

            split(0, 0)
            chunks(act, step)

        @block.vector
        def _(dve):
            def mixed(c, j):
                for s in range(2):
                    n = c * 4 + 2 * j + s
                    past(dve, og_ok, n - 1)
                    dve.wait_ge(t_ok, n + 1)
                    nc.vector.scalar_tensor_tensor(o32[:, s, :], V[0][:, :], W2["att"][:, s, 0, j:j + 1], t1[:, s, :],
                                                   ALU.mult, ALU.add).then_inc(o_ok, 1)

            def low(c, h, j):
                for s in range(2):
                    dve.wait_ge(ogh_ok, c * 4 + 2 * j + s + 1)
                    nc.vector.tensor_tensor(og_lo[:, h, s, j, :], og32[:, s, :], og_hi[:, h, s, j, :].bitcast(F32),
                                            ALU.subtract).then_inc(ogl_ok, 1)

            def moments(c, h, s):
                dve.wait_ge(h_ld[h], (c - h) * 16 + 32)
                past(dve, xn_ok[s], c * TPC)
                for i in range(2):
                    dve.wait_ge(op, c * 4 + 2 * s + i + 1)
                    nc.vector.tensor_tensor(base[:, s, bass.ds(c * TPC + 2 * i, 2), :], OP[s][i][:, :],
                                            h_in[:, h, s, 2 * i:2 * i + 2, :], ALU.add).then_inc(h2_ok, 1)
                for j in range(TPC):
                    dve.wait_ge(h2_ok, c * 4 + 2 * s + j // 2 + 1)
                    pr.stand_alone(dve)
                    nc.vector.bn_stats(stats[:, s, j, :], base[:, s, c * TPC + j, :]).then_inc(st_ok, 1)
                for j in range(TPC):
                    dve.wait_ge(st_ok, c * 8 + 4 * s + j + 1)
                    pr.stand_alone(dve)
                    nc.vector.bn_aggr(mv[:, s, j, :], stats[:, s, j, :]).then_inc(mv_ok, 1)

            def route(c, h):
                past(dve, w_kept, c + 1)
                for s in range(2):
                    dve.wait_ge(xn_ok[s], (c + 1) * TPC)
                    for j in range(TPC):
                        past(dve, w_ok, c * 8 + 4 * s + j)
                        nc.vector.tensor_tensor_reduce(out=scrap[:, :], in0=xn[:, h, s, j, :], in1=W2["wr"][:, :],
                                                       scale=1.0, scalar=0.0, op0=ALU.mult, op1=ALU.add,
                                                       accum_out=w_now[:, s, j:j + 1]).then_inc(w_ok, 1)
                dve.wait_ge(w_ok, (c + 1) * 8)
                nc.vector.tensor_copy(router[:, :, bass.ds(c * TPC, TPC)], w_now[:, :, :]).then_inc(w_kept, 1)

            def step(c, h):
                if within(c):
                    mixed(c, 0)
                if within(c, 1):
                    low(c - 1, 1 - h, 1)
                    moments(c - 1, 1 - h, 0)
                if within(c):
                    mixed(c, 1)
                    low(c, h, 0)
                if within(c, 1):
                    moments(c - 1, 1 - h, 1)
                if within(c, 2):
                    route(c - 2, h)

            dve.sem_inc(w_kept, 1)
            chunks(dve, step)
            dve.wait_ge(w_kept, NC + 1)

        @block.gpsimd
        def _(pool):
            nc.gpsimd.memset(power[:, :, :], -0.5).then_inc(power_ok, 1)

            def split(c, h):
                pool.wait_ge(hi_ok, c + 1)
                nc.gpsimd.tensor_tensor(m_lo[:, h], m32[:, :, :, :], m_hi[:, h].bitcast(F32), ALU.subtract).then_inc(lo_ok, 1)

            def gated(c, j):
                for s in range(2):
                    n = c * 4 + 2 * j + s
                    past(pool, ogl_ok, n - 1)
                    pool.wait_ge(o_ok, n + 1)
                    pool.wait_ge(g_ok, n + 1)
                    nc.gpsimd.tensor_tensor(og32[:, s, :], o32[:, s, :], g_sb[:, s, :], ALU.mult).then_inc(og_ok, 1)

            def scale(c, s):
                pool.wait_ge(mv_ok, c * 8 + 4 * s + 4)
                pr.stand_alone(pool)
                nc.gpsimd.tensor_scalar(spread[:, s, :], mv[:, s, :, 1], EPS, None, ALU.add).then_inc(sp_ok, 1)
                pool.wait_ge(power_ok, 1)
                pool.wait_ge(sp_ok, c * 2 + s + 1)
                nc.gpsimd.tensor_tensor(rstd[:, s, :], spread[:, s, :], power[:, s, :], ALU.pow).then_inc(rs_ok, 1)
                pool.wait_ge(rs_ok, c * 2 + s + 1)
                nc.gpsimd.tensor_tensor(shift[:, s, :], mv[:, s, :, 0], rstd[:, s, :], ALU.mult).then_inc(rs2_ok, 1)
                pool.wait_ge(rs2_ok, c * 2 + s + 1)
                pr.stand_alone(pool)
                nc.gpsimd.tensor_scalar(shift[:, s, :], shift[:, s, :], -1.0, None, ALU.mult).then_inc(sh_ok, 1)

            def step(c, h):
                if within(c):
                    gated(c, 0)
                if within(c, 1):
                    scale(c - 1, 0)
                if within(c, -1):
                    split(c + 1, 1 - h)
                if within(c):
                    gated(c, 1)
                if within(c, 1):
                    scale(c - 1, 1)

            split(0, 0)
            chunks(pool, step)

        @block.tensor
        def _(pe):
            def values_and_gates(c, h, j):
                cols = slice(j * P, (j + 1) * P)
                n = c * 4 + 2 * j
                past(pe, o_ok, n)
                for w, bank, sem, b in (("v", V[1], vv, 1), ("v", V[0], vv, 0), ("g", GB[0], gg, 0), ("g", GB[1], gg, 1)):
                    if w == "g":
                        past(pe, g_ok, n - 1 + b)
                    i = 0
                    for k in range(KD):
                        for ww, x in split_products(W2[w + "_hi"][:, k, cols], W2[w + "_lo"][:, k, cols],
                                                    m_hi[:, h, b, k, :], m_lo[:, h, b, k, :]):
                            i += 1
                            mm = pe.matmul(bank[:, :], ww, x, start=i == 1, stop=i == 3 * KD)
                    mm.then_inc(sem, 1)

            def project(c, h, s):
                pe.wait_ge(ogl_ok, c * 4 + 3 + s)
                past(pe, h2_ok, c * 4 + 2 * s - 2)
                for i in range(2):
                    for j in (2 * i, 2 * i + 1):
                        rows = slice(j * P, (j + 1) * P)
                        n = 0
                        for k in range(KD):
                            for x, w in split_products(og_hi[:, h, s, k, rows], og_lo[:, h, s, k, rows],
                                                       W2["o_hi"][:, k, :], W2["o_lo"][:, k, :]):
                                mm = pe.matmul(OP[s][i][:, (j % 2) * D:(j % 2 + 1) * D], x, w,
                                               start=j % 2 == 0 and n == 0, stop=n == 5, skip_group_check=True)
                                n += 1
                    mm.then_inc(op, 1)

            def step(c, h):
                if within(c):
                    pe.wait_ge(lo_ok, c + 1)
                    values_and_gates(c, h, 0)
                if within(c, 1):
                    project(c - 1, 1 - h, 0)
                if within(c):
                    values_and_gates(c, h, 1)
                if within(c, 1):
                    project(c - 1, 1 - h, 1)

            chunks(pe, step)


STEPS = 4
PIV = 15
SEARCH = 4


def split_mlp_weights(pr, W3, raw):
    nc, ins = pr.nc, pr.ins
    with ExitStack() as ctx:
        ld, hi, lo, made = (pr.sem(n) for n in ("mw_ld", "mw_hi", "mw_lo", "mw_made"))
        block = ctx.enter_context(nc.Block())

        @block.sync
        def _(sp):
            for i in range(2):
                sp.dma_start(W3["b2"][:, i, :], ins["ffn_b2"].partition_broadcast(P)).then_inc(ld, 16)
            with nc.allow_non_contiguous_dma(reason="a bias column, once"):
                sp.dma_start(W3["b1"][:, :], ins["ffn_b1"].rearrange("(k p) -> p k", p=P)).then_inc(ld, 16)
            sp.wait_ge(ld, 48)

        @block.gpsimd
        def _(pool):
            nc.gpsimd.memset(W3["ones"][:, :], 1.0).then_inc(made, 1)
            pool.wait_ge(made, 1)
            nc.gpsimd.affine_select(out=W3["before"][:, :], in_=W3["ones"][:, :], compare_op=ALU.is_gt, fill=0.0,
                                    base=0, pattern=[[1, P]], channel_multiplier=-1).then_inc(made, 1)
            nc.gpsimd.iota(W3["index"][:, :], pattern=[[1, PIV]], base=1, channel_multiplier=0).then_inc(made, 1)
            pool.wait_ge(made, 3)
            nc.gpsimd.tensor_copy(W3["digit"][:, :], W3["index"][:, :]).then_inc(made, 1)
            pool.wait_ge(made, 4)

        @block.scalar
        def _(act):
            nc.scalar.activation(W3["w1_hi"][:, :, :], raw["w1"], ACT.Copy).then_inc(hi, 1)
            nc.scalar.activation(W3["w2_hi"][:, :, :], raw["w2"], ACT.Copy).then_inc(hi, 1)

        @block.vector
        def _(dve):
            for n, x in enumerate(("w1", "w2")):
                dve.wait_ge(hi, n + 1)
                nc.vector.tensor_tensor(W3[x + "_lo"][:, :, :], raw[x], W3[x + "_hi"][:, :, :].bitcast(F32),
                                        ALU.subtract).then_inc(lo, 1)
            dve.wait_ge(lo, 2)


def mlp(pr, W2, W3, ident_r, scratch, base, router, work):
    nc, D, KD, NC, ST, F, B = pr.nc, pr.D, pr.KD, pr.NC, pr.ST, pr.F, pr.B
    FT, NU = F // P, B * NC
    K = max(1, int(0.5 * pr.T)) - 1
    LAG = 2
    SPLIT, TURN, SPLIT_T = 1, 3, 4
    assert FT == 8 and SEARCH * 2 == STEPS * 2 and NU >= SEARCH + 4
    with ExitStack() as ctx:
        out_sb = work[:, 0:2 * TPC * D].rearrange("p (h j d) -> p h j d", h=2, j=TPC)
        act32 = work[:, 2 * TPC * D:2 * TPC * D + 2 * CH].rearrange("p (i t) -> p i t", i=2)
        x32 = work[:, 3 * TPC * D:4 * TPC * D].rearrange("p (j d) -> p j d", j=TPC)
        s_hi, s_lo = (sb(nc, ctx, n, [P, TPC, D], F32R) for n in ("xn_hi", "xn_lo"))
        x_hi, x_lo = (sb(nc, ctx, n, [P, 2, KD, CH], F32R) for n in ("fx_hi", "fx_lo"))
        a_hi, a_lo = (sb(nc, ctx, n, [P, 2, CH], F32R) for n in ("act_hi", "act_lo"))
        y = sb(nc, ctx, "y", [P, B * ST, D])
        key_f, w_br = sb(nc, ctx, "key_f", [P, B, ST]), sb(nc, ctx, "w_br", [P, B, ST])
        low_f, above, equal, pick = (sb(nc, ctx, n, [P, B, ST]) for n in ("low_f", "above", "equal", "pick"))
        sign, key, part = (sb(nc, ctx, n, [P, B, ST], I32) for n in ("sign", "key", "part"))
        equal_b, earlier_b = (sb(nc, ctx, n, [P, B, ST], BF16) for n in ("equal_b", "earlier_b"))
        pivots, counts = sb(nc, ctx, "pivots", [P, B, PIV]), sb(nc, ctx, "counts", [P, B * PIV], BF16)
        passed = sb(nc, ctx, "passed", [P, B, PIV, ST], BF16)
        found, digit, need = sb(nc, ctx, "found", [P, B]), sb(nc, ctx, "dig", [P, B]), sb(nc, ctx, "need", [P, B])
        reach, zero = sb(nc, ctx, "reach", [P, B, PIV]), sb(nc, ctx, "zero", [P, ST])
        above_n = sb(nc, ctx, "above_n", [P, B], BF16)
        HB = [ps(nc, ctx, f"HB{i}") for i in range(2)]
        YB = [ps(nc, ctx, f"YB{i}") for i in range(2)]
        TR = [ps(nc, ctx, f"XT{i}") for i in range(KD)]
        CB = ps(nc, ctx, "CB")
        (x_ld, shi_ok, slo_ok, turned, hi_ok, lo_ok, base_ok, h1, gelu_ok, ah_ok, al_ok, y_done, y_kept, chain,
         counted, summed, out_ok) = (
            pr.sem("ff_" + n) for n in ("x_ld", "shi_ok", "slo_ok", "turned", "hi_ok", "lo_ok", "base_ok", "h1",
                                        "gelu_ok", "ah_ok", "al_ok", "y_done", "y_kept", "chain", "counted",
                                        "summed", "out_ok"))
        st_out = [pr.sem(f"ff_st_out{h}") for h in range(2)]
        block = ctx.enter_context(nc.Block())
        x_all = scratch["xn"].rearrange("b c p j d -> (b c) p j d")
        out_all = pr.out.rearrange("b (c j p) d -> (b c) p j d", p=P, j=TPC)
        all_base = base[:, :, :, :].rearrange("p b t d -> p (b t) d")
        all_pick = pick[:, :, :].rearrange("p b t -> p (b t)")

        def chunks(eng, step):
            for u in range(SEARCH + 2):
                step(u, u % 2)
            if NU > SEARCH + 4:
                with eng.Fori(SEARCH // 2 + 1, NU // 2 - 1) as p:
                    for h in range(2):
                        step(p * 2 + h, h)
            for u in range(NU - 2, NU):
                step(u, u % 2)

        def last(u):
            return isinstance(u, int) and u == NU - 1

        def given(u, h):
            if early(u, SEARCH):
                return ()
            if early(u, SEARCH + 2):
                return ((2 * (u - SEARCH), 0), (2 * (u - SEARCH) + 1, 1))
            return ((u - 2, h),)

        @block.sync
        def _(sp):
            def load(u):
                sp.dma_start(x32, x_all[u]).then_inc(x_ld, 16)

            def store(k, h):
                sp.wait_ge(out_ok, (k + 1) * TPC)
                sp.dma_start(out_all[k], out_sb[:, h]).then_inc(st_out[h], 16)

            def step(u, h):
                if not last(u):
                    sp.wait_ge(slo_ok, u + 1)
                    sp.wait_ge(base_ok, u + 1)
                    load(u + 1)
                for k, kh in given(u, h):
                    store(k, kh)

            load(0)
            chunks(sp, step)
            store(NU - 2, 0)
            store(NU - 1, 1)
            for h in range(2):
                sp.wait_ge(st_out[h], 16 * (NU // 2))

        @block.gpsimd
        def _(pool):
            def step(u, h):
                pool.wait_ge(x_ld, (u + 1) * 16)
                nc.gpsimd.tensor_tensor(all_base[:, bass.ds(u * TPC, TPC), :], all_base[:, bass.ds(u * TPC, TPC), :],
                                        x32, ALU.add).then_inc(base_ok, 1)

            chunks(pool, step)

        @block.scalar
        def _(act):
            def split(u):
                past(act, turned, u)
                act.wait_ge(x_ld, (u + 1) * 16)
                nc.scalar.activation(s_hi[:, :, :], x32, ACT.Copy).then_inc(shi_ok, 1)

            def split_turned(u, h):
                act.wait_ge(turned, u + 1)
                for k in range(KD):
                    nc.scalar.activation(x_hi[:, h, k, :], TR[k][:, :], ACT.Copy).then_inc(hi_ok, 1)

            def step(u, h):
                for j in range(FT):
                    act.wait_ge(h1, u * FT + j + 1)
                    past(act, al_ok, u * FT + j - 1)
                    nc.scalar.activation(act32[:, j % 2, :], HB[j % 2][:, :], ACT.Gelu_apprx_tanh,
                                         bias=W3["b1"][:, j:j + 1]).then_inc(gelu_ok, 1)
                    past(act, y_done, u * FT + j - 1)
                    act.wait_ge(gelu_ok, u * FT + j + 1)
                    nc.scalar.activation(a_hi[:, j % 2, :], act32[:, j % 2, :], ACT.Copy).then_inc(ah_ok, 1)
                    if j == SPLIT and not last(u):
                        split(u + 1)
                    if j == SPLIT_T and not last(u):
                        split_turned(u + 1, 1 - h)

            split(0)
            split_turned(0, 0)
            chunks(act, step)

        @block.vector
        def _(dve):
            links = [0]

            def link(ins):
                links[0] += 1
                ins.then_inc(chain, 1)
                dve.wait_ge(chain, links[0])

            def split(u):
                dve.wait_ge(shi_ok, u + 1)
                nc.vector.tensor_tensor(s_lo[:, :, :], x32, s_hi[:, :, :].bitcast(F32), ALU.subtract).then_inc(slo_ok, 1)

            def split_turned(u, h):
                for k in range(KD):
                    dve.wait_ge(hi_ok, u * KD + k + 1)
                    nc.vector.tensor_tensor(x_lo[:, h, k, :], TR[k][:, :], x_hi[:, h, k, :].bitcast(F32),
                                            ALU.subtract).then_inc(lo_ok, 1)

            def make_keys():
                w = w_br[:, :, :]
                link(nc.vector.tensor_scalar(w, router[:, :, :], W2["br"][:, 0:1], None, ALU.add))
                bits = w.bitcast(I32)
                link(nc.vector.tensor_scalar(sign[:, :, :], bits, 31, -2147483648, ALU.arith_shift_right, ALU.bitwise_or))
                link(nc.vector.tensor_tensor(key[:, :, :], bits, sign[:, :, :], ALU.bitwise_xor))
                link(nc.vector.tensor_scalar(part[:, :, :], key[:, :, :], 16, None, ALU.logical_shift_right))
                link(nc.vector.tensor_copy(key_f[:, :, :], part[:, :, :]))
                link(nc.vector.tensor_scalar(part[:, :, :], key[:, :, :], 65535, None, ALU.bitwise_and))
                link(nc.vector.tensor_copy(low_f[:, :, :], part[:, :, :]))
                link(nc.vector.memset(found[:, :], 0.0))
                link(nc.vector.memset(zero[:, :], 0.0))

            def count(q):
                for b in range(B):
                    link(nc.vector.tensor_scalar(pivots[:, b, :], W3["digit"][:, :], float(16 ** (STEPS - 1 - q)),
                                                 found[:, b:b + 1], ALU.mult, ALU.add))
                shape = [P, B, PIV, ST]
                link(nc.vector.tensor_tensor(passed[:, :, :, :], key_f[:, :, :].unsqueeze(2).to_broadcast(shape),
                                             pivots[:, :, :].unsqueeze(3).to_broadcast(shape), ALU.is_ge))
                with nc.allow_low_precision("counts up to 32"):
                    nc.vector.tensor_reduce(counts[:, :], passed[:, :, :, :].rearrange("p b q t -> p (b q) t"), AX_X,
                                            ALU.add).then_inc(counted, 1)

            def advance(n, q):
                dve.wait_ge(summed, n + 1)
                for b in range(B):
                    link(nc.vector.tensor_scalar(reach[:, b, :], CB[:, b * PIV:(b + 1) * PIV], float(K), None, ALU.is_ge))
                link(nc.vector.tensor_reduce(digit[:, :], reach[:, :, :], AX_X, ALU.add))
                link(nc.vector.scalar_tensor_tensor(found[:, :], digit[:, :], float(16 ** (STEPS - 1 - q)), found[:, :],
                                                    ALU.mult, ALU.add))

            def compare(out, in0, op):
                for b in range(B):
                    link(nc.vector.tensor_scalar(out[:, b, :], in0[:, b, :], found[:, b:b + 1], None, op))

            def low_keys():
                compare(above, key_f, ALU.is_gt)
                compare(equal, key_f, ALU.is_equal)
                link(nc.vector.scalar_tensor_tensor(low_f[:, :, :], low_f[:, :, :], 1.0, equal[:, :, :], ALU.add, ALU.mult))
                link(nc.vector.scalar_tensor_tensor(key_f[:, :, :], above[:, :, :], 131072.0, low_f[:, :, :], ALU.mult, ALU.add))
                link(nc.vector.memset(found[:, :], 1.0))

            def tie_counts():
                compare(above, key_f, ALU.is_gt)
                compare(equal, key_f, ALU.is_equal)
                with nc.allow_low_precision("counts up to 32"):
                    link(nc.vector.tensor_reduce(above_n[:, :], above[:, :, :], AX_X, ALU.add))
                link(nc.vector.tensor_copy(equal_b[:, :, :], equal[:, :, :]))
                for b in range(B):
                    link(nc.vector.tensor_tensor_scan(pick[:, b, :], zero[:, :], equal[:, b, :], 0.0, ALU.add, ALU.add))
                nc.vector.tensor_tensor(earlier_b[:, :, :], pick[:, :, :], equal[:, :, :], ALU.subtract).then_inc(counted, 1)

            def choose():
                dve.wait_ge(summed, 2 * STEPS + 1)
                link(nc.vector.tensor_scalar(need[:, :], CB[:, 256:256 + B], -1.0, float(K), ALU.mult, ALU.add))
                for b in range(B):
                    link(nc.vector.tensor_scalar(pick[:, b, :], CB[:, b * ST:(b + 1) * ST], need[:, b:b + 1], None, ALU.is_lt))
                link(nc.vector.tensor_tensor(pick[:, :, :], pick[:, :, :], equal[:, :, :], ALU.mult))
                link(nc.vector.tensor_tensor(pick[:, :, :], pick[:, :, :], above[:, :, :], ALU.add))
                link(nc.vector.tensor_tensor(pick[:, :, :], pick[:, :, :], w_br[:, :, :], ALU.mult))

            def keep_y(u):
                dve.wait_ge(y_done, (u + 1) * FT)
                for i in range(2):
                    nc.vector.tensor_tensor(y[:, bass.ds(u * TPC + 2 * i, 2), :], YB[i][:, :], W3["b2"][:, :, :],
                                            ALU.add).then_inc(y_kept, 1)

            def give(k, h):
                past(dve, st_out[h], (k - h) * 8)
                dve.wait_ge(base_ok, k + 1)
                dve.wait_ge(y_kept, (k + 1) * 2)
                for j in range(TPC):
                    nc.vector.scalar_tensor_tensor(out_sb[:, h, j, :], y[:, k * TPC + j, :],
                                                   all_pick[:, bass.ds(k * TPC + j, 1)], all_base[:, k * TPC + j, :],
                                                   ALU.mult, ALU.add).then_inc(out_ok, 1)

            def step(u, h):
                for j in range(FT):
                    dve.wait_ge(ah_ok, u * FT + j + 1)
                    nc.vector.tensor_tensor(a_lo[:, j % 2, :], act32[:, j % 2, :], a_hi[:, j % 2, :].bitcast(F32),
                                            ALU.subtract).then_inc(al_ok, 1)
                    if j == 0 and not early(u, 1):
                        keep_y(u - 1)
                    if j == SPLIT and not last(u):
                        split(u + 1)
                    if j == SPLIT_T and not last(u):
                        split_turned(u + 1, 1 - h)
                    if j in (3, 6):
                        for k, kh in given(u, h)[j // 5:j // 5 + 1]:
                            give(k, kh)
                    if early(u, SEARCH):
                        n = 2 * u + j // 4
                        if j % 4 == 1:
                            count(n % STEPS)
                        if j % 4 == 3:
                            advance(n, n % STEPS)
                            if n == STEPS - 1:
                                low_keys()
                            if n == 2 * STEPS - 1:
                                tie_counts()
                    if isinstance(u, int) and u == SEARCH and j == 2:
                        choose()

            split(0)
            make_keys()
            split_turned(0, 0)
            chunks(dve, step)
            give(NU - 2, 0)
            keep_y(NU - 1)
            give(NU - 1, 1)

        @block.tensor
        def _(pe):
            def turn(u):
                past(pe, lo_ok, u * KD)
                pe.wait_ge(slo_ok, u + 1)
                for k in range(KD):
                    for j in range(TPC):
                        out, d = TR[k][:, j * P:(j + 1) * P], slice(k * P, (k + 1) * P)
                        pe.matmul(out, s_hi[:, j, d], ident_r[:, :], start=True, stop=False)
                        t = pe.matmul(out, s_lo[:, j, d], ident_r[:, :], start=False, stop=True)
                t.then_inc(turned, 1)

            def second(u, j):
                pe.wait_ge(al_ok, u * FT + j + 1)
                if j == 0:
                    past(pe, y_kept, u * 2)
                for t in range(TPC):
                    rows = slice(t * P, (t + 1) * P)
                    for n, (a, w) in enumerate(split_products(a_hi[:, j % 2, rows], a_lo[:, j % 2, rows],
                                                              W3["w2_hi"][:, j, :], W3["w2_lo"][:, j, :])):
                        mm = pe.matmul(YB[t // 2][:, (t % 2) * D:(t % 2 + 1) * D], a, w,
                                       start=j == 0 and t % 2 == 0 and n == 0, stop=j == FT - 1 and n == 2,
                                       skip_group_check=True)
                mm.then_inc(y_done, 1)

            def step(u, h):
                pe.wait_ge(lo_ok, (u + 1) * KD)
                for j in range(FT):
                    past(pe, gelu_ok, u * FT + j - 1)
                    cols = slice(j * P, (j + 1) * P)
                    n = 0
                    for k in range(KD):
                        for w, x in split_products(W3["w1_hi"][:, k, cols], W3["w1_lo"][:, k, cols],
                                                   x_hi[:, h, k, :], x_lo[:, h, k, :]):
                            n += 1
                            mm = pe.matmul(HB[j % 2][:, :], w, x, start=n == 1, stop=n == 3 * KD)
                    mm.then_inc(h1, 1)
                    if j >= LAG:
                        second(u, j - LAG)
                    elif j == 0 and not early(u, 1):
                        for back in range(LAG, 0, -1):
                            second(u - 1, FT - back)
                    if j == TURN and not last(u):
                        turn(u + 1)
                    if early(u, SEARCH) and j % 4 == 3:
                        n = 2 * u + j // 4
                        pe.wait_ge(counted, n + 1)
                        pe.matmul(CB[:, 0:B * PIV], W3["ones"][:, :], counts[:, :], start=True, stop=True).then_inc(summed, 1)
                    if isinstance(u, int) and u == SEARCH and j == 1:
                        pe.wait_ge(counted, 2 * STEPS + 1)
                        flat = (equal_b[:, :, :].rearrange("p b t -> p (b t)"), earlier_b[:, :, :].rearrange("p b t -> p (b t)"))
                        pe.matmul(CB[:, 0:B * ST], W3["before"][:, :], flat[0], start=True, stop=False, skip_group_check=True)
                        pe.matmul(CB[:, 0:B * ST], W3["ones"][:, :], flat[1], start=False, stop=True, skip_group_check=True)
                        pe.matmul(CB[:, 256:256 + B], W3["ones"][:, :], above_n[:, :], start=False, stop=True,
                                  skip_group_check=True).then_inc(summed, 1)

            turn(0)
            chunks(pe, step)
            for back in range(LAG, 0, -1):
                second(NU - 1, FT - back)


def tokenizer_tables(pr, ctx):
    nc, KD, D = pr.nc, pr.KD, pr.D
    W = {n: sb(nc, ctx, n, [P, D]) for n in ("gamma", "beta", "attn_bo")}
    W["prelu"] = sb(nc, ctx, "prelu", [P, 1])
    W["bo_col"], W["bk_col"] = sb(nc, ctx, "bo_col", [P, KD]), sb(nc, ctx, "bk_col", [P, KD])
    W["v_bias"] = sb(nc, ctx, "v_bias", [P, D + 2])
    W["a_hi"], W["a_lo"] = (sb(nc, ctx, n, [P, KD, D], F32R) for n in ("a_hi", "a_lo"))
    W["vo_hi"], W["vo_lo"] = (sb(nc, ctx, n, [P, KD, D + 2], F32R) for n in ("vo_hi", "vo_lo"))
    return W


def build(nc, ins, out, batches, tokens, width, heads, hidden):
    KD, NC, FT = width // P, tokens // CH, hidden // P
    with ExitStack() as ctx:
        pr = Program(nc, ctx, ins, out, batches, tokens, width, heads, hidden)
        scratch = {n: nc.dram_tensor(f"scratch_{n}", (batches, NC, P) + s, F32, kind="Internal").ap() for n, s in (
            ("h", (TPC, width)), ("mn", (TPC, width)), ("mnT", (KD, CH)), ("xn", (TPC, width)))}
        ident_r = sb(nc, ctx, "ident_r", [P, P], F32R)
        work = sb(nc, ctx, "work", [P, 2 * KD * hidden])
        with ExitStack() as phase:
            W = tokenizer_tables(pr, phase)
            setup_weights(pr, W, ident_r)
            tokenizer(pr, W, ident_r, scratch, work)
        base = sb(nc, ctx, "base", [P, batches, pr.ST, width])
        router = sb(nc, ctx, "router", [P, batches, pr.ST])
        W2 = {"wr": sb(nc, ctx, "wr", [P, width]), "br": sb(nc, ctx, "br", [P, 1])}
        mlp_raw = {"w1": work[:, 0:KD * hidden].rearrange("p (k n) -> p k n", k=KD),
                   "w2": work[:, KD * hidden:2 * KD * hidden].rearrange("p (k n) -> p k n", k=FT)}
        with ExitStack() as phase:
            W2["bg_col"], W2["att"] = sb(nc, phase, "bg_col", [P, KD]), sb(nc, phase, "att_w", [P, 2, 2, KD])
            for x in "vgo":
                W2[x + "_hi"], W2[x + "_lo"] = (sb(nc, phase, f"w{x}{n}", [P, KD, width], F32R) for n in ("_hi", "_lo"))
            head_weights(pr, W2, gram_view(work, width))
            mix(pr, W2, scratch, base, router, mlp_raw)
        with ExitStack() as phase:
            W3 = {f"{w}_{n}": sb(nc, phase, f"{w}_{n}", s, F32R) for w, s in (
                ("w1", [P, KD, hidden]), ("w2", [P, hidden // P, width])) for n in ("hi", "lo")}
            W3["b1"], W3["b2"] = sb(nc, phase, "b1", [P, hidden // P]), sb(nc, phase, "b2", [P, 2, width])
            W3["ones"], W3["before"] = sb(nc, phase, "ones", [P, P], BF16), sb(nc, phase, "before", [P, P], BF16)
            W3["index"], W3["digit"] = sb(nc, phase, "index", [P, PIV], I32), sb(nc, phase, "digit", [P, PIV])
            split_mlp_weights(pr, W3, mlp_raw)
            mlp(pr, W2, W3, ident_r, scratch, base, router, work)


def _layouts(inputs):
    import numpy as np

    a = {k: np.asarray(v) for k, v in inputs.items()}
    x, dg = a["x"], a["L0_tok_d_gamma_batched"]
    B, _, T, D = x.shape
    out = {
        "xT": x.reshape(B, T // CH, CH, D // P, P).transpose(0, 1, 4, 3, 2),
        "gateT": dg.reshape(T // CH, CH, T // P // GT, GT, P).transpose(0, 2, 4, 3, 1),
    }
    for n in ("Wq", "Wk", "Wv"):
        out[f"tok_{n}T"] = a[f"L0_tok_{n}"].T
    for n in ("Wo", "bq", "bk", "bv", "bo"):
        out[f"tok_{n}"] = a[f"L0_tok_{n}"]
    out["tok_prelu_a"] = a["L0_tok_prelu_a"].reshape(1)
    for n in ("gamma", "beta", "Wq", "Wk", "Wv", "Wg", "bg", "Wo", "bo"):
        out[f"attn_{n}"] = a[f"L0_attn_{n}"]
    out["ffn_wr"] = a["L0_ffn_wr"].reshape(-1)
    for n in ("br", "w1", "b1", "w2", "b2"):
        out[f"ffn_{n}"] = a[f"L0_ffn_{n}"]
    return {k: np.ascontiguousarray(v) for k, v in out.items()}, (B, T, D, a["L0_ffn_w1"].shape[1])


def kernel(**inputs):
    import concourse.bacc as bacc
    from concourse.bass_utils import run_bass_kernel_spmd

    arrays, (B, T, D, F) = _layouts(inputs)
    nc = bacc.Bacc("TRN2", target_bir_lowering=False, num_devices=1, dynamic_dma_scratch_size=1024)
    ins = {n: nc.dram_tensor(f"in_{n}", a.shape, mybir.dt.from_np(a.dtype), kind="ExternalInput").ap()
           for n, a in arrays.items()}
    out = nc.dram_tensor("out_0", (B, T, D), F32, kind="ExternalOutput").ap()
    build(nc, ins, out, B, T, D, HEADS, F)
    r = run_bass_kernel_spmd(nc, [{f"in_{n}": a for n, a in arrays.items()}], core_ids=[0])
    return r.results[0]["out_0"]
```

```python
from contextlib import ExitStack

import concourse.bass as bass
from concourse import mybir

P = 128
CH = 512
TPC = CH // P
GT = 2
RG = 4
RP = 4
EPS = 1e-5
HEADS = 8

F32 = mybir.dt.float32
F32R = mybir.dt.float32r
BF16 = mybir.dt.bfloat16
I32 = mybir.dt.int32
ALU = mybir.AluOpType
ACT = mybir.ActivationFunctionType
AX_X = mybir.AxisListType.X


def split_products(hi_w, lo_w, hi_x, lo_x):
    return ((hi_w, hi_x), (hi_w, lo_x), (lo_w, hi_x))


class Program:

    def __init__(self, nc, ctx, ins, out, batches, tokens, width, heads, hidden):
        self.nc, self.ctx, self.ins, self.out = nc, ctx, ins, out
        self.B, self.T, self.D, self.H, self.F = batches, tokens, width, heads, hidden
        self.KD = width // P
        self.NC = tokens // CH
        self.ST = tokens // P
        self.NG = self.ST // GT
        self.used = {}

    def stand_alone(self, eng):
        eng.sem_inc(self.sem("went_on"), 1)

    def sem(self, name):
        if name not in self.used:
            self.used[name] = self.ctx.enter_context(self.nc.semaphore(name))
        return self.used[name]


def early(c, n):
    return isinstance(c, int) and c < n


def past(eng, sem, n):
    if not early(n, 1):
        eng.wait_ge(sem, n)


def sb(nc, ctx, name, shape, dt=F32):
    return ctx.enter_context(nc.sbuf_tensor(name, shape, dt))


def ps(nc, ctx, name, shape=(P, CH), dt=F32):
    return ctx.enter_context(nc.psum_tensor(name, list(shape), dt))


def setup_weights(pr, W, ident_r, work):
    nc, ins, KD, D = pr.nc, pr.ins, pr.KD, pr.D
    with ExitStack() as ctx:
        wqT, wkT, wvT, wo = (sb(nc, ctx, n, [P, KD, D]) for n in ("wqT", "wkT", "wvT", "wo"))
        bq2, bk2, bv2 = (sb(nc, ctx, n, [P, KD, 2]) for n in ("bq2", "bk2", "bv2"))
        ones, ident = sb(nc, ctx, "ones_setup", [P, P]), sb(nc, ctx, "ident", [P, P])
        bq_rows, bv_rows = (sb(nc, ctx, n, [P, KD, P]) for n in ("bq_rows", "bv_rows"))
        a_f, vo_f = sb(nc, ctx, "a_f", [P, KD, D]), sb(nc, ctx, "vo_f", [P, KD, D + 2])
        pa, pv, (pb, pr_) = pr.banks[0:2], pr.banks[2:4], pr.banks[4:6]
        qk_loaded, vo_loaded, loaded, made, rows, prod, kept, hi_ok, lo_ok = (
            pr.sem("w_" + n) for n in ("qk_loaded", "vo_loaded", "loaded", "consts", "rows", "products", "kept",
                                       "hi", "lo"))
        n_loads = 3 * 2 + 1 + 4
        x_ld, x_hi_ok, x_lo_ok = pr.sem("xp_ld0"), pr.sem("xp_hi"), pr.sem("xp_lo")
        x32 = query_tiles(work, KD)[0]
        block = pr.block

        @block.sync
        def _(sp):
            for t, name, sem in ((wqT, "tok_WqT", qk_loaded), (wkT, "tok_WkT", qk_loaded),
                                 (wvT, "tok_WvT", vo_loaded), (wo, "tok_Wo", vo_loaded)):
                sp.dma_start(t[:, :, :], ins[name].rearrange("(k p) n -> p k n", p=P)).then_inc(sem, 16)
            sp.dma_start(x32, ins["xT"][0, 0]).then_inc(x_ld, 16)
            with nc.allow_non_contiguous_dma(reason="bias columns, once"):
                for t, name in ((bq2, "tok_bq"), (bk2, "tok_bk"), (bv2, "tok_bv")):
                    for j in range(2):
                        sp.dma_start(t[:, :, j], ins[name].rearrange("(k p) -> p k", p=P)).then_inc(loaded, 16)
                sp.dma_start(W["bo_col"][:, :], ins["tok_bo"].rearrange("(k p) -> p k", p=P)).then_inc(loaded, 16)
            sp.dma_start(W["gamma"][:, :], ins["attn_gamma"].partition_broadcast(P)).then_inc(loaded, 16)
            sp.dma_start(W["beta"][:, :], ins["attn_beta"].partition_broadcast(P)).then_inc(loaded, 16)
            sp.dma_start(W["attn_bo"][:, :], ins["attn_bo"].partition_broadcast(P)).then_inc(loaded, 16)
            sp.dma_start(W["prelu"][:, :], ins["tok_prelu_a"].partition_broadcast(P)).then_inc(loaded, 16)

        @block.gpsimd
        def _(pool):
            nc.gpsimd.memset(ident[:, :], 0.0).then_inc(made, 1)
            nc.gpsimd.memset(ones[:, :], 1.0).then_inc(made, 1)
            pool.wait_ge(made, 2)
            nc.gpsimd.affine_select(out=ident[:, :], in_=ident[:, :], compare_op=ALU.not_equal, fill=1.0,
                                    base=0, pattern=[[-1, P]], channel_multiplier=1).then_inc(made, 1)

        @block.vector
        def _(dve):
            for j in range(KD):
                dve.wait_ge(prod, j + 1)
                nc.vector.tensor_copy(a_f[:, j, :], pa[j][:, 0:D]).then_inc(kept, 1)
            dve.wait_ge(hi_ok, 1)
            nc.vector.tensor_tensor(W["a_lo"][:, :, :], a_f[:, :, :], W["a_hi"][:, :, :].bitcast(F32),
                                    ALU.subtract).then_inc(lo_ok, 1)
            dve.wait_ge(x_hi_ok, 1)
            nc.vector.tensor_tensor(W["x_lo"][:, 0], x32, W["x_hi"][:, 0].bitcast(F32), ALU.subtract).then_inc(x_lo_ok, 1)
            dve.wait_ge(loaded, 16 * n_loads)
            dve.wait_ge(made, 3)
            for k in range(KD):
                nc.vector.tensor_scalar(bq_rows[:, k, :], ones[:, :], bq2[:, k, 0:1], None,
                                        ALU.mult).then_inc(rows, 1)
                nc.vector.tensor_scalar(bv_rows[:, k, :], ones[:, :], bv2[:, k, 0:1], None,
                                        ALU.mult).then_inc(rows, 1)
            dve.wait_ge(prod, KD + 1)
            nc.vector.tensor_copy(W["bk_col"][:, :], pb[:, 0:2 * KD:2]).then_inc(kept, 1)
            for j in range(KD):
                nc.vector.tensor_copy(vo_f[:, j, :], pv[j][:, 0:D + 2]).then_inc(kept, 1)
            nc.vector.tensor_copy(W["v_bias"][:, :], pr_[:, 0:D + 2]).then_inc(kept, 1)
            dve.wait_ge(hi_ok, 2)
            nc.vector.tensor_tensor(W["vo_lo"][:, :, :], vo_f[:, :, :], W["vo_hi"][:, :, :].bitcast(F32),
                                    ALU.subtract).then_inc(lo_ok, 1)

        @block.scalar
        def _(act):
            act.wait_ge(made, 3)
            nc.scalar.activation(ident_r[:, :], ident[:, :], ACT.Copy).then_inc(made, 1)
            act.wait_ge(kept, KD)
            nc.scalar.activation(W["a_hi"][:, :, :], a_f[:, :, :], ACT.Copy).then_inc(hi_ok, 1)
            act.wait_ge(x_ld, 16)
            nc.scalar.activation(W["x_hi"][:, 0], x32, ACT.Copy).then_inc(x_hi_ok, 1)
            act.wait_ge(kept, 2 * KD + 1)
            nc.scalar.activation(W["vo_hi"][:, :, :], vo_f[:, :, :], ACT.Copy).then_inc(hi_ok, 1)

        @block.tensor
        def _(pe):
            pe.wait_ge(qk_loaded, 32)
            for j in range(KD):
                for k in range(KD):
                    mm = pe.matmul(pa[j][:, 0:D], wkT[:, k, j * P:(j + 1) * P], wqT[:, k, :], start=k == 0,
                                   stop=k == KD - 1)
                mm.then_inc(prod, 1)
            pe.wait_ge(vo_loaded, 32)
            for j in range(KD):
                for k in range(KD):
                    pe.matmul(pv[j][:, 0:D], wvT[:, k, j * P:(j + 1) * P], wo[:, k, :], start=k == 0, stop=k == KD - 1,
                              skip_group_check=True)
            pe.wait_ge(rows, 2 * KD)
            for j in range(KD):
                cols = slice(j * P, (j + 1) * P)
                for k in range(KD):
                    pe.matmul(pv[j][:, D:D + 2], wkT[:, k, cols], bq2[:, k, :], start=False,
                              stop=k == KD - 1, skip_group_check=True)
                for k in range(KD):
                    pe.matmul(pb[:, 2 * j:2 * j + 2], wqT[:, k, cols], bk2[:, k, :], start=j == 0 and k == 0,
                              stop=k == KD - 1, skip_group_check=True)
            for k in range(KD):
                pe.matmul(pr_[:, 0:D], bv_rows[:, k, :], wo[:, k, :], start=k == 0, stop=k == KD - 1,
                          skip_group_check=True)
            for k in range(KD):
                last = pe.matmul(pr_[:, D:D + 2], bq_rows[:, k, :], bk2[:, k, :], start=False,
                                 stop=k == KD - 1, skip_group_check=True)
            last.then_inc(prod, 1)


def gram_view(work, D):
    return work[:, 0:4 * 2 * D].rearrange("p (i n) -> p i n", i=4)


def query_tiles(work, KD):
    return [work[:, (RP + i * KD) * CH:(RP + (i + 1) * KD) * CH].rearrange("p (k t) -> p k t", k=KD) for i in (1, 0)]


def tokenizer(pr, W, ident_r, scratch, work):
    nc, ins, D, KD, NC, ST, NG = pr.nc, pr.ins, pr.D, pr.KD, pr.NC, pr.ST, pr.NG
    assert KD == 2 and NG % RG == 0 and NC % 2 == 0 and pr.B == 2 and RG * GT * CH == 2 * 2 * TPC * D
    PAIRS = NC // 2
    TURN_Y, RECTIFY, MOMENTS, NORM, SPLIT_X = 4, 5, 7, 10, 12
    MN_HI, MN_LO, TURN_MN, KEEP_MN = (max(n, ST * m // 16) for n, m in ((13, 7), (14, 8), (15, 10), (15, 12)))

    with ExitStack() as ctx:
        kt_hi, kt_lo = W["kt"][:, 0], W["kt"][:, 1]
        v_hi, v_lo = (sb(nc, ctx, n, [P, ST, D], F32R) for n in ("v_hi", "v_lo"))
        d_col = sb(nc, ctx, "d_col", [P, ST])
        gate = sb(nc, ctx, "gate", [P, RG, GT, CH])
        p32 = work[:, 0:RP * CH].rearrange("p (i t) -> p i t", i=RP)
        h_sb = work[:, RP * CH:RP * CH + TPC * D].rearrange("p (j d) -> p j d", j=TPC)
        x32 = query_tiles(work, KD)
        x_hi, x_lo = W["x_hi"], W["x_lo"]
        p_hi, p_lo = (sb(nc, ctx, n, [P, 2, CH], F32R) for n in ("p_hi", "p_lo"))
        vf = sb(nc, ctx, "vf", [P, TPC, D + 2])
        turn_hi, turn_lo = (sb(nc, ctx, n, [P, TPC * D], F32R) for n in ("turn_hi", "turn_lo"))
        mn_sb = sb(nc, ctx, "mn_sb", [P, TPC, D])
        mnT_sb = sb(nc, ctx, "mnT_sb", [P, KD, CH])
        stats, mv = sb(nc, ctx, "stats", [P, TPC, 6]), sb(nc, ctx, "mv", [P, TPC, 2])
        spread, rstd, power = (sb(nc, ctx, n, [P, TPC]) for n in ("spread", "rstd", "power"))
        yT_hi, yT_lo = (t[:, :].rearrange("p (m t) -> p m t", m=KD) for t in (turn_hi, turn_lo))
        mn_hi, mn_lo = (t[:, :].rearrange("p (j d) -> p j d", j=TPC) for t in (turn_hi, turn_lo))
        g32 = gate[:, :, :, :].rearrange("p (h b) g t -> p h b (g t)", h=2)
        g_hi, g_lo = (W["kt"][:, :, :, :].rearrange("p i k t -> p (i k t)")[:, i * 4 * TPC * D:(i + 1) * 4 * TPC * D]
                      .rearrange("p (h b n) -> p h b n", h=2, b=2) for i in range(2))
        S, Y, TR = pr.banks[0:2], pr.banks[2:4], pr.banks[4:8]
        KP, VP, G = S, [Y[0], Y[1], TR[0], TR[1]], [S[0], S[1], Y[0], Y[1]]

        pr.last_mnT = mnT_sb[:, :, :]
        (xp_hi, xp_lo, kp, k_evac, k_hi_ok, k_lo_ok, vp, v_evac, v_hi_ok, v_lo_ok, d_ok,
         xm_ld, xm_hi, xm_lo, scores, mul_done, hi_done, lo_done, ret_done, y_hi_ok, y_evac,
         y_turned, neg_ok, h_ok, stats_ok, mv_ok, spread_ok, rstd_ok, z_ok, scaled, mn_ok, hb_ok,
         mn_hi_ok, mn_lo_ok, mn_turned, mnT_ok, st_h, st_mn, st_mnT, power_ok, g_hi_ok, g_lo_ok,
         g_done) = (pr.sem(n) for n in (
            "xp_hi", "xp_lo", "kp", "k_evac", "k_hi_ok", "k_lo_ok", "vp", "v_evac", "v_hi_ok",
            "v_lo_ok", "d_ok", "xm_ld", "xm_hi", "xm_lo", "scores", "mul_done", "hi_done", "lo_done",
            "ret_done", "y_hi_ok", "y_evac", "y_turned", "neg_ok", "h_ok", "stats_ok", "mv_ok", "spread_ok",
            "rstd_ok", "z_ok", "scaled", "mn_ok", "hb_ok", "mn_hi_ok", "mn_lo_ok", "mn_turned", "mnT_ok",
            "st_h", "st_mn", "st_mnT", "power_ok", "g_hi_ok", "g_lo_ok", "g_done"))
        gate_ld = [pr.sem(f"gate_ld{r}") for r in range(RG)]
        xp_ld = [pr.sem(f"xp_ld{h}") for h in range(2)]
        w_lo = pr.sem("w_lo")
        block = pr.block
        END = pr.B * NC

        def chunks(eng, b, step):
            for c in range(2):
                step(c, b * NC + c, c)
            if PAIRS > 2:
                with eng.Fori(1, PAIRS - 1) as p:
                    for h in range(2):
                        step(p * 2 + h, b * NC + p * 2 + h, h)
            for c in range(NC - 2, NC):
                step(c, b * NC + c, c % 2)

        def gram_chunks(eng, step):
            for c in range(2):
                step(c, c)
            if PAIRS > 2:
                with eng.Fori(1, PAIRS - 1) as p:
                    for h in range(2):
                        step(p * 2 + h, h)
            for c in range(NC - 2, NC):
                step(c, c % 2)

        def is_last(c):
            return isinstance(c, int) and c == NC - 1

        def before(b, c):
            return (b - 1, NC - 1) if early(c, 1) else (b, c - 1)

        @block.sync
        def _(sp):
            def load_x(b, c, sem, h=0):
                sp.dma_start(x32[h], ins["xT"][b, c]).then_inc(sem, 16)

            def store(Q, b, c, sem, ready, count, tile, dram):
                sp.wait_ge(ready, (Q + 1) * count)
                sp.dma_start(dram[b, c], tile).then_inc(sem, 16)

            stores = ((max(NG // 2, 6), st_h, hb_ok, TPC, h_sb[:, :, :], scratch["h"]),
                      (max(NG * 5 // 8, 6), st_mn, mn_ok, TPC, mn_sb[:, :, :], scratch["mn"]),
                      (NG - 1, st_mnT, mnT_ok, 2, mnT_sb[:, :, :], scratch["mnT"]))

            def load_gate(c, M, g):
                past(sp, mul_done, M * ST + (g - RG + 1) * GT)
                sp.dma_start(gate[:, g % RG, :, :], ins["gateT"][c, g]).then_inc(gate_ld[g % RG], 16)

            for b in range(pr.B):
                def project(c, J, h):
                    if early(c, 1):
                        past(sp, st_h, (b * NC - 1) * 16)
                        load_x(b, 1, xp_ld[1], 1)
                    sp.wait_ge(xp_lo, J + 1)
                    if isinstance(c, int) and c == NC - 2:
                        load_x(b, 0, xm_ld)
                    elif not is_last(c):
                        load_x(b, c + 2, xp_ld[h], h)
                    if early(c, 1):
                        for g in range(RG):
                            load_gate(0, b * NC, g)

                chunks(sp, b, project)

                def attend(c, M, h):
                    if not (is_last(c) and b == pr.B - 1):
                        sp.wait_ge(xm_lo, M + 1)
                        if is_last(c):
                            load_x(b + 1, 0, xp_ld[0])
                        else:
                            load_x(b, c + 1, xm_ld)
                    for g in range(NG):
                        if not (early(c, 1) and g < RG):
                            load_gate(c, M, g)
                        if not early(M, 1):
                            for at, *what in stores:
                                if g == at:
                                    store(M - 1, *before(b, c), *what)

                chunks(sp, b, attend)

            def load_mn(c, h, last):
                if early(c, 1):
                    sp.wait_ge(mul_done, END * ST - 2 * GT)
                elif early(c, 2):
                    sp.wait_ge(mul_done, END * ST)
                if last:
                    for _, *what in stores[0:2]:
                        store(END - 1, pr.B - 1, NC - 1, *what)
                    sp.wait_ge(st_mn, 16 * END)
                past(sp, g_lo_ok, c - 1)
                for s in range(2):
                    sp.dma_start(gate[:, 2 * h + s, :, :], scratch["mn"][s, c].rearrange("p j d -> p (j d)")).then_inc(
                        gate_ld[2 * h + s], 16)

            sp.wait_ge(st_mn, 16 * (END - 1))
            gram_chunks(sp, lambda c, h: load_mn(c, h, is_last(c)))

        @block.scalar
        def _(act):
            def split_x(half, tile, sem_ld, loads, sem_hi):
                act.wait_ge(sem_ld, loads * 16)
                nc.scalar.activation(x_hi[:, half], x32[tile], ACT.Copy).then_inc(sem_hi, 1)

            def keep_y(Q):
                act.wait_ge(ret_done, (Q + 1) * ST)
                for m in range(KD):
                    nc.scalar.activation(yT_hi[:, m, :], Y[m][:, :], ACT.Identity,
                                         bias=W["bo_col"][:, m:m + 1]).then_inc(y_hi_ok, 1)

            def split_mn(Q):
                act.wait_ge(mn_ok, (Q + 1) * TPC)
                act.wait_ge(y_turned, Q + 1)
                nc.scalar.activation(mn_hi, mn_sb[:, :, :], ACT.Copy).then_inc(mn_hi_ok, 1)

            def keep_mnT(Q):
                past(act, st_mnT, Q * 16)
                act.wait_ge(mn_turned, Q + 1)
                for m in range(KD):
                    nc.scalar.activation(mnT_sb[:, m, :], TR[2 + m][:, :], ACT.Copy).then_inc(mnT_ok, 1)

            for b in range(pr.B):
                def project(c, J, h):
                    if is_last(c):
                        split_x(0, 0, xm_ld, b * NC + 1, xm_hi)
                    else:
                        act.wait_ge(xp_ld[1 - h], (J + 1 - (1 - h)) * 8 + 16)
                        nc.scalar.activation(x_hi[:, 1 - h], x32[1 - h], ACT.Copy).then_inc(xp_hi, 1)
                    for m in range(KD):
                        past(act, k_lo_ok, J * 2 + m - 3)
                        act.wait_ge(kp, J * 2 + m + 1)
                        nc.scalar.activation(p32[:, 2 * h + m, :], KP[m][:, :], ACT.Identity,
                                             bias=W["bk_col"][:, m:m + 1]).then_inc(k_evac, 1)
                    for m in range(KD):
                        act.wait_ge(k_evac, J * 2 + m + 1)
                        nc.scalar.activation(kt_hi[:, m, bass.ds(c * CH, CH)], p32[:, 2 * h + m, :],
                                             ACT.Copy).then_inc(k_hi_ok, 1)
                    for j in range(TPC):
                        act.wait_ge(v_evac, J * TPC + j + 1)
                        nc.scalar.activation(v_hi[:, c * TPC + j, :], vf[:, j, 0:D], ACT.Copy).then_inc(v_hi_ok, 1)

                chunks(act, b, project)

                def attend(c, M, h):
                    for i in range(ST):
                        if i == 1 and not early(c, 1):
                            keep_y(M - 1)
                        act.wait_ge(mul_done, M * ST + i + 1)
                        past(act, ret_done, M * ST + i - 1)
                        nc.scalar.activation(p_hi[:, i % 2, :], p32[:, i % RP, :], ACT.Copy).then_inc(hi_done, 1)
                        if i == SPLIT_X and not is_last(c):
                            split_x(1 - h, 0, xm_ld, M + 2, xm_hi)
                        if not early(M, 1):
                            if i == MN_HI:
                                split_mn(M - 1)
                            if i == KEEP_MN:
                                keep_mnT(M - 1)
                    if is_last(c):
                        if b < pr.B - 1:
                            split_x(0, 0, xp_ld[0], (b + 1) * PAIRS + 1, xp_hi)
                            keep_y(M)

                chunks(act, b, attend)

            def gram(c, h):
                act.wait_ge(gate_ld[2 * h], END * (NG // RG) * 16 + (c - h) * 8 + 16)
                act.wait_ge(gate_ld[2 * h + 1], END * (NG // RG) * 16 + (c - h) * 8 + 16)
                past(act, g_done, c - 1)
                nc.scalar.activation(g_hi[:, h], g32[:, h], ACT.Copy).then_inc(g_hi_ok, 1)
                if early(c, 1):
                    keep_y(END - 1)
                if isinstance(c, int) and c == NC - 2:
                    split_mn(END - 1)
                if is_last(c):
                    keep_mnT(END - 1)

            gram_chunks(act, gram)

        @block.vector
        def _(dve):
            def split_x(half, sem_hi, sem_lo, J, tile=0):
                dve.wait_ge(sem_hi, J + 1)
                nc.vector.tensor_tensor(x_lo[:, half], x32[tile], x_hi[:, half].bitcast(F32),
                                        ALU.subtract).then_inc(sem_lo, 1)

            def keep_y(Q):
                for m in range(KD):
                    dve.wait_ge(y_hi_ok, Q * 2 + m + 1)
                    nc.vector.scalar_tensor_tensor(yT_lo[:, m, :], Y[m][:, :], W["bo_col"][:, m:m + 1],
                                                   yT_hi[:, m, :].bitcast(F32), ALU.add, ALU.subtract).then_inc(y_evac, 1)

            def rectify(Q, part):
                for i in range(2):
                    if part == 0:
                        dve.wait_ge(y_turned, Q + 1)
                        past(dve, st_h, Q * 16)
                        past(dve, st_mn, Q * 16)
                        nc.vector.tensor_scalar(mn_sb[:, 2 * i:2 * i + 2, :], TR[i][:, :], 0.0, W["prelu"][:, 0:1],
                                                ALU.min, ALU.mult).then_inc(neg_ok, 1)
                    else:
                        dve.wait_ge(neg_ok, Q * 2 + i + 1)
                        nc.vector.scalar_tensor_tensor(h_sb[:, 2 * i:2 * i + 2, :], TR[i][:, :], 0.0,
                                                       mn_sb[:, 2 * i:2 * i + 2, :], ALU.max, ALU.add).then_inc(h_ok, 1)

            def moments(Q, part):
                for j in (2 * part, 2 * part + 1):
                    dve.wait_ge(h_ok, Q * 2 + part + 1)
                    nc.vector.bn_stats(stats[:, j, :], h_sb[:, j, :]).then_inc(stats_ok, 1)
                for j in (2 * part, 2 * part + 1):
                    dve.wait_ge(stats_ok, Q * TPC + j + 1)
                    pr.stand_alone(dve)
                    nc.vector.bn_aggr(mv[:, j, :], stats[:, j, :]).then_inc(mv_ok, 1)

            def norm(Q, part):
                dve.wait_ge(rstd_ok, Q + 1)
                for j in (2 * part, 2 * part + 1):
                    nc.vector.tensor_scalar(mn_sb[:, j, :], h_sb[:, j, :], mv[:, j, 0:1], rstd[:, j:j + 1],
                                            ALU.subtract, ALU.mult).then_inc(z_ok, 1)

            def split_mn(Q):
                dve.wait_ge(mn_hi_ok, Q + 1)
                nc.vector.tensor_tensor(mn_lo, mn_sb[:, :, :], mn_hi.bitcast(F32), ALU.subtract).then_inc(mn_lo_ok, 1)

            for b in range(pr.B):
                def project(c, J, h):
                    def low_k(m):
                        dve.wait_ge(k_hi_ok, J * 2 + m + 1)
                        nc.vector.tensor_tensor(kt_lo[:, m, bass.ds(c * CH, CH)], p32[:, 2 * h + m, :],
                                                kt_hi[:, m, bass.ds(c * CH, CH)].bitcast(F32),
                                                ALU.subtract).then_inc(k_lo_ok, 1)

                    if is_last(c):
                        split_x(1 - h, xm_hi, xm_lo, b * NC)
                    else:
                        split_x(1 - h, xp_hi, xp_lo, J + 1, 1 - h)
                    for j in range(TPC):
                        past(dve, v_lo_ok, J * TPC + j - 3)
                        dve.wait_ge(vp, J * TPC + j + 1)
                        nc.vector.tensor_tensor(vf[:, j, :], VP[j][:, 0:D + 2], W["v_bias"][:, :],
                                                ALU.add).then_inc(v_evac, 1)
                        if j < KD:
                            low_k(j)

                chunks(dve, b, project)
                dve.wait_ge(d_ok, (b + 1) * NC * TPC - TPC)
                dve.wait_ge(k_lo_ok, (b + 1) * NC * KD)
                pr.stand_alone(dve)

                def attend(c, M, h):
                    def low(i):
                        dve.wait_ge(hi_done, M * ST + i + 1)
                        nc.vector.tensor_tensor(p_lo[:, i % 2, :], p32[:, i % RP, :], p_hi[:, i % 2, :].bitcast(F32),
                                                ALU.subtract).then_inc(lo_done, 1)

                    for i in range(ST):
                        g, j = i // GT, i % GT
                        if early(c, 1) and i == ST - TPC:
                            dve.wait_ge(d_ok, (b + 1) * NC * TPC)
                        dve.wait_ge(scores, M * ST + i + 1)
                        if j == 0:
                            dve.wait_ge(gate_ld[g % RG], (M * (NG // RG) + g // RG + 1) * 16)
                        past(dve, lo_done, M * ST + i - RP + 1)
                        nc.vector.scalar_tensor_tensor(p32[:, i % RP, :], S[i % 2][:, :], d_col[:, i:i + 1],
                                                       gate[:, g % RG, j, :], ALU.add, ALU.mult).then_inc(mul_done, 1)
                        if i == 0 and not early(c, 1):
                            low(0)
                            keep_y(M - 1)
                        elif i > 1 or i == 1 and early(c, 1):
                            low(i - 1)
                        if i == SPLIT_X + 1 and not is_last(c):
                            split_x(1 - h, xm_hi, xm_lo, M + 1)
                        if not early(M, 1):
                            for at, what in ((RECTIFY, rectify), (MOMENTS, moments), (NORM, norm)):
                                if i in (at, at + 1):
                                    what(M - 1, i - at)
                            if i == MN_LO:
                                split_mn(M - 1)
                    low(ST - 1)
                    if is_last(c):
                        if b < pr.B - 1:
                            split_x(0, xp_hi, xp_lo, (b + 1) * NC)
                            keep_y(M)

                chunks(dve, b, attend)

            def gram(c, h):
                dve.wait_ge(g_hi_ok, c + 1)
                nc.vector.tensor_tensor(g_lo[:, h], g32[:, h], g_hi[:, h].bitcast(F32), ALU.subtract).then_inc(g_lo_ok, 1)
                if early(c, 1):
                    keep_y(END - 1)
                    for what in (rectify, moments):
                        for part in range(2):
                            what(END - 1, part)
                elif early(c, 2):
                    for part in range(2):
                        norm(END - 1, part)
                if isinstance(c, int) and c == NC - 2:
                    split_mn(END - 1)

            gram_chunks(dve, gram)
        @block.gpsimd
        def _(pool):
            nc.gpsimd.memset(power[:, :], -0.5).then_inc(power_ok, 1)

            def scale(Q):
                pool.wait_ge(mv_ok, (Q + 1) * TPC)
                pr.stand_alone(pool)
                nc.gpsimd.tensor_scalar(spread[:, :], mv[:, :, 1], 1.0 + EPS, EPS * EPS, ALU.mult,
                                        ALU.add).then_inc(spread_ok, 1)
                pool.wait_ge(spread_ok, Q + 1)
                pool.wait_ge(power_ok, 1)
                nc.gpsimd.tensor_tensor(rstd[:, :], spread[:, :], power[:, :], ALU.pow).then_inc(rstd_ok, 1)
                pool.wait_ge(z_ok, (Q + 1) * TPC)
                for j in range(TPC):
                    nc.gpsimd.tensor_tensor(mn_sb[:, j, :], mn_sb[:, j, :], W["gamma"][:, :],
                                            ALU.mult).then_inc(scaled, 1)
                for j in range(TPC):
                    pool.wait_ge(scaled, Q * TPC + j + 1)
                    nc.gpsimd.tensor_tensor(mn_sb[:, j, :], mn_sb[:, j, :], W["beta"][:, :], ALU.add).then_inc(mn_ok, 1)
                for j in range(TPC):
                    nc.gpsimd.tensor_tensor(h_sb[:, j, :], h_sb[:, j, :], W["attn_bo"][:, :], ALU.add).then_inc(hb_ok, 1)

            for b in range(pr.B):
                def project(c, J, h):
                    for j in range(TPC):
                        pool.wait_ge(v_evac, J * TPC + j + 1)
                        pr.stand_alone(pool)
                        nc.gpsimd.tensor_copy(d_col[:, bass.ds(c * TPC + j, 1)], vf[:, j, D:D + 1]).then_inc(d_ok, 1)
                        pool.wait_ge(v_hi_ok, J * TPC + j + 1)
                        nc.gpsimd.tensor_tensor(v_lo[:, c * TPC + j, :], vf[:, j, 0:D],
                                                v_hi[:, c * TPC + j, :].bitcast(F32), ALU.subtract).then_inc(v_lo_ok, 1)

                chunks(pool, b, project)

                def attend(c, M, h):
                    if not early(M, 1):
                        scale(M - 1)

                chunks(pool, b, attend)
            scale(END - 1)

        @block.tensor
        def _(pe):
            def turn(out, hi, lo):
                pe.matmul(out, hi, ident_r[:, :], start=True, stop=False)
                return pe.matmul(out, lo, ident_r[:, :], start=False, stop=True)

            def turn_y(Q):
                pe.wait_ge(y_evac, (Q + 1) * 2)
                for j in range(TPC):
                    for m in range(KD):
                        t = slice(j * P, (j + 1) * P)
                        last = turn(TR[j // 2][:, (j % 2) * D + m * P:(j % 2) * D + (m + 1) * P],
                                    yT_hi[:, m, t], yT_lo[:, m, t])
                last.then_inc(y_turned, 1)

            def turn_mn(Q):
                past(pe, mnT_ok, Q * 2)
                pe.wait_ge(mn_lo_ok, Q + 1)
                for m in range(KD):
                    for j in range(TPC):
                        d = slice(m * P, (m + 1) * P)
                        last = turn(TR[2 + m][:, j * P:(j + 1) * P], mn_hi[:, j, d], mn_lo[:, j, d])
                last.then_inc(mn_turned, 1)

            pe.wait_ge(w_lo, 1)
            for b in range(pr.B):
                def project(c, J, h):
                    pe.wait_ge(xp_lo, J + 1)
                    for m in range(KD):
                        past(pe, k_evac, J * 2 + m - 1)
                        cols = slice(m * P, (m + 1) * P)
                        n = 0
                        for k in range(KD):
                            for w, x in split_products(W["a_hi"][:, k, cols], W["a_lo"][:, k, cols],
                                                       x_hi[:, h, k, :], x_lo[:, h, k, :]):
                                n += 1
                                mm = pe.matmul(KP[m][:, :], w, x, start=n == 1, stop=n == 3 * KD)
                        mm.then_inc(kp, 1)
                    if early(c, 1):
                        pe.wait_ge(w_lo, 2)
                        past(pe, y_evac, b * NC * 2)
                    for j in range(TPC):
                        past(pe, v_evac, J * TPC + j - 3)
                        rows = slice(j * P, (j + 1) * P)
                        n = 0
                        for k in range(KD):
                            for x, w in split_products(x_hi[:, h, k, rows], x_lo[:, h, k, rows],
                                                       W["vo_hi"][:, k, :], W["vo_lo"][:, k, :]):
                                n += 1
                                mm = pe.matmul(VP[j][:, 0:D + 2], x, w, start=n == 1, stop=n == 3 * KD)
                        mm.then_inc(vp, 1)

                chunks(pe, b, project)
                pe.wait_ge(k_lo_ok, (b + 1) * NC * 2 - 2)
                pe.wait_ge(k_evac, (b + 1) * NC * 2)

                def retain(M, i):
                    if i == 0:
                        past(pe, y_evac, M * 2)
                    pe.wait_ge(lo_done, M * ST + i + 1)
                    for m in range(KD):
                        cols = slice(m * P, (m + 1) * P)
                        for n, (v, p) in enumerate(split_products(v_hi[:, i, cols], v_lo[:, i, cols],
                                                                  p_hi[:, i % 2, :], p_lo[:, i % 2, :])):
                            mm = pe.matmul(Y[m][:, :], v, p, start=i == 0 and n == 0, stop=i == ST - 1 and n == 2)
                    mm.then_inc(ret_done, 1)

                def attend(c, M, h):
                    pe.wait_ge(xm_lo, M + 1)
                    for i in range(ST):
                        if early(c, 1) and i == ST - TPC:
                            pe.wait_ge(k_lo_ok, (b + 1) * NC * 2)
                        past(pe, mul_done, M * ST + i - 1)
                        rows = slice(i * P, (i + 1) * P)
                        n = 0
                        for k in range(KD):
                            for w, x in split_products(kt_hi[:, k, rows], kt_lo[:, k, rows],
                                                       x_hi[:, h, k, :], x_lo[:, h, k, :]):
                                n += 1
                                mm = pe.matmul(S[i % 2][:, :], w, x, start=n == 1, stop=n == 3 * KD)
                        mm.then_inc(scores, 1)
                        if early(c, 1) and i == 2:
                            pe.wait_ge(v_lo_ok, (b + 1) * NC * TPC)
                        if i >= 2:
                            retain(M, i - 2)
                        elif i == 0 and not early(c, 1):
                            for back in (2, 1):
                                retain(M - 1, ST - back)
                        if not early(M, 1):
                            if i == TURN_Y:
                                turn_y(M - 1)
                            if i == TURN_MN:
                                turn_mn(M - 1)
                    if is_last(c):
                        for back in (2, 1):
                            retain(M, ST - back)

                chunks(pe, b, attend)

            def gram(c, h):
                if is_last(c):
                    turn_mn(END - 1)
                pe.wait_ge(g_lo_ok, c + 1)
                for j in range(TPC):
                    for i in range(4):
                        s, m = i // 2, i % 2
                        if early(c, 1) and j == 0 and i == 2:
                            pe.wait_ge(y_evac, END * 2)
                        cols = slice(j * D + m * P, j * D + (m + 1) * P)
                        tile = slice(j * D, (j + 1) * D)
                        out = G[i][:, 0:2 * D] if s == 0 else G[i][:, 0:D]
                        for n, (w, x) in enumerate(split_products(
                                g_hi[:, h, s, cols], g_lo[:, h, s, cols],
                                g_hi[:, h, s:2, tile], g_lo[:, h, s:2, tile])):
                            mm = pe.matmul(out, w, x, start=early(c, 1) and j == 0 and n == 0,
                                           stop=False, skip_group_check=True)
                    if early(c, 1) and j == 0:
                        turn_y(END - 1)
                mm.then_inc(g_done, 1)

            gram_chunks(pe, gram)


def start_mix(pr, W2, heads_in, M, scratch, last_mnT):
    nc, ins, D, KD, END = pr.nc, pr.ins, pr.D, pr.KD, pr.B * pr.NC
    (ld, made, whi, wlo, m_ld, hi_ok, lo_ok, vv, gg) = (pr.sem(n) for n in (
        "hw_ld", "hw_made", "hw_hi", "hw_lo", "mx_m_ld", "mx_hi_ok", "mx_lo_ok", "mx_vv", "mx_gg"))
    head = D // pr.H
    block = pr.block

    @block.sync
    def _(sp):
        sp.wait_ge(pr.sem("ret_done"), END * pr.ST)
        for x in "vg":
            sp.dma_start(heads_in[x][:, :, :], ins[f"attn_W{x}"].rearrange("(k p) n -> p k n", p=P)).then_inc(ld, 16)
        for b in range(2):
            sp.dma_start(M["m32"][:, b], scratch["mnT"][b, 0]).then_inc(m_ld, 16)
        for x in "okq":
            sp.dma_start(heads_in[x][:, :, :], ins[f"attn_W{x}"].rearrange("(k p) n -> p k n", p=P)).then_inc(ld, 16)
        with nc.allow_non_contiguous_dma(reason="a bias column, once"):
            sp.dma_start(W2["bg_col"][:, :], ins["attn_bg"].rearrange("(k p) -> p k", p=P)).then_inc(ld, 16)
        sp.dma_start(W2["wr"][:, :], ins["ffn_wr"].partition_broadcast(P)).then_inc(ld, 16)
        sp.dma_start(W2["br"][:, :], ins["ffn_br"].partition_broadcast(P)).then_inc(ld, 16)
        sp.wait_ge(pr.sem("mnT_ok"), END * 2)
        sp.dma_start(scratch["mnT"][pr.B - 1, pr.NC - 1], last_mnT).then_inc(pr.sem("st_mnT"), 16)
        for n in ("st_h", "st_mn", "st_mnT"):
            sp.wait_ge(pr.sem(n), 16 * END)

    @block.gpsimd
    def _(pool):
        pool.wait_ge(pr.sem("ret_done"), END * pr.ST)
        nc.gpsimd.memset(heads_in["same_head"][:, :], 0.0).then_inc(made, 1)
        nc.gpsimd.memset(heads_in["ones"][:, :], 1.0).then_inc(made, 1)
        pool.wait_ge(made, 2)
        for h in range(P // head):
            r = slice(h * head, (h + 1) * head)
            nc.gpsimd.memset(heads_in["same_head"][r, r], 1.0).then_inc(made, 1)
        pool.wait_ge(made, 2 + P // head)
        pool.wait_ge(hi_ok, 1)
        nc.gpsimd.tensor_tensor(M["m_lo"][:, 0], M["m32"], M["m_hi"][:, 0].bitcast(F32), ALU.subtract).then_inc(lo_ok, 1)

    @block.scalar
    def _(act):
        act.wait_ge(m_ld, 32)
        nc.scalar.activation(M["m_hi"][:, 0], M["m32"], ACT.Copy).then_inc(hi_ok, 1)
        act.wait_ge(ld, 16 * 8)
        for x in "vgo":
            nc.scalar.activation(W2[x + "_hi"][:, :, :], heads_in[x][:, :, :], ACT.Copy).then_inc(whi, 1)

    @block.vector
    def _(dve):
        for n, x in enumerate("vgo"):
            dve.wait_ge(whi, n + 1)
            nc.vector.tensor_tensor(W2[x + "_lo"][:, :, :], heads_in[x][:, :, :], W2[x + "_hi"][:, :, :].bitcast(F32),
                                    ALU.subtract).then_inc(wlo, 1)

    @block.tensor
    def _(pe):
        pe.wait_ge(lo_ok, 1)
        pe.wait_ge(wlo, 2)
        pe.wait_ge(pr.sem("h_ok"), END * 2)
        pe.wait_ge(pr.sem("mnT_ok"), END * 2)
        values_and_gates(pr, pe, W2, M, 0, 0)


def values_and_gates(pr, pe, W2, M, h, j, gates_free=()):
    cols = slice(j * P, (j + 1) * P)
    vv, gg = pr.sem("mx_vv"), pr.sem("mx_gg")
    for w, bank, sem, b in (("v", M["V"][1], vv, 1), ("v", M["V"][0], vv, 0), ("g", M["GB"][0], gg, 0),
                            ("g", M["GB"][1], gg, 1)):
        if w == "g" and gates_free:
            past(pe, pr.sem("mx_g_ok"), gates_free[b])
        i = 0
        for k in range(pr.KD):
            for ww, x in split_products(W2[w + "_hi"][:, k, cols], W2[w + "_lo"][:, k, cols],
                                        M["m_hi"][:, h, b, k, :], M["m_lo"][:, h, b, k, :]):
                i += 1
                mm = pe.matmul(bank[:, :], ww, x, start=i == 1, stop=i == 3 * pr.KD)
        mm.then_inc(sem, 1)


def head_weights(pr, W2, heads_in, grams, banks):
    nc, D, KD, B = pr.nc, pr.D, pr.KD, pr.B
    head = D // pr.H
    scale = head ** -0.5 * pr.T ** -0.5
    wq, wk, prod, cols, att = (heads_in[n] for n in ("q", "k", "prod", "cols", "att"))
    top, shifted, expd, total, inv = (heads_in[n] for n in ("top", "shifted", "expd", "total", "inv"))
    TP = [b[:, :].rearrange("p (m n) -> p m n", m=KD) for b in banks[0:3]]
    colp, attp = banks[3][:, 0:16], banks[3][:, 64:80]
    ld, made, kept, tp, prod_ok, col_ok, cols_sb, att_ok, step, exp_ok = (pr.sem(n) for n in (
        "hw_ld", "hw_made", "hw_kept", "hw_tp", "hw_prod", "hw_col", "hw_cols", "hw_att", "hw_step", "hw_exp"))
    block = pr.block

    @block.tensor
    def _(pe):
        pe.wait_ge(kept, 4)
        for i, (g0, c0, w) in enumerate(((0, 0, wk), (0, D, wq), (0, D, wk), (2, 0, wk))):
            if i == 3:
                pe.wait_ge(prod_ok, 1)
            for m in range(KD):
                for k in range(KD):
                    mm = pe.matmul(TP[i % 3][:, m, :], grams[:, g0 + k, c0 + m * P:c0 + (m + 1) * P], w[:, k, :],
                                   start=m == 0 and k == 0, stop=k == KD - 1, skip_group_check=True)
            mm.then_inc(tp, 1)
        pe.wait_ge(made, 2 + P // head)
        for i in range(4):
            pe.wait_ge(prod_ok, i + 1)
            for j in range(KD):
                for m in range(KD):
                    at = 4 * i + 2 * j
                    mm = pe.matmul(colp[:, at:at + 2], prod[:, i, m, j * P:(j + 1) * P], heads_in["ones"][:, :],
                                   start=i == 0 and j == 0 and m == 0, stop=m == KD - 1, skip_group_check=True)
        mm.then_inc(col_ok, 1)
        pe.wait_ge(cols_sb, 1)
        pe.matmul(attp, heads_in["same_head"][:, :], cols[:, :], start=True, stop=True).then_inc(att_ok, 1)

    @block.vector
    def _(dve):
        dve.wait_ge(pr.sem("g_done"), pr.NC)
        for i in range(4):
            n = 2 * D if i < 2 else D
            nc.vector.tensor_copy(grams[:, i, 0:n], banks[i][:, 0:n]).then_inc(kept, 1)
        dve.wait_ge(ld, 16 * 8)
        for i, w in enumerate((wq, wk, wq, wq)):
            dve.wait_ge(tp, i + 1)
            nc.vector.tensor_tensor(prod[:, i], TP[i % 3][:, :, :], w[:, :, :], ALU.mult).then_inc(prod_ok, 1)
        dve.wait_ge(col_ok, 1)
        nc.vector.tensor_copy(cols[:, :], colp).then_inc(cols_sb, 1)
        dve.wait_ge(att_ok, 1)
        nc.vector.tensor_copy(att[:, :, :, :], banks[3][:, 64:80:2].rearrange("p (s t j) -> p s t j", s=2, t=2)).then_inc(step, 1)
        dve.wait_ge(step, 1)
        nc.vector.tensor_tensor(top[:, :, :], att[:, :, 0, :], att[:, :, 1, :], ALU.max).then_inc(step, 1)
        dve.wait_ge(step, 2)
        for t in range(2):
            nc.vector.tensor_tensor(shifted[:, :, t, :], att[:, :, t, :], top[:, :, :], ALU.subtract).then_inc(step, 1)
        dve.wait_ge(exp_ok, 1)
        nc.vector.tensor_tensor(total[:, :, :], expd[:, :, 0, :], expd[:, :, 1, :], ALU.add).then_inc(step, 1)
        dve.wait_ge(step, 5)
        nc.vector.reciprocal(inv[:, :, :], total[:, :, :]).then_inc(step, 1)
        dve.wait_ge(step, 6)
        for t in range(2):
            nc.vector.tensor_tensor(W2["att"][:, :, t, :], expd[:, :, t, :], inv[:, :, :], ALU.mult).then_inc(step, 1)
        dve.wait_ge(step, 8)

    @block.scalar
    def _(act):
        act.wait_ge(step, 4)
        nc.scalar.activation(expd[:, :, :, :], shifted[:, :, :, :], ACT.Exp, scale=scale).then_inc(exp_ok, 1)


def mix(pr, W2, M, OP, ahead, late, scratch, base, router, mlp_raw, W3):
    nc, ins, D, KD, NC = pr.nc, pr.ins, pr.D, pr.KD, pr.NC
    with ExitStack() as ctx:
        m32, m_hi, m_lo, V, GB = (M[n] for n in ("m32", "m_hi", "m_lo", "V", "GB"))
        og_hi, og_lo = (sb(nc, ctx, n, [P, 2, 2, KD, CH], F32R) for n in ("og_hi", "og_lo"))
        h_in = sb(nc, ctx, "h_in", [P, 2, 2, TPC, D])
        x_first = ahead.x_first = h_in[:, 0, 0]
        xn = sb(nc, ctx, "xn", [P, 2, 2, TPC, D])
        t1, o32, g_sb, og32 = (late[:, i * 2 * CH:(i + 1) * 2 * CH].rearrange("p (i t) -> p i t", i=2)
                               for i in range(4))
        stats, mv = sb(nc, ctx, "stats2", [P, 2, TPC, 6]), sb(nc, ctx, "mv2", [P, 2, TPC, 2])
        spread, rstd, power, shift = (sb(nc, ctx, n, [P, 2, TPC]) for n in ("spread2", "rstd2", "power2", "shift2"))
        scrap, w_now = sb(nc, ctx, "scrap", [P, D]), sb(nc, ctx, "w_now", [P, 2, TPC])
        (m_ld, hi_ok, lo_ok, vv, gg, t_ok, g_ok, o_ok, og_ok, ogh_ok, ogl_ok, op, h2_ok, st_ok, mv_ok,
         sp_ok, rs_ok, rs2_ok, sh_ok, xn_ok, w_ok, w_kept, power_ok, raw_ld) = (pr.sem("mx_" + n) for n in (
            "m_ld", "hi_ok", "lo_ok", "vv", "gg", "t_ok", "g_ok", "o_ok", "og_ok", "ogh_ok", "ogl_ok", "op",
            "h2_ok", "st_ok", "mv_ok", "sp_ok", "rs_ok", "rs2_ok", "sh_ok", "xn_ok", "w_ok", "w_kept", "power_ok", "raw_ld"))
        xn_ok = [xn_ok, pr.sem("mx_xn_ok1")]
        h_ld = [pr.sem(f"mx_h_ld{h}") for h in range(2)]
        st_x = [[pr.sem(f"mx_st_x{s}{h}") for h in range(2)] for s in range(2)]
        block = pr.block

        def chunks(eng, step):
            for c in range(2):
                step(c, c)
            if NC > 4:
                with eng.Fori(1, NC // 2 - 1) as p:
                    for h in range(2):
                        step(p * 2 + h, h)
            for c in range(NC - 2, NC + 2):
                step(c, c % 2)

        def within(c, back=0):
            return not isinstance(c, int) or 0 <= c - back < NC

        @block.sync
        def _(sp):
            def load_m(c):
                for b in range(2):
                    sp.dma_start(m32[:, b], scratch["mnT"][b, c]).then_inc(m_ld, 16)

            def store(c, h, s):
                sp.wait_ge(xn_ok[s], (c + 1) * TPC)
                sp.dma_start(scratch["xn"][s, c], xn[:, h, s]).then_inc(st_x[s][h], 16)

            def step(c, h):
                if within(c, -1):
                    sp.wait_ge(lo_ok, c + 1)
                    load_m(c + 1)
                if isinstance(c, int) and c == NC - 1:
                    sp.wait_ge(h2_ok, 4 * (NC - 2) + 2)
                    sp.dma_start(x_first, scratch["xn"][0, 0]).then_inc(pr.sem("ff_x_ld"), 16)
                if within(c):
                    past(sp, h2_ok, c * 4 - 4)
                    for s in range(2):
                        sp.dma_start(h_in[:, h, s], scratch["h"][s, c]).then_inc(h_ld[h], 16)
                if within(c, 2) and not (isinstance(c, int) and c == NC + 1):
                    store(c - 2, h, 1)
                if within(c, 1) and within(c):
                    store(c - 1, 1 - h, 0)

            for s in range(2):
                for h in range(2):
                    sp.sem_inc(st_x[s][h], 1)
            sp.wait_ge(pr.sem("hw_tp"), 4)
            sp.dma_start(mlp_raw["w1"], ins["ffn_w1"].rearrange("(k p) n -> p k n", p=P)).then_inc(raw_ld, 16)
            sp.dma_start(mlp_raw["w2"], ins["ffn_w2"].rearrange("(k p) n -> p k n", p=P)).then_inc(raw_ld, 16)
            with nc.allow_non_contiguous_dma(reason="a bias column, once"):
                sp.dma_start(W3["b1"][:, :], ins["ffn_b1"].rearrange("(k p) -> p k", p=P)).then_inc(raw_ld, 16)
            chunks(sp, step)
            def store_last(s):
                store(NC - 1, 1, s)

            ahead.store_last = store_last

        @block.scalar
        def _(act):
            def split(c, h):
                act.wait_ge(m_ld, (c + 1) * 32)
                nc.scalar.activation(m_hi[:, h], m32[:, :, :, :], ACT.Copy).then_inc(hi_ok, 1)

            def norm(c, h, s):
                past(act, st_x[s][h], (c - h) * 8 + 1)
                act.wait_ge(sh_ok, c * 2 + s + 1)
                for j in range(TPC):
                    nc.scalar.activation(xn[:, h, s, j, :], base[:, s, c * TPC + j, :], ACT.Identity,
                                         bias=shift[:, s, j:j + 1], scale=rstd[:, s, j:j + 1]).then_inc(xn_ok[s], 1)

            def blend(c, j):
                n = c * 4 + 2 * j
                act.wait_ge(vv, n + 2)
                past(act, o_ok, n)
                for s in range(2):
                    nc.scalar.activation(t1[:, s, :], V[1][:, :], ACT.Copy,
                                         scale=W2["att"][:, s, 1, j:j + 1]).then_inc(t_ok, 1)
                past(act, og_ok, n)
                for s in range(2):
                    act.wait_ge(gg, n + s + 1)
                    nc.scalar.activation(g_sb[:, s, :], GB[s][:, :], ACT.Sigmoid,
                                         bias=W2["bg_col"][:, j:j + 1]).then_inc(g_ok, 1)

            def high(c, h, j):
                past(act, op, (c - 1) * 4)
                for s in range(2):
                    act.wait_ge(og_ok, c * 4 + 2 * j + s + 1)
                    nc.scalar.activation(og_hi[:, h, s, j, :], og32[:, s, :], ACT.Copy).then_inc(ogh_ok, 1)

            def step(c, h):
                if within(c):
                    blend(c, 0)
                if within(c, -1):
                    split(c + 1, 1 - h)
                if within(c):
                    high(c, h, 0)
                if isinstance(c, int) and c == NC:
                    ahead.act_split(x_first)
                    act.wait_ge(raw_ld, 48)
                    for x in ("w1", "w2"):
                        nc.scalar.activation(W3[x + "_hi"], mlp_raw[x], ACT.Copy).then_inc(pr.sem("mw_hi"), 1)
                    norm(NC - 2, 0, 1)
                    act.wait_ge(ogl_ok, 4 * NC)
                    ahead.act_split_turned()
                if within(c, 2) and within(c):
                    norm(c - 2, h, 1)
                if within(c):
                    blend(c, 1)
                if within(c, 1) and within(c):
                    norm(c - 1, 1 - h, 0)
                if within(c):
                    high(c, h, 1)

            def norm_last(s):
                norm(NC - 1, 1, s)

            ahead.norm_last = norm_last
            for n in ("st_mn", "st_mnT"):
                act.wait_ge(pr.sem(n), 16 * pr.B * NC)
            act.wait_ge(pr.sem("hw_step"), 8)
            chunks(act, step)

        @block.vector
        def _(dve):
            def mixed(c, j):
                for s in range(2):
                    n = c * 4 + 2 * j + s
                    past(dve, og_ok, n - 1)
                    dve.wait_ge(t_ok, n + 1)
                    nc.vector.scalar_tensor_tensor(o32[:, s, :], V[0][:, :], W2["att"][:, s, 0, j:j + 1], t1[:, s, :],
                                                   ALU.mult, ALU.add).then_inc(o_ok, 1)

            def low(c, h, j):
                for s in range(2):
                    dve.wait_ge(ogh_ok, c * 4 + 2 * j + s + 1)
                    nc.vector.tensor_tensor(og_lo[:, h, s, j, :], og32[:, s, :], og_hi[:, h, s, j, :].bitcast(F32),
                                            ALU.subtract).then_inc(ogl_ok, 1)

            def moments(c, h, s):
                dve.wait_ge(h_ld[h], (c - h) * 16 + 32)
                past(dve, xn_ok[s], c * TPC)
                for i in range(2):
                    dve.wait_ge(op, c * 4 + 2 * s + i + 1)
                    nc.vector.tensor_tensor(base[:, s, bass.ds(c * TPC + 2 * i, 2), :], OP[s][i][:, :],
                                            h_in[:, h, s, 2 * i:2 * i + 2, :], ALU.add).then_inc(h2_ok, 1)
                for j in range(TPC):
                    dve.wait_ge(h2_ok, c * 4 + 2 * s + j // 2 + 1)
                    pr.stand_alone(dve)
                    nc.vector.bn_stats(stats[:, s, j, :], base[:, s, c * TPC + j, :]).then_inc(st_ok, 1)
                for j in range(TPC):
                    dve.wait_ge(st_ok, c * 8 + 4 * s + j + 1)
                    pr.stand_alone(dve)
                    nc.vector.bn_aggr(mv[:, s, j, :], stats[:, s, j, :]).then_inc(mv_ok, 1)

            def route(c, h, s):
                past(dve, w_kept, c + 1)
                dve.wait_ge(xn_ok[s], (c + 1) * TPC)
                for j in range(TPC):
                    past(dve, w_ok, c * 8 + 4 * s + j)
                    nc.vector.tensor_tensor_reduce(out=scrap[:, :], in0=xn[:, h, s, j, :], in1=W2["wr"][:, :],
                                                   scale=1.0, scalar=0.0, op0=ALU.mult, op1=ALU.add,
                                                   accum_out=w_now[:, s, j:j + 1]).then_inc(w_ok, 1)
                if s == 1:
                    dve.wait_ge(w_ok, (c + 1) * 8)
                    nc.vector.tensor_copy(router[:, :, bass.ds(c * TPC, TPC)], w_now[:, :, :]).then_inc(w_kept, 1)

            def step(c, h):
                if within(c, 2):
                    moments(c - 2, h, 1)
                if within(c, 1):
                    low(c - 1, 1 - h, 1)
                if within(c):
                    mixed(c, 0)
                if within(c, 2) and within(c):
                    route(c - 2, h, 0)
                if isinstance(c, int) and c == NC:
                    ahead.dve_split(x_first)
                    dve.wait_ge(pr.sem("mw_hi"), 1)
                    nc.vector.tensor_tensor(W3["w1_lo"], mlp_raw["w1"], W3["w1_hi"].bitcast(F32),
                                            ALU.subtract).then_inc(pr.sem("mw_lo1"), 1)
                if within(c, 1):
                    moments(c - 1, 1 - h, 0)
                if within(c):
                    low(c, h, 0)
                if isinstance(c, int) and c == NC:
                    ahead.dve_split_turned()
                if within(c):
                    mixed(c, 1)
                if within(c, 2) and within(c):
                    route(c - 2, h, 1)

            for n in ("st_mn", "st_mnT"):
                dve.wait_ge(pr.sem(n), 16 * pr.B * NC)
            dve.sem_inc(w_kept, 1)
            chunks(dve, step)
            def route_last(i):
                route(NC - 2 + i // 2, i // 2, i % 2)

            ahead.route_last = route_last

        @block.gpsimd
        def _(pool):
            pool.wait_ge(pr.sem("hw_step"), 8)
            for n in ("st_mn", "st_mnT"):
                pool.wait_ge(pr.sem(n), 16 * pr.B * NC)
            made = pr.sem("mw_made")
            nc.gpsimd.memset(power[:, :, :], -0.5).then_inc(power_ok, 1)
            nc.gpsimd.memset(W3["ones"][:, :], 1.0).then_inc(made, 1)
            pool.wait_ge(made, 1)
            nc.gpsimd.affine_select(out=W3["before"][:, :], in_=W3["ones"][:, :], compare_op=ALU.is_gt, fill=0.0,
                                    base=0, pattern=[[1, P]], channel_multiplier=-1).then_inc(made, 1)
            nc.gpsimd.iota(W3["index"][:, :], pattern=[[1, PIV]], base=1, channel_multiplier=0).then_inc(made, 1)
            pool.wait_ge(made, 3)
            nc.gpsimd.tensor_copy(W3["digit"][:, :], W3["index"][:, :]).then_inc(made, 1)

            def split(c, h):
                pool.wait_ge(hi_ok, c + 1)
                nc.gpsimd.tensor_tensor(m_lo[:, h], m32[:, :, :, :], m_hi[:, h].bitcast(F32), ALU.subtract).then_inc(lo_ok, 1)

            def gated(c, j):
                for s in range(2):
                    n = c * 4 + 2 * j + s
                    past(pool, ogl_ok, n - 1)
                    pool.wait_ge(o_ok, n + 1)
                    pool.wait_ge(g_ok, n + 1)
                    nc.gpsimd.tensor_tensor(og32[:, s, :], o32[:, s, :], g_sb[:, s, :], ALU.mult).then_inc(og_ok, 1)

            def scale(c, s):
                pool.wait_ge(mv_ok, c * 8 + 4 * s + 4)
                pr.stand_alone(pool)
                nc.gpsimd.tensor_scalar(spread[:, s, :], mv[:, s, :, 1], EPS, None, ALU.add).then_inc(sp_ok, 1)
                pool.wait_ge(power_ok, 1)
                pool.wait_ge(sp_ok, c * 2 + s + 1)
                nc.gpsimd.tensor_tensor(rstd[:, s, :], spread[:, s, :], power[:, s, :], ALU.pow).then_inc(rs_ok, 1)
                pool.wait_ge(rs_ok, c * 2 + s + 1)
                nc.gpsimd.tensor_tensor(shift[:, s, :], mv[:, s, :, 0], rstd[:, s, :], ALU.mult).then_inc(rs2_ok, 1)
                pool.wait_ge(rs2_ok, c * 2 + s + 1)
                pr.stand_alone(pool)
                nc.gpsimd.tensor_scalar(shift[:, s, :], shift[:, s, :], -1.0, None, ALU.mult).then_inc(sh_ok, 1)

            def step(c, h):
                if within(c, 2):
                    scale(c - 2, 1)
                if within(c):
                    gated(c, 0)
                if within(c, -1):
                    split(c + 1, 1 - h)
                if isinstance(c, int) and c == NC:
                    pool.wait_ge(pr.sem("mw_hi"), 2)
                    nc.gpsimd.tensor_tensor(W3["w2_lo"], mlp_raw["w2"], W3["w2_hi"].bitcast(F32),
                                            ALU.subtract).then_inc(pr.sem("mw_lo2"), 1)
                if within(c, 1):
                    scale(c - 1, 0)
                if within(c):
                    gated(c, 1)

            chunks(pool, step)

        @block.tensor
        def _(pe):
            def project(c, h, s):
                pe.wait_ge(ogl_ok, c * 4 + 3 + s)
                past(pe, h2_ok, c * 4 + 2 * s - 2)
                for i in range(2):
                    for j in (2 * i, 2 * i + 1):
                        rows = slice(j * P, (j + 1) * P)
                        n = 0
                        for k in range(KD):
                            for x, w in split_products(og_hi[:, h, s, k, rows], og_lo[:, h, s, k, rows],
                                                       W2["o_hi"][:, k, :], W2["o_lo"][:, k, :]):
                                mm = pe.matmul(OP[s][i][:, (j % 2) * D:(j % 2 + 1) * D], x, w,
                                               start=j % 2 == 0 and n == 0, stop=n == 5, skip_group_check=True)
                                n += 1
                    mm.then_inc(op, 1)

            def step(c, h):
                if within(c) and not early(c, 1):
                    pe.wait_ge(lo_ok, c + 1)
                    past(pe, o_ok, c * 4)
                    values_and_gates(pr, pe, W2, M, h, 0, (c * 4 - 1, c * 4))
                if within(c, 1):
                    project(c - 1, 1 - h, 0)
                if within(c):
                    pe.wait_ge(o_ok, c * 4 + 2)
                    values_and_gates(pr, pe, W2, M, h, 1, (c * 4 + 1, c * 4 + 2))
                if within(c, 1):
                    project(c - 1, 1 - h, 1)

            chunks(pe, step)
            pe.wait_ge(g_ok, 4 * NC)
            ahead.pe_turn()


STEPS = 4
PIV = 15
SEARCH = 5


class AheadOfMLP:

    def __init__(self, pr, ident_r, s_hi, s_lo, x_hi, x_lo, TR):
        self.pr, self.ident_r, self.s_hi, self.s_lo, self.TR = pr, ident_r, s_hi, s_lo, TR
        self.x_hi, self.x_lo = [x_hi], [x_lo]
        (self.x_ld, self.shi_ok, self.slo_ok, self.turned, self.hi_ok, self.lo_ok) = (pr.sem("ff_" + n) for n in (
            "x_ld", "shi_ok", "slo_ok", "turned", "hi_ok", "lo_ok"))

    def act_split(self, x32, u=0):
        pr, act = self.pr, self.pr.nc.scalar
        past(act, self.turned, u)
        if early(u, 1):
            act.wait_ge(pr.sem("mx_lo_ok"), pr.NC)
        act.wait_ge(self.x_ld, (u + 1) * 16)
        act.activation(self.s_hi, x32, ACT.Copy).then_inc(self.shi_ok, 1)

    def dve_split(self, x32, u=0):
        dve = self.pr.nc.vector
        dve.wait_ge(self.shi_ok, u + 1)
        dve.tensor_tensor(self.s_lo, x32, self.s_hi.bitcast(F32), ALU.subtract).then_inc(self.slo_ok, 1)

    def pe_turn(self, u=0):
        pe, KD = self.pr.nc.tensor, self.pr.KD
        past(pe, self.lo_ok, u * KD)
        pe.wait_ge(self.slo_ok, u + 1)
        for k in range(KD):
            for j in range(TPC):
                out, d = self.TR[k][:, j * P:(j + 1) * P], slice(k * P, (k + 1) * P)
                pe.matmul(out, self.s_hi[:, j, d], self.ident_r[:, :], start=True, stop=False)
                t = pe.matmul(out, self.s_lo[:, j, d], self.ident_r[:, :], start=False, stop=True)
        t.then_inc(self.turned, 1)

    def act_split_turned(self, u=0, h=0):
        act = self.pr.nc.scalar
        act.wait_ge(self.turned, u + 1)
        for k in range(self.pr.KD):
            act.activation(self.x_hi[h][:, k, :], self.TR[k][:, :], ACT.Copy).then_inc(self.hi_ok, 1)

    def dve_split_turned(self, u=0, h=0):
        dve = self.pr.nc.vector
        for k in range(self.pr.KD):
            dve.wait_ge(self.hi_ok, u * self.pr.KD + k + 1)
            dve.tensor_tensor(self.x_lo[h][:, k, :], self.TR[k][:, :], self.x_hi[h][:, k, :].bitcast(F32),
                              ALU.subtract).then_inc(self.lo_ok, 1)


def mlp(pr, W2, W3, ahead, act_halves, scratch, base, router, work):
    nc, ins, D, KD, NC, ST, F, B = pr.nc, pr.ins, pr.D, pr.KD, pr.NC, pr.ST, pr.F, pr.B
    FT, NU = F // P, B * NC
    K = max(1, int(0.5 * pr.T)) - 1
    LAG = 2
    SPLIT, TURN, SPLIT_T = 1, 3, 4
    CATCH_UP = SEARCH - 2
    assert FT == 8 and SEARCH == STEPS + 1 and NU >= SEARCH + CATCH_UP + 2
    with ExitStack() as ctx:
        out_sb = work[:, 0:2 * TPC * D].rearrange("p (h j d) -> p h j d", h=2, j=TPC)
        act32 = work[:, 2 * TPC * D:2 * TPC * D + 2 * CH].rearrange("p (i t) -> p i t", i=2)
        x32 = work[:, 3 * TPC * D:4 * TPC * D].rearrange("p (j d) -> p j d", j=TPC)
        a_hi, a_lo = act_halves
        y = sb(nc, ctx, "y", [P, B * ST, D])
        ahead.x_hi.append(sb(nc, ctx, "fx_hi1", [P, KD, CH], F32R))
        ahead.x_lo.append(sb(nc, ctx, "fx_lo1", [P, KD, CH], F32R))
        W3["b2"] = sb(nc, ctx, "b2", [P, 2, D])
        key_f, w_br = sb(nc, ctx, "key_f", [P, B, ST]), sb(nc, ctx, "w_br", [P, B, ST])
        low_f, above, equal, pick = (sb(nc, ctx, n, [P, B, ST]) for n in ("low_f", "above", "equal", "pick"))
        sign, key, part = (sb(nc, ctx, n, [P, B, ST], I32) for n in ("sign", "key", "part"))
        equal_b, earlier_b = (sb(nc, ctx, n, [P, B, ST], BF16) for n in ("equal_b", "earlier_b"))
        pivots, counts = sb(nc, ctx, "pivots", [P, B, PIV]), sb(nc, ctx, "counts", [P, B * PIV], BF16)
        passed = sb(nc, ctx, "passed", [P, B, PIV, ST], BF16)
        found, digit, need = sb(nc, ctx, "found", [P, B]), sb(nc, ctx, "dig", [P, B]), sb(nc, ctx, "need", [P, B])
        reach, zero = sb(nc, ctx, "reach", [P, B, PIV]), sb(nc, ctx, "zero", [P, ST])
        above_n = sb(nc, ctx, "above_n", [P, B], BF16)
        YB, CB, TIES, HB = pr.banks[0:2], pr.banks[2], pr.banks[3], pr.banks[4:6]
        (x_ld, slo_ok, lo_ok, base_ok, h1, gelu_ok, ah_ok, al_ok, y_done, y_kept, chain, counted, summed, out_ok,
         b2_ld) = (
            pr.sem("ff_" + n) for n in ("x_ld", "slo_ok", "lo_ok", "base_ok", "h1", "gelu_ok", "ah_ok", "al_ok",
                                        "y_done", "y_kept", "chain", "counted", "summed", "out_ok", "b2_ld"))
        st_x = [pr.sem(f"mx_st_x{s}{h}") for s in range(2) for h in range(2)]
        st_out = [pr.sem(f"ff_st_out{h}") for h in range(2)]
        block = pr.block
        x_all = scratch["xn"].rearrange("b c p j d -> (b c) p j d")
        out_all = pr.out.rearrange("b (c j p) d -> (b c) p j d", p=P, j=TPC)
        all_base = base[:, :, :, :].rearrange("p b t d -> p (b t) d")
        all_pick = pick[:, :, :].rearrange("p b t -> p (b t)")

        def chunks(eng, step):
            for u in range(SEARCH + CATCH_UP):
                step(u, u % 2)
            if NU > SEARCH + CATCH_UP + 2:
                with eng.Fori((SEARCH + CATCH_UP) // 2, NU // 2 - 1) as p:
                    for h in range(2):
                        step(p * 2 + h, h)
            for u in range(NU - 2, NU):
                step(u, u % 2)

        def last(u):
            return isinstance(u, int) and u == NU - 1

        def given(u, h):
            if early(u, SEARCH):
                return ()
            if early(u, SEARCH + CATCH_UP):
                return ((2 * (u - SEARCH), 0), (2 * (u - SEARCH) + 1, 1))
            return ((u - 2, h),)

        @block.sync
        def _(sp):
            def load(u):
                sp.dma_start(x32, x_all[u]).then_inc(x_ld, 16)

            def store(k, h):
                sp.wait_ge(out_ok, (k + 1) * TPC)
                sp.dma_start(out_all[k], out_sb[:, h]).then_inc(st_out[h], 16)

            def store_last():
                for j in (0, 2):
                    sp.wait_ge(out_ok, (NU - 1) * TPC + j + 2)
                    sp.dma_start(out_all[NU - 1, :, j:j + 2], out_sb[:, 1, j:j + 2]).then_inc(st_out[1], 16)

            def step(u, h):
                if not last(u) and not early(u, 1):
                    sp.wait_ge(slo_ok, u + 1)
                    sp.wait_ge(base_ok, u + 1)
                    load(u + 1)
                if early(u, 1):
                    sp.wait_ge(pr.sem("mw_lo1"), 1)
                    load(1)
                    for s in range(2):
                        ahead.store_last(s)
                    for sem in st_x:
                        sp.wait_ge(sem, 8 * NC + 1)
                    sp.wait_ge(pr.sem("mx_w_kept"), NC + 1)
                    for i in range(2):
                        sp.dma_start(W3["b2"][:, i, :], ins["ffn_b2"].partition_broadcast(P)).then_inc(b2_ld, 16)
                for k, kh in given(u, h):
                    store(k, kh)

            chunks(sp, step)
            store(NU - 2, 0)
            store_last()
            for h in range(2):
                sp.wait_ge(st_out[h], 16 * (NU // 2 + h))

        @block.gpsimd
        def _(pool):
            def step(u, h):
                pool.wait_ge(x_ld, (u + 1) * 16)
                x = ahead.x_first if early(u, 1) else x32
                nc.gpsimd.tensor_tensor(all_base[:, bass.ds(u * TPC, TPC), :], all_base[:, bass.ds(u * TPC, TPC), :],
                                        x, ALU.add).then_inc(base_ok, 1)

            chunks(pool, step)

        @block.scalar
        def _(act):
            def step(u, h):
                for j in range(FT):
                    act.wait_ge(h1, u * FT + j + 1)
                    past(act, al_ok, u * FT + j - 1)
                    nc.scalar.activation(act32[:, j % 2, :], HB[j % 2][:, :], ACT.Gelu_apprx_tanh,
                                         bias=W3["b1"][:, j:j + 1]).then_inc(gelu_ok, 1)
                    past(act, y_done, u * FT + j - 1)
                    act.wait_ge(gelu_ok, u * FT + j + 1)
                    nc.scalar.activation(a_hi[:, j % 2, :], act32[:, j % 2, :], ACT.Copy).then_inc(ah_ok, 1)
                    if early(u, 1) and j < 2:
                        ahead.norm_last(j)
                    if j == SPLIT and not last(u):
                        ahead.act_split(x32, u + 1)
                    if j == SPLIT_T and not last(u):
                        if early(u, 1):
                            act.wait_ge(pr.sem("mx_w_kept"), NC + 1)
                            for sem in st_x:
                                act.wait_ge(sem, 8 * NC + 1)
                        ahead.act_split_turned(u + 1, 1 - h)

            chunks(act, step)

        @block.vector
        def _(dve):
            links = [0]

            def link(ins):
                links[0] += 1
                ins.then_inc(chain, 1)
                dve.wait_ge(chain, links[0])

            def make_keys():
                w = w_br[:, :, :]
                link(nc.vector.tensor_scalar(w, router[:, :, :], W2["br"][:, 0:1], None, ALU.add))
                bits = w.bitcast(I32)
                link(nc.vector.tensor_scalar(sign[:, :, :], bits, 31, -2147483648, ALU.arith_shift_right, ALU.bitwise_or))
                link(nc.vector.tensor_tensor(key[:, :, :], bits, sign[:, :, :], ALU.bitwise_xor))
                link(nc.vector.tensor_scalar(part[:, :, :], key[:, :, :], 16, None, ALU.logical_shift_right))
                link(nc.vector.tensor_copy(key_f[:, :, :], part[:, :, :]))
                link(nc.vector.tensor_scalar(part[:, :, :], key[:, :, :], 65535, None, ALU.bitwise_and))
                link(nc.vector.tensor_copy(low_f[:, :, :], part[:, :, :]))
                link(nc.vector.memset(found[:, :], 0.0))
                link(nc.vector.memset(zero[:, :], 0.0))

            def count(q):
                for b in range(B):
                    link(nc.vector.tensor_scalar(pivots[:, b, :], W3["digit"][:, :], float(16 ** (STEPS - 1 - q)),
                                                 found[:, b:b + 1], ALU.mult, ALU.add))
                shape = [P, B, PIV, ST]
                link(nc.vector.tensor_tensor(passed[:, :, :, :], key_f[:, :, :].unsqueeze(2).to_broadcast(shape),
                                             pivots[:, :, :].unsqueeze(3).to_broadcast(shape), ALU.is_ge))
                with nc.allow_low_precision("counts up to 32"):
                    nc.vector.tensor_reduce(counts[:, :], passed[:, :, :, :].rearrange("p b q t -> p (b q) t"), AX_X,
                                            ALU.add).then_inc(counted, 1)

            def advance(n, q):
                dve.wait_ge(summed, n + 1)
                for b in range(B):
                    link(nc.vector.tensor_scalar(reach[:, b, :], CB[:, b * PIV:(b + 1) * PIV], float(K), None, ALU.is_ge))
                link(nc.vector.tensor_reduce(digit[:, :], reach[:, :, :], AX_X, ALU.add))
                link(nc.vector.scalar_tensor_tensor(found[:, :], digit[:, :], float(16 ** (STEPS - 1 - q)), found[:, :],
                                                    ALU.mult, ALU.add))

            def compare(out, in0, op):
                for b in range(B):
                    link(nc.vector.tensor_scalar(out[:, b, :], in0[:, b, :], found[:, b:b + 1], None, op))

            def low_keys():
                compare(above, key_f, ALU.is_gt)
                compare(equal, key_f, ALU.is_equal)
                link(nc.vector.scalar_tensor_tensor(low_f[:, :, :], low_f[:, :, :], 1.0, equal[:, :, :], ALU.add, ALU.mult))
                link(nc.vector.scalar_tensor_tensor(key_f[:, :, :], above[:, :, :], 131072.0, low_f[:, :, :], ALU.mult, ALU.add))
                link(nc.vector.memset(found[:, :], 1.0))

            def tie_counts():
                compare(above, key_f, ALU.is_gt)
                compare(equal, key_f, ALU.is_equal)
                with nc.allow_low_precision("counts up to 32"):
                    link(nc.vector.tensor_reduce(above_n[:, :], above[:, :, :], AX_X, ALU.add))
                link(nc.vector.tensor_copy(equal_b[:, :, :], equal[:, :, :]))
                for b in range(B):
                    link(nc.vector.tensor_tensor_scan(pick[:, b, :], zero[:, :], equal[:, b, :], 0.0, ALU.add, ALU.add))
                nc.vector.tensor_tensor(earlier_b[:, :, :], pick[:, :, :], equal[:, :, :], ALU.subtract).then_inc(counted, 1)

            def choose():
                dve.wait_ge(summed, 2 * STEPS + 1)
                link(nc.vector.tensor_scalar(need[:, :], TIES[:, 256:256 + B], -1.0, float(K), ALU.mult, ALU.add))
                for b in range(B):
                    link(nc.vector.tensor_scalar(pick[:, b, :], TIES[:, b * ST:(b + 1) * ST], need[:, b:b + 1], None, ALU.is_lt))
                link(nc.vector.tensor_tensor(pick[:, :, :], pick[:, :, :], equal[:, :, :], ALU.mult))
                link(nc.vector.tensor_tensor(pick[:, :, :], pick[:, :, :], above[:, :, :], ALU.add))
                link(nc.vector.tensor_tensor(pick[:, :, :], pick[:, :, :], w_br[:, :, :], ALU.mult))

            def keep_y(u):
                dve.wait_ge(y_done, (u + 1) * FT)
                for i in range(2):
                    nc.vector.tensor_tensor(y[:, bass.ds(u * TPC + 2 * i, 2), :], YB[i][:, :], W3["b2"][:, :, :],
                                            ALU.add).then_inc(y_kept, 1)

            def give(k, h):
                past(dve, st_out[h], (k - h) * 8)
                dve.wait_ge(base_ok, k + 1)
                for j in range(TPC):
                    dve.wait_ge(y_kept, k * 2 + j // 2 + 1)
                    nc.vector.scalar_tensor_tensor(out_sb[:, h, j, :], y[:, k * TPC + j, :],
                                                   all_pick[:, bass.ds(k * TPC + j, 1)], all_base[:, k * TPC + j, :],
                                                   ALU.mult, ALU.add).then_inc(out_ok, 1)

            def step(u, h):
                for j in range(FT):
                    dve.wait_ge(ah_ok, u * FT + j + 1)
                    nc.vector.tensor_tensor(a_lo[:, j % 2, :], act32[:, j % 2, :], a_hi[:, j % 2, :].bitcast(F32),
                                            ALU.subtract).then_inc(al_ok, 1)
                    if j == 0 and not early(u, 1):
                        if early(u, 2):
                            dve.wait_ge(b2_ld, 32)
                        keep_y(u - 1)
                    if early(u, 1) and 1 <= j <= 4:
                        ahead.route_last(j - 1)
                    if early(u, 1) and j == 6:
                        dve.wait_ge(pr.sem("mx_w_kept"), NC + 1)
                        for sem in st_x:
                            dve.wait_ge(sem, 8 * NC + 1)
                        make_keys()
                    if j == SPLIT and not last(u):
                        ahead.dve_split(x32, u + 1)
                    if j == SPLIT_T and not last(u):
                        ahead.dve_split_turned(u + 1, 1 - h)
                    if j in (3, 6):
                        for k, kh in given(u, h)[j // 5:j // 5 + 1]:
                            give(k, kh)
                    if early(u, SEARCH) and not early(u, 1):
                        n = 2 * (u - 1) + j // 4
                        if j % 4 == 1:
                            count(n % STEPS)
                        if j % 4 == 3:
                            advance(n, n % STEPS)
                            if n == STEPS - 1:
                                low_keys()
                            if n == 2 * STEPS - 1:
                                tie_counts()
                    if isinstance(u, int) and u == SEARCH and j == 2:
                        choose()

            chunks(dve, step)
            give(NU - 2, 0)
            keep_y(NU - 1)
            give(NU - 1, 1)

        @block.tensor
        def _(pe):
            def second(u, j):
                pe.wait_ge(al_ok, u * FT + j + 1)
                if j == 0:
                    past(pe, y_kept, u * 2)
                    if early(u, 1):
                        pe.wait_ge(pr.sem("mx_h2_ok"), 4 * NC)
                        pe.wait_ge(pr.sem("mw_lo2"), 1)
                for t in range(TPC):
                    rows = slice(t * P, (t + 1) * P)
                    for n, (a, w) in enumerate(split_products(a_hi[:, j % 2, rows], a_lo[:, j % 2, rows],
                                                              W3["w2_hi"][:, j, :], W3["w2_lo"][:, j, :])):
                        mm = pe.matmul(YB[t // 2][:, (t % 2) * D:(t % 2 + 1) * D], a, w,
                                       start=j == 0 and t % 2 == 0 and n == 0, stop=j == FT - 1 and n == 2,
                                       skip_group_check=True)
                mm.then_inc(y_done, 1)

            def step(u, h):
                pe.wait_ge(lo_ok, (u + 1) * KD)
                for j in range(FT):
                    past(pe, gelu_ok, u * FT + j - 1)
                    cols = slice(j * P, (j + 1) * P)
                    n = 0
                    for k in range(KD):
                        for w, x in split_products(W3["w1_hi"][:, k, cols], W3["w1_lo"][:, k, cols],
                                                   ahead.x_hi[h][:, k, :], ahead.x_lo[h][:, k, :]):
                            n += 1
                            mm = pe.matmul(HB[j % 2][:, :], w, x, start=n == 1, stop=n == 3 * KD)
                    mm.then_inc(h1, 1)
                    if j >= LAG:
                        second(u, j - LAG)
                    elif j == 0 and not early(u, 1):
                        for back in range(LAG, 0, -1):
                            second(u - 1, FT - back)
                    if j == TURN and not last(u):
                        ahead.pe_turn(u + 1)
                    if early(u, SEARCH) and not early(u, 1) and j % 4 == 3:
                        n = 2 * (u - 1) + j // 4
                        pe.wait_ge(counted, n + 1)
                        pe.matmul(CB[:, 0:B * PIV], W3["ones"][:, :], counts[:, :], start=True, stop=True).then_inc(summed, 1)
                    if isinstance(u, int) and u == SEARCH and j == 1:
                        pe.wait_ge(counted, 2 * STEPS + 1)
                        flat = (equal_b[:, :, :].rearrange("p b t -> p (b t)"), earlier_b[:, :, :].rearrange("p b t -> p (b t)"))
                        pe.matmul(TIES[:, 0:B * ST], W3["before"][:, :], flat[0], start=True, stop=False, skip_group_check=True)
                        pe.matmul(TIES[:, 0:B * ST], W3["ones"][:, :], flat[1], start=False, stop=True, skip_group_check=True)
                        pe.matmul(TIES[:, 256:256 + B], W3["ones"][:, :], above_n[:, :], start=False, stop=True,
                                  skip_group_check=True).then_inc(summed, 1)

            pe.wait_ge(pr.sem("mx_o_ok"), 4 * NC)
            chunks(pe, step)
            for back in range(LAG, 0, -1):
                second(NU - 1, FT - back)


def tokenizer_tables(pr, ctx):
    nc, KD, D = pr.nc, pr.KD, pr.D
    W = {n: sb(nc, ctx, n, [P, D]) for n in ("gamma", "beta", "attn_bo")}
    W["prelu"] = sb(nc, ctx, "prelu", [P, 1])
    W["bo_col"], W["bk_col"] = sb(nc, ctx, "bo_col", [P, KD]), sb(nc, ctx, "bk_col", [P, KD])
    W["kt"] = sb(nc, ctx, "kt", [P, 2, KD, pr.T], F32R)
    W["x_hi"], W["x_lo"] = (sb(nc, ctx, n, [P, 2, KD, CH], F32R) for n in ("x_hi", "x_lo"))
    W["v_bias"] = sb(nc, ctx, "v_bias", [P, D + 2])
    W["a_hi"], W["a_lo"] = (sb(nc, ctx, n, [P, KD, D], F32R) for n in ("a_hi", "a_lo"))
    W["vo_hi"], W["vo_lo"] = (sb(nc, ctx, n, [P, KD, D + 2], F32R) for n in ("vo_hi", "vo_lo"))
    return W


def build(nc, ins, out, batches, tokens, width, heads, hidden):
    KD, NC, FT = width // P, tokens // CH, hidden // P
    with ExitStack() as ctx:
        pr = Program(nc, ctx, ins, out, batches, tokens, width, heads, hidden)
        scratch = {n: nc.dram_tensor(f"scratch_{n}", (batches, NC, P) + s, F32, kind="Internal").ap() for n, s in (
            ("h", (TPC, width)), ("mn", (TPC, width)), ("mnT", (KD, CH)), ("xn", (TPC, width)))}
        pr.block = ctx.enter_context(nc.Block())
        banks = pr.banks = [ps(nc, ctx, f"bank{i}") for i in range(8)]
        ident_r = sb(nc, ctx, "ident_r", [P, P], F32R)
        work = sb(nc, ctx, "work", [P, 2 * KD * hidden])
        with ExitStack() as phase:
            W = tokenizer_tables(pr, phase)
            setup_weights(pr, W, ident_r, work)
            tokenizer(pr, W, ident_r, scratch, work)
        base = sb(nc, ctx, "base", [P, batches, pr.ST, width])
        router = sb(nc, ctx, "router", [P, batches, pr.ST])
        W2 = {"wr": sb(nc, ctx, "wr", [P, width]), "br": sb(nc, ctx, "br", [P, 1])}
        W3 = {"b1": sb(nc, ctx, "b1", [P, FT]), "digit": sb(nc, ctx, "digit", [P, PIV])}
        W3["ones"], W3["before"] = sb(nc, ctx, "ones", [P, P], BF16), sb(nc, ctx, "before", [P, P], BF16)
        W3["index"] = sb(nc, ctx, "index", [P, PIV], I32)
        places = [-(-nc.sbuf_base // 32) * 32]
        piece = sb(nc, ctx, "piece", [P, 2 * TPC * width])
        halves = sb(nc, ctx, "halves", [P, 4 * KD * hidden], F32R)
        places.append(-(-nc.sbuf_base // 32) * 32)
        late = sb(nc, ctx, "late", [P, 8 * CH])
        n = KD * hidden
        for i, x in enumerate(("w1_hi", "w1_lo", "w2_hi", "w2_lo")):
            W3[x] = halves[:, i * n:(i + 1) * n].rearrange("p (k n) -> p k n", k=KD if i < 2 else FT)
        M = {"m32": piece[:, :].rearrange("p (b k t) -> p b k t", b=2, k=KD),
             "V": banks[4:6], "GB": banks[6:8]}
        M["m_hi"], M["m_lo"] = (halves[:, i * 2 * n:(i + 1) * 2 * n].rearrange(
            "p (h b k t) -> p h b k t", h=2, b=2, k=KD) for i in range(2))
        s_hi, s_lo = (nc.alloc_sbuf_tensor_at(n, [P, TPC, width], F32R, offset=places[0] + i * TPC * width * 4)[:, :, :]
                      for i, n in enumerate(("xn_hi", "xn_lo")))
        x_hi, x_lo, a_hi, a_lo = (nc.alloc_sbuf_tensor_at(n, [P, 2, CH], F32R, offset=places[1] + i * 2 * CH * 4)
                                  for i, n in enumerate(("fx_hi0", "fx_lo0", "act_hi", "act_lo")))
        ahead = AheadOfMLP(pr, ident_r, s_hi, s_lo, x_hi, x_lo, banks[6:8])
        mlp_raw = {"w2": work[:, 0:n].rearrange("p (k n) -> p k n", k=FT),
                   "w1": work[:, n:2 * n].rearrange("p (k n) -> p k n", k=KD)}
        with ExitStack() as phase:
            W2["bg_col"], W2["att"] = sb(nc, phase, "bg_col", [P, KD]), sb(nc, phase, "att_w", [P, 2, 2, KD])
            for x in "vgo":
                W2[x + "_hi"], W2[x + "_lo"] = (sb(nc, phase, f"w{x}{n}", [P, KD, width], F32R) for n in ("_hi", "_lo"))
            with ExitStack() as heads_phase:
                heads_in = {n: sb(nc, heads_phase, f"hw_{n}", shape) for n, shape in (
                    [(x, [P, KD, width]) for x in "vgokq"] +
                    [("prod", [P, 4, KD, width]), ("same_head", [P, P]), ("ones", [P, 2]), ("cols", [P, 16]),
                     ("att", [P, 2, 2, 2]), ("top", [P, 2, 2]), ("shifted", [P, 2, 2, 2]), ("expd", [P, 2, 2, 2]),
                     ("total", [P, 2, 2]), ("inv", [P, 2, 2])])}
                start_mix(pr, W2, heads_in, M, scratch, pr.last_mnT)
                head_weights(pr, W2, heads_in, gram_view(work, width), banks[0:4])
            mix(pr, W2, M, (banks[0:2], banks[2:4]), ahead, late, scratch, base, router, mlp_raw, W3)
        mlp(pr, W2, W3, ahead, (a_hi, a_lo), scratch, base, router, work)


def _layouts(inputs):
    import numpy as np

    a = {k: np.asarray(v) for k, v in inputs.items()}
    x, dg = a["x"], a["L0_tok_d_gamma_batched"]
    B, _, T, D = x.shape
    out = {
        "xT": x.reshape(B, T // CH, CH, D // P, P).transpose(0, 1, 4, 3, 2),
        "gateT": dg.reshape(T // CH, CH, T // P // GT, GT, P).transpose(0, 2, 4, 3, 1),
    }
    for n in ("Wq", "Wk", "Wv"):
        out[f"tok_{n}T"] = a[f"L0_tok_{n}"].T
    for n in ("Wo", "bq", "bk", "bv", "bo"):
        out[f"tok_{n}"] = a[f"L0_tok_{n}"]
    out["tok_prelu_a"] = a["L0_tok_prelu_a"].reshape(1)
    for n in ("gamma", "beta", "Wq", "Wk", "Wv", "Wg", "bg", "Wo", "bo"):
        out[f"attn_{n}"] = a[f"L0_attn_{n}"]
    out["ffn_wr"] = a["L0_ffn_wr"].reshape(-1)
    for n in ("br", "w1", "b1", "w2", "b2"):
        out[f"ffn_{n}"] = a[f"L0_ffn_{n}"]
    return {k: np.ascontiguousarray(v) for k, v in out.items()}, (B, T, D, a["L0_ffn_w1"].shape[1])


def kernel(**inputs):
    import concourse.bacc as bacc
    from concourse.bass_utils import run_bass_kernel_spmd

    arrays, (B, T, D, F) = _layouts(inputs)
    nc = bacc.Bacc("TRN2", target_bir_lowering=False, num_devices=1, dynamic_dma_scratch_size=1024)
    ins = {n: nc.dram_tensor(f"in_{n}", a.shape, mybir.dt.from_np(a.dtype), kind="ExternalInput").ap()
           for n, a in arrays.items()}
    out = nc.dram_tensor("out_0", (B, T, D), F32, kind="ExternalOutput").ap()
    build(nc, ins, out, B, T, D, HEADS, F)
    r = run_bass_kernel_spmd(nc, [{f"in_{n}": a for n, a in arrays.items()}], core_ids=[0])
    return r.results[0]["out_0"]
```
